# Optimizing a Trainium2 kernel written in Bass

```python
import numpy as np
import jax
import jax.numpy as jnp

def _softmax(x, axis=-1):
    return jax.nn.softmax(x, axis=axis)

def _gelu(x):
    return jax.nn.gelu(x, approximate=True)

def _silu(x):
    return jax.nn.silu(x)

def _sigmoid(x):
    return jax.nn.sigmoid(x)

def _layernorm(x, axis=-1, eps=1e-05):
    m = jnp.mean(x, axis=axis, keepdims=True)
    v = jnp.var(x, axis=axis, keepdims=True)
    return (x - m) / jnp.sqrt(v + eps)

def _scatter_add(tgt, idx, src, axis=0):
    return tgt.at[idx].add(src)

def _segment_sum(src, seg, n):
    return jax.ops.segment_sum(src, seg, n)
kernel_name = 'mk_hybrid_d1_jaxref_r4_0f8b5d'

def setup_inputs(seed: int=0):
    np.random.seed(seed)
    _w = jnp.asarray

    def _L0_attn_a_setup():
        import jax, jax.numpy as jnp
        import numpy as np
        N_HEADS = 16
        N_KV_HEADS = 4
        MAX_TIMESCALE = 10000.0

        def rms_norm(x):
            var = jnp.mean(jnp.square(x.astype(jnp.float32)), axis=-1, keepdims=True)
            return (x * jax.lax.rsqrt(var + 1e-06)).astype(x.dtype)

        def rotate_half(x):
            x1, x2 = jnp.split(x, 2, axis=-1)
            return jnp.concatenate([-x2, x1], axis=-1)

        def sine_table(features, length):
            fraction = jnp.arange(0, features, 2, dtype=jnp.float32) / features
            inv_freq = 1.0 / MAX_TIMESCALE ** fraction
            sinusoid = jnp.arange(length, dtype=jnp.float32)[:, None] * inv_freq[None, :]
            sinusoid = jnp.concatenate([sinusoid, sinusoid], axis=-1)
            return (jnp.sin(sinusoid), jnp.cos(sinusoid))
        key = jax.random.key(seed)
        ks = jax.random.split(key, 5)
        B, T, C = (2, 256, 512)
        N, K = (N_HEADS, N_KV_HEADS)
        H = C // N
        init_std = np.sqrt(2.0 / (5.0 * C))
        wang_std = 2.0 / 24 / np.sqrt(N * H)
        x = jax.random.normal(ks[0], (B, T, C), dtype=jnp.float32)
        q_kernel = jax.random.normal(ks[1], (C, N * H), dtype=jnp.float32) * init_std
        k_kernel = jax.random.normal(ks[2], (C, K * H), dtype=jnp.float32) * init_std
        v_kernel = jax.random.normal(ks[3], (C, K * H), dtype=jnp.float32) * init_std
        out_kernel = jax.random.normal(ks[4], (N * H, C), dtype=jnp.float32) * wang_std
        return {'x': x, 'q_kernel': q_kernel, 'k_kernel': k_kernel, 'v_kernel': v_kernel, 'out_kernel': out_kernel}
    _L0_attn_a_in = _L0_attn_a_setup()

    def _L0_attn_b_setup():
        import jax, jax.numpy as jnp
        import numpy as np
        D_MODEL = 512
        D_STATE = 16
        D_CONV = 4
        EXPAND = 2
        D_INNER = EXPAND * D_MODEL
        HEAD_DIM = 64
        N_HEADS = D_INNER // HEAD_DIM
        N_GROUPS = 1
        CONV_DIM = D_INNER + 2 * N_GROUPS * D_STATE
        IN_DIM = D_INNER + CONV_DIM + N_HEADS
        BATCH, SEQ = (2, 1024)
        EPS = 1e-05
        key = jax.random.key(seed)
        ks = jax.random.split(key, 8)
        s = 0.02
        return {'hidden_states': jax.random.normal(ks[0], (BATCH, SEQ, D_MODEL), jnp.float32), 'W_in': jax.random.normal(ks[1], (D_MODEL, IN_DIM), jnp.float32) * s, 'conv_w': jax.random.normal(ks[2], (CONV_DIM, D_CONV), jnp.float32) * s, 'conv_b': jnp.zeros((CONV_DIM,), jnp.float32), 'A_log': jnp.log(jax.random.uniform(ks[3], (N_HEADS,), jnp.float32, 1.0, 16.0)), 'D_skip': jnp.ones((N_HEADS,), jnp.float32), 'dt_bias': jnp.ones((N_HEADS,), jnp.float32), 'norm_w': jnp.ones((D_INNER,), jnp.float32), 'W_out': jax.random.normal(ks[4], (D_INNER, D_MODEL), jnp.float32) * s}
    _L0_attn_b_in = _L0_attn_b_setup()

    def _L0_ffn_setup():
        import jax, jax.numpy as jnp
        import numpy as np
        HIDDEN = 512
        INTER = 1408
        B, S = (2, 512)

        def _ternary(key, shape):
            return jax.random.randint(key, shape, -1, 2).astype(jnp.float32)
        key = jax.random.key(seed)
        ks = jax.random.split(key, 7)
        x = jax.random.normal(ks[0], (B, S, HIDDEN), dtype=jnp.float32)
        gate_w = _ternary(ks[1], (INTER, HIDDEN))
        up_w = _ternary(ks[2], (INTER, HIDDEN))
        down_w = _ternary(ks[3], (HIDDEN, INTER))
        gate_s = jax.random.uniform(ks[4], (INTER,), minval=0.01, maxval=0.1, dtype=jnp.float32)
        up_s = jax.random.uniform(ks[5], (INTER,), minval=0.01, maxval=0.1, dtype=jnp.float32)
        down_s = jax.random.uniform(ks[6], (HIDDEN,), minval=0.01, maxval=0.1, dtype=jnp.float32)
        return {'x': x, 'gate_w': gate_w, 'up_w': up_w, 'down_w': down_w, 'gate_s': gate_s, 'up_s': up_s, 'down_s': down_s}
    _L0_ffn_in = _L0_ffn_setup()
    _d = {'L0_attn_a_x': _L0_attn_a_in['x'], 'L0_attn_a_q_kernel': _L0_attn_a_in['q_kernel'], 'L0_attn_a_k_kernel': _L0_attn_a_in['k_kernel'], 'L0_attn_a_v_kernel': _L0_attn_a_in['v_kernel'], 'L0_attn_a_out_kernel': _L0_attn_a_in['out_kernel'], 'L0_attn_b_W_in': _L0_attn_b_in['W_in'], 'L0_attn_b_conv_w': _L0_attn_b_in['conv_w'], 'L0_attn_b_conv_b': _L0_attn_b_in['conv_b'], 'L0_attn_b_A_log': _L0_attn_b_in['A_log'], 'L0_attn_b_D_skip': _L0_attn_b_in['D_skip'], 'L0_attn_b_dt_bias': _L0_attn_b_in['dt_bias'], 'L0_attn_b_norm_w': _L0_attn_b_in['norm_w'], 'L0_attn_b_W_out': _L0_attn_b_in['W_out'], 'L0_ffn_gate_w': _L0_ffn_in['gate_w'], 'L0_ffn_up_w': _L0_ffn_in['up_w'], 'L0_ffn_down_w': _L0_ffn_in['down_w'], 'L0_ffn_gate_s': _L0_ffn_in['gate_s'], 'L0_ffn_up_s': _L0_ffn_in['up_s'], 'L0_ffn_down_s': _L0_ffn_in['down_s']}
    _x0 = _d['L0_attn_a_x']
    _d['L0_attn_a_x'] = jax.random.normal(jax.random.fold_in(jax.random.key(seed), 1), (1, 2048, 512), dtype=_x0.dtype)
    del _x0
    return _d

def reference(L0_attn_a_x, L0_attn_a_q_kernel, L0_attn_a_k_kernel, L0_attn_a_v_kernel, L0_attn_a_out_kernel, L0_attn_b_W_in, L0_attn_b_conv_w, L0_attn_b_conv_b, L0_attn_b_A_log, L0_attn_b_D_skip, L0_attn_b_dt_bias, L0_attn_b_norm_w, L0_attn_b_W_out, L0_ffn_gate_w, L0_ffn_up_w, L0_ffn_down_w, L0_ffn_gate_s, L0_ffn_up_s, L0_ffn_down_s):

    def _L0_attn_a_ref(x, q_kernel, k_kernel, v_kernel, out_kernel):
        import jax, jax.numpy as jnp
        import numpy as np
        N_HEADS = 16
        N_KV_HEADS = 4
        MAX_TIMESCALE = 10000.0

        def rms_norm(x):
            var = jnp.mean(jnp.square(x.astype(jnp.float32)), axis=-1, keepdims=True)
            return (x * jax.lax.rsqrt(var + 1e-06)).astype(x.dtype)

        def rotate_half(x):
            x1, x2 = jnp.split(x, 2, axis=-1)
            return jnp.concatenate([-x2, x1], axis=-1)

        def sine_table(features, length):
            fraction = jnp.arange(0, features, 2, dtype=jnp.float32) / features
            inv_freq = 1.0 / MAX_TIMESCALE ** fraction
            sinusoid = jnp.arange(length, dtype=jnp.float32)[:, None] * inv_freq[None, :]
            sinusoid = jnp.concatenate([sinusoid, sinusoid], axis=-1)
            return (jnp.sin(sinusoid), jnp.cos(sinusoid))
        B, T, C = x.shape
        N, K = (N_HEADS, N_KV_HEADS)
        G = N // K
        H = C // N
        q = rms_norm(jnp.dot(x, q_kernel))
        k = rms_norm(jnp.dot(x, k_kernel))
        v = jnp.dot(x, v_kernel)
        q = q.reshape(B, T, K, G, H)
        k = k.reshape(B, T, K, H)
        v = v.reshape(B, T, K, H)
        sin, cos = sine_table(H, T)
        qcos = cos[None, :, None, None, :]
        qsin = sin[None, :, None, None, :]
        kcos = cos[None, :, None, :]
        ksin = sin[None, :, None, :]
        q = (q * qcos + rotate_half(q) * qsin).astype(x.dtype)
        k = (k * kcos + rotate_half(k) * ksin).astype(x.dtype)
        scale = jax.lax.rsqrt(jnp.array(H, dtype=jnp.float32)).astype(q.dtype)
        logits = jnp.einsum('btkgh,bskh->bkgts', q * scale, k)
        probs = jax.nn.softmax(logits.astype(jnp.float32), axis=-1).astype(logits.dtype)
        encoded = jnp.einsum('bkgts,bskh->btkgh', probs, v)
        encoded = encoded.reshape(B, T, N * H)
        return jnp.dot(encoded, out_kernel)

    def _L0_attn_b_ref(hidden_states, W_in, conv_w, conv_b, A_log, D_skip, dt_bias, norm_w, W_out):
        import jax, jax.numpy as jnp
        import numpy as np
        D_MODEL = 512
        D_STATE = 16
        D_CONV = 4
        EXPAND = 2
        D_INNER = EXPAND * D_MODEL
        HEAD_DIM = 64
        N_HEADS = D_INNER // HEAD_DIM
        N_GROUPS = 1
        CONV_DIM = D_INNER + 2 * N_GROUPS * D_STATE
        IN_DIM = D_INNER + CONV_DIM + N_HEADS
        BATCH, SEQ = (2, 1024)
        EPS = 1e-05
        b, l, _ = hidden_states.shape
        zxbcdt = jnp.einsum('bld,di->bli', hidden_states, W_in)
        gate = zxbcdt[..., :D_INNER]
        xBC = zxbcdt[..., D_INNER:D_INNER + CONV_DIM]
        dt = zxbcdt[..., D_INNER + CONV_DIM:]
        xpad = jnp.pad(xBC, ((0, 0), (D_CONV - 1, 0), (0, 0)))
        conv = conv_b
        for k in range(D_CONV):
            conv = conv + xpad[:, k:k + l, :] * conv_w[:, k]
        xBC = jax.nn.silu(conv)
        x = xBC[..., :D_INNER].reshape(b, l, N_HEADS, HEAD_DIM)
        Bm = xBC[..., D_INNER:D_INNER + D_STATE]
        Cm = xBC[..., D_INNER + D_STATE:]
        dt = jax.nn.softplus(dt + dt_bias)
        A = -jnp.exp(A_log)
        dA = jnp.exp(dt * A)
        xs = x.transpose(1, 0, 2, 3)
        Bs = Bm.transpose(1, 0, 2)
        Cs = Cm.transpose(1, 0, 2)
        dts = dt.transpose(1, 0, 2)
        dAs = dA.transpose(1, 0, 2)
        h0 = jnp.zeros((b, N_HEADS, HEAD_DIM, D_STATE), hidden_states.dtype)

        def step(h, inp):
            x_t, B_t, C_t, dt_t, dA_t = inp
            h = h * dA_t[:, :, None, None] + (dt_t[:, :, None] * x_t)[..., None] * B_t[:, None, None, :]
            y = jnp.einsum('bhpn,bn->bhp', h, C_t)
            return (h, y)
        _, ys = jax.lax.scan(step, h0, (xs, Bs, Cs, dts, dAs))
        y = ys.transpose(1, 0, 2, 3) + D_skip[None, None, :, None] * x
        y = y.reshape(b, l, D_INNER)
        y = y * jax.nn.silu(gate)
        var = jnp.mean(y * y, axis=-1, keepdims=True)
        y = y * jax.lax.rsqrt(var + EPS) * norm_w
        return jnp.einsum('bld,do->blo', y, W_out)

    def _L0_ffn_ref(x, gate_w, up_w, down_w, gate_s, up_s, down_s):
        import jax, jax.numpy as jnp
        import numpy as np
        HIDDEN = 512
        INTER = 1408
        B, S = (2, 512)

        def _ternary(key, shape):
            return jax.random.randint(key, shape, -1, 2).astype(jnp.float32)
        b, s, h = x.shape
        xf = x.reshape(b * s, h)
        g = jnp.einsum('th,ih->ti', xf, gate_w) * gate_s
        u = jnp.einsum('th,ih->ti', xf, up_w) * up_s
        hdn = jax.nn.silu(g) * u
        out = jnp.einsum('ti,hi->th', hdn, down_w) * down_s
        return out.reshape(b, s, -1)
    x = L0_attn_a_x
    x = x + _L0_attn_a_ref(_layernorm(x, axis=-1), L0_attn_a_q_kernel, L0_attn_a_k_kernel, L0_attn_a_v_kernel, L0_attn_a_out_kernel)
    x = x + _L0_ffn_ref(_layernorm(x, axis=-1), L0_ffn_gate_w, L0_ffn_up_w, L0_ffn_down_w, L0_ffn_gate_s, L0_ffn_up_s, L0_ffn_down_s)
    x = x + _L0_attn_b_ref(_layernorm(x, axis=-1), L0_attn_b_W_in, L0_attn_b_conv_w, L0_attn_b_conv_b, L0_attn_b_A_log, L0_attn_b_D_skip, L0_attn_b_dt_bias, L0_attn_b_norm_w, L0_attn_b_W_out)
    x = x + _L0_ffn_ref(_layernorm(x, axis=-1), L0_ffn_gate_w, L0_ffn_up_w, L0_ffn_down_w, L0_ffn_gate_s, L0_ffn_up_s, L0_ffn_down_s)
    return x

_drawn_inputs = setup_inputs


def setup_inputs(seed=0):
    import zlib

    import numpy as np

    out = dict(_drawn_inputs(seed))
    spreads = {'L0_attn_b_conv_b': (0.0, 0.1),
     'L0_attn_b_D_skip': (1.0, 0.2),
     'L0_attn_b_dt_bias': (1.0, 0.6),
     'L0_attn_b_norm_w': (1.0, 0.2)}
    factors = {'L0_attn_a_q_kernel': 8.0,
     'L0_attn_a_k_kernel': 8.0,
     'L0_attn_a_v_kernel': 8.0,
     'L0_attn_a_out_kernel': 8.0,
     'L0_attn_b_A_log': 64.0}
    for name, (base, spread) in spreads.items():
        noise = np.random.default_rng([zlib.crc32(name.encode()), seed]).standard_normal(out[name].shape)
        drawn = base * np.exp(spread * noise) if base else spread * noise
        out[name] = jnp.asarray(drawn.astype(out[name].dtype))
    for name, factor in factors.items():
        out[name] = (out[name] * factor).astype(out[name].dtype)
    return out
```

```python
from contextlib import ExitStack

import concourse.bass as bass
from concourse import mybir

F32 = mybir.dt.float32
F32R = mybir.dt.float32r
ALU = mybir.AluOpType
ACT = mybir.ActivationFunctionType

P = 128
LN_EPS = 1e-5
RMS_EPS = 1e-6
GATE_EPS = 1e-5

HEADS = 16
KV_HEADS = 4
GROUP = HEADS // KV_HEADS
HEAD = 32

SSM_HEADS = 16
SSM_HEAD = 64
STATE = 16
TAPS = 4
B_ROW, C_ROW, DT_ROW = 0, 32, 64


def build_qkv(nc, new_sem, x_in, w_qkv, rope, ident, neg_half, q_all, k_stack, v_all):
    T, C = x_in.shape
    K_TILES = C // P
    TILES = T // P
    QC, KC = HEADS * HEAD, KV_HEADS * HEAD
    N = QC + 2 * KC
    QK = QC + KC
    HALF = HEAD // 2
    x_tile = x_in.rearrange("(t p) c -> t p c", p=P)

    with ExitStack() as ctx:
        def sb(n, shape, dt=F32):
            return ctx.enter_context(nc.sbuf_tensor(f"qkv_{n}", shape, dt))

        def sem(n):
            return new_sem(f"qkv_{n}")

        def pair(n, shape, dt=F32):
            return [sb(f"{n}{k}", shape, dt) for k in range(2)]

        w_raw = sb("w_raw", [P, K_TILES, N])
        w_hi = sb("w_hi", [P, K_TILES, N], F32R)
        w_lo = sb("w_lo", [P, K_TILES, N], F32R)
        rope_sb = sb("rope", [P, TILES, 2, HEAD])
        x = pair("x", [P, C])
        u = pair("u", [P, C])
        u_hi = pair("u_hi", [P, C], F32R)
        u_lo = pair("u_lo", [P, C], F32R)
        stats = pair("stats", [P, 6])
        mv = pair("mv", [P, 2])
        veps = pair("veps", [P, 1])
        rstd = pair("rstd", [P, 1])
        square = pair("square", [P, QK])
        ssq = pair("ssq", [P, 2])
        qeps = pair("qeps", [P, 2])
        qk_rms = pair("qk_rms", [P, 2])
        normed = pair("normed", [P, QK])
        by_cos = pair("by_cos", [P, QK])
        by_sin = pair("by_sin", [P, QK])
        k_rot = pair("k_rot", [P, KC])
        k_rows = pair("k_rows", [P, KV_HEADS, 4, HEAD], F32R)

        def bank(n, cols):
            return [ctx.enter_context(nc.psum_tensor(f"qkv_{n}{k}", [P, cols], F32)) for k in range(2)]

        turn_ps = bank("turn_ps", 512)
        proj = bank("proj", 1024)
        k_ps = bank("k_ps", 512)

        w_in = sem("w_in")
        rope_in = sem("rope_in")
        w_hi_made = sem("w_hi_made")
        w_split = sem("w_split")
        x_landed = [sem(f"x_landed{k}") for k in range(2)]
        stats_made = sem("stats_made")
        stats_seen = sem("stats_seen")
        mean_made = sem("mean_made")
        veps_made = sem("veps_made")
        rstd_made = sem("rstd_made")
        u_made = sem("u_made")
        turned = sem("turned")
        uhi_made = sem("uhi_made")
        u_split = sem("u_split")
        proj_done = sem("proj_done")
        squares_made = sem("squares_made")
        qeps_made = sem("qeps_made")
        qk_rms_made = sem("qk_rms_made")
        normed_made = sem("normed_made")
        v_copied = sem("v_copied")
        cos_made = sem("cos_made")
        sin_made = sem("sin_made")
        q_made = sem("q_made")
        k_made = sem("k_made")
        khi_made = sem("khi_made")
        k_rows_made = sem("k_rows_made")
        k_turned = sem("k_turned")
        k_stored = sem("k_stored")

        LAGS = 4
        FIRST, LAST = 3, TILES // 2 - 1

        def steps(step):
            def run(engine):
                for t in range(2 * FIRST):
                    step(t // 2, t % 2, t)
                with engine.Fori(FIRST, LAST) as m:
                    for k in range(2):
                        step(m, k, 2 * m + k)
                for t in range(2 * LAST, TILES + LAGS):
                    step(t // 2, t % 2, t)
            return run

        def has(t, lag):
            return not isinstance(t, int) or 0 <= t - lag < TILES

        def freed(engine, signal, count):
            if not isinstance(count, int) or count > 0:
                engine.wait_ge(signal, count)

        def tile_of(tensor, t):
            return tensor[:, t] if isinstance(t, int) else tensor[:, bass.ds(t, 1)].squeeze(1)

        with nc.Block() as block:

            @block.sync
            def _(sp):
                sp.dma_start(x[0][:, :], x_tile[0]).then_inc(x_landed[0], 16)
                for c in range(K_TILES):
                    sp.dma_start(w_raw[:, c, :], w_qkv[:, c, :]).then_inc(w_in, 16)
                sp.dma_start(x[1][:, :], x_tile[1]).then_inc(x_landed[1], 16)
                sp.dma_start(rope_sb[:, :, :, :], rope).then_inc(rope_in, 16)
                with sp.Fori(1, TILES // 2) as m:
                    for k in range(2):
                        sp.wait_ge(u_made, 2 * m + k - 1)
                        sp.dma_start(x[k][:, :], x_tile[2 * m + k]).then_inc(x_landed[k], 16)

            @block.gpsimd
            def _(pool):
                def rstd_tile(t, k):
                    pool.wait_ge(veps_made, t + 1)
                    pool.tensor_tensor(rstd[k][:, :], veps[k][:, :], neg_half[:, 0:1],
                                       ALU.pow).then_inc(rstd_made, 1)

                def step(m, k, t):
                    if has(t, -1):
                        rstd_tile(t + 1, 1 - k)
                    if has(t, 2):
                        pool.wait_ge(qeps_made, t - 1)
                        pool.tensor_tensor(qk_rms[k][:, :], qeps[k][:, :], neg_half[:, 0:2],
                                           ALU.pow).then_inc(qk_rms_made, 1)
                        pool.wait_ge(normed_made, t - 1)
                        freed(pool, k_made, t - 3)
                        src = normed[k][:, :].rearrange("p (h s d) -> p h s d", s=2, d=HALF)
                        dst = by_sin[k][:, :].rearrange("p (h s d) -> p h s d", s=2, d=HALF)
                        sin = tile_of(rope_sb, t - 2)[:, 1, :]
                        for s in range(2):
                            last = pool.tensor_tensor(
                                dst[:, :, s, :], src[:, :, 1 - s, :],
                                sin[:, s * HALF:(s + 1) * HALF].unsqueeze(1).to_broadcast([P, QK // HEAD, HALF]),
                                ALU.mult)
                        last.then_inc(sin_made, 1)

                rstd_tile(0, 0)
                pool.wait_ge(w_hi_made, 1)
                pool.tensor_tensor(w_lo[:, :, :], w_raw[:, :, :], w_hi[:, :, :].bitcast(F32),
                                   ALU.subtract).then_inc(w_split, 1)
                pool.wait_ge(rope_in, 16)
                steps(step)(pool)

            @block.scalar
            def _(act):
                act.wait_ge(w_in, 16 * K_TILES)
                act.activation(w_hi[:, :, :], w_raw[:, :, :], ACT.Copy).then_inc(w_hi_made, 1)

                def step(m, k, t):
                    if has(t, 2):
                        act.wait_ge(proj_done, t - 1)
                        freed(act, squares_made, t - 3)
                        act.activation(square[k][:, 0:QC], proj[k][:, 0:QC], ACT.Square, accum_out=ssq[k][:, 0:1])
                        act.activation(square[k][:, QC:QK], proj[k][:, QC:QK], ACT.Square,
                                       accum_out=ssq[k][:, 1:2]).then_inc(squares_made, 1)
                    if has(t, 0):
                        act.wait_ge(turned, t + 1)
                        freed(act, proj_done, t - 1)
                        act.activation(u_hi[k][:, :], turn_ps[k][:, :], ACT.Copy).then_inc(uhi_made, 1)
                    if has(t, 2):
                        act.wait_ge(qk_rms_made, t - 1)
                        freed(act, sin_made, t - 3)
                        freed(act, cos_made, t - 3)
                        act.activation(normed[k][:, 0:QC], proj[k][:, 0:QC], ACT.Copy, scale=qk_rms[k][:, 0:1])
                        act.activation(normed[k][:, QC:QK], proj[k][:, QC:QK], ACT.Copy,
                                       scale=qk_rms[k][:, 1:2]).then_inc(normed_made, 1)
                        act.activation(tile_of(v_all, t - 2), proj[k][:, QK:N], ACT.Copy).then_inc(v_copied, 1)
                    if has(t, 4):
                        act.wait_ge(k_turned, t - 3)
                        act.activation(k_stack[:, :, bass.ds((t - 4) * P, P)],
                                       k_ps[k][:, :].rearrange("p (g s) -> p g s", g=KV_HEADS),
                                       ACT.Copy).then_inc(k_stored, 1)

                steps(step)(act)

            @block.vector
            def _(dve):
                def stats_tile(t, k, landed):
                    dve.wait_ge(x_landed[k], 16 * landed)
                    dve.bn_stats(stats[k][:, :], x[k][:, :]).then_inc(stats_made, 1)
                    dve.wait_ge(stats_made, t + 1)
                    dve.sem_inc(stats_seen, 1)
                    dve.bn_aggr(mv[k][:, :], stats[k][:, :]).then_inc(mean_made, 1)
                    dve.wait_ge(mean_made, t + 1)
                    dve.tensor_scalar(veps[k][:, :], mv[k][:, 1:2], LN_EPS, None, ALU.add).then_inc(veps_made, 1)

                def step(m, k, t):
                    if has(t, 0):
                        dve.wait_ge(rstd_made, t + 1)
                        freed(dve, turned, t - 1)
                        dve.tensor_scalar(u[k][:, :], x[k][:, :], mv[k][:, 0:1], rstd[k][:, 0:1],
                                          ALU.subtract, ALU.mult).then_inc(u_made, 1)
                    if has(t, -1):
                        stats_tile(t + 1, 1 - k, m + 1 + k)
                    if has(t, 2):
                        dve.wait_ge(squares_made, t - 1)
                        dve.tensor_scalar(qeps[k][:, 0:1], ssq[k][:, 0:1], 1.0 / QC, RMS_EPS, ALU.mult, ALU.add)
                        dve.tensor_scalar(qeps[k][:, 1:2], ssq[k][:, 1:2], 1.0 / KC, RMS_EPS, ALU.mult,
                                          ALU.add).then_inc(qeps_made, 1)
                    if has(t, 3):
                        dve.wait_ge(sin_made, t - 2)
                        dve.wait_ge(cos_made, t - 2)
                        dve.tensor_tensor(k_rot[1 - k][:, :], by_cos[1 - k][:, QC:QK], by_sin[1 - k][:, QC:QK],
                                          ALU.add)
                        dve.tensor_tensor(tile_of(q_all, t - 3), by_cos[1 - k][:, 0:QC], by_sin[1 - k][:, 0:QC],
                                          ALU.add).then_inc(k_made, 1)
                    if has(t, 0):
                        dve.wait_ge(uhi_made, t + 1)
                        dve.tensor_tensor(u_lo[k][:, :], turn_ps[k][:, :], u_hi[k][:, :].bitcast(F32),
                                          ALU.subtract).then_inc(u_split, 1)
                    if has(t, 3):
                        dve.wait_ge(k_made, t - 2)
                        freed(dve, k_turned, t - 4)
                        rot = k_rot[1 - k][:, :].rearrange("p (g d) -> p g d", d=HEAD)
                        rows = k_rows[1 - k]
                        for r in (0, 2):
                            last = dve.tensor_copy(rows[:, :, r, :], rot)
                        last.then_inc(khi_made, 1)
                        dve.wait_ge(khi_made, t - 2)
                        for r in (1, 3):
                            last = dve.tensor_tensor(rows[:, :, r, :], rot, rows[:, :, 0, :].bitcast(F32),
                                                     ALU.subtract)
                        last.then_inc(k_rows_made, 1)
                    if has(t, 2):
                        dve.wait_ge(normed_made, t - 1)
                        dve.tensor_tensor(
                            by_cos[k][:, :].rearrange("p (h d) -> p h d", d=HEAD),
                            normed[k][:, :].rearrange("p (h d) -> p h d", d=HEAD),
                            tile_of(rope_sb, t - 2)[:, 0, :].unsqueeze(1).to_broadcast([P, QK // HEAD, HEAD]),
                            ALU.mult).then_inc(cos_made, 1)

                stats_tile(0, 0, 1)
                dve.wait_ge(rope_in, 16)
                steps(step)(dve)

            @block.tensor
            def _(pe):
                def step(m, k, t):
                    if has(t, 0):
                        pe.wait_ge(u_made, t + 1)
                        freed(pe, u_split, t - 1)
                        for c in range(K_TILES):
                            last = pe.transpose(turn_ps[k][:, c * P:(c + 1) * P], u[k][:, c * P:(c + 1) * P],
                                                ident[:, :])
                        last.then_inc(turned, 1)
                    if has(t, 1):
                        j = 1 - k
                        pe.wait_ge(u_split, t)
                        if isinstance(t, int) and t == 1:
                            pe.wait_ge(w_split, 1)
                        freed(pe, v_copied, t - 2)
                        for a, b in ((0, QC), (QC, N)):
                            for c in range(K_TILES):
                                cols = slice(c * P, (c + 1) * P)
                                for n, (v, w) in enumerate(((u_hi, w_hi), (u_hi, w_lo), (u_lo, w_hi))):
                                    last = pe.matmul(proj[j][:, a:b], v[j][:, cols], w[:, c, a:b],
                                                     start=(c == 0 and n == 0),
                                                     stop=(c == K_TILES - 1 and n == 2))
                        last.then_inc(proj_done, 1)
                    if has(t, 4):
                        pe.wait_ge(k_rows_made, t - 3)
                        freed(pe, k_stored, t - 5)
                        for g in range(KV_HEADS):
                            last = pe.transpose(k_ps[k][:, g * P:(g + 1) * P],
                                                k_rows[k][:, g].rearrange("p r d -> p (r d)").bitcast(F32),
                                                ident[:, :])
                        last.then_inc(k_turned, 1)

                steps(step)(pe)


def build_attention(nc, new_sem, x_in, x_out, w_out, ident, q_all, k_stack, v_all):
    T, C = x_in.shape
    TILES = T // P
    J = 4
    BLOCK = J * P
    BLOCKS = T // BLOCK
    STEPS = TILES
    N = KV_HEADS * STEPS
    WIDE = GROUP * BLOCK
    RING = 4
    DVE_COLS = 1280
    SCALE = float(HEAD) ** -0.5
    x_blk = x_in.rearrange("(b j p) c -> b p j c", p=P, j=J)
    y_blk = x_out.rearrange("(b j p) c -> b p j c", p=P, j=J)

    Q_AT = (6, 8)
    OUT_AT = (12, 14)
    uses = []
    for n in range(N):
        if n % STEPS in Q_AT:
            uses.append(("q", n // STEPS, Q_AT.index(n % STEPS)))
        if n in OUT_AT:
            uses.append(("out", 0, OUT_AT.index(n)))
        uses += [("exp", n, 0), ("exp", n, 1)]
    assert len(uses) % 3 == 0
    place = {use: i for i, use in enumerate(uses)}

    with ExitStack() as ctx:
        def sb(n, shape, dt=F32):
            return ctx.enter_context(nc.sbuf_tensor(f"at_{n}", shape, dt))

        def sem(n):
            return new_sem(f"at_{n}")

        wo_raw = sb("wo_raw", [P, KV_HEADS, C])
        wo_hi = sb("wo_hi", [P, KV_HEADS, C], F32R)
        wo_lo = sb("wo_lo", [P, KV_HEADS, C], F32R)
        ones = sb("ones", [P, HEAD])
        q_rows = sb("q_rows", [P, J, GROUP, 4, HEAD], F32R)
        q_stack = [sb(f"q_stack{k}", [P, GROUP, BLOCK], F32R) for k in range(2)]
        probs = sb("probs", [P, RING, WIDE])
        sums = [sb(f"sums{k}", [P, WIDE]) for k in range(2)]
        pv_sb = sb("pv_sb", [P, BLOCK])
        inverse = sb("inverse", [P, BLOCK])
        enc = sb("enc", [P, BLOCK])
        enc_hi = sb("enc_hi", [P, KV_HEADS, BLOCK], F32R)
        enc_lo = sb("enc_lo", [P, KV_HEADS, BLOCK], F32R)
        y = sb("y", [P, J, C])
        slots = [ctx.enter_context(nc.psum_tensor(f"at_slot{k}", [P, 2, BLOCK], F32)) for k in range(3)]
        pv = ctx.enter_context(nc.psum_tensor("at_pv", [P, BLOCK], F32))
        den = ctx.enter_context(nc.psum_tensor("at_den", [P, BLOCK], F32))

        PRIME = 4
        qk_done = sem("qk_done")
        exp_done = sem("exp_done")
        pv_done = sem("pv_done")
        dve_added = sem("dve_added")
        pool_added = sem("pool_added")
        den_done = sem("den_done")
        inverted = sem("inverted")
        pv_saved = sem("pv_saved")
        enc_made = sem("enc_made")
        enc_hi_made = sem("enc_hi_made")
        enc_split = sem("enc_split")
        out_done = sem("out_done")
        qhi_made = sem("qhi_made")
        q_rows_made = sem("q_rows_made")
        q_turned = sem("q_turned")
        q_stacked = sem("q_stacked")
        wo_in = sem("wo_in")
        wo_hi_made = sem("wo_hi_made")
        wo_split = sem("wo_split")
        ones_made = sem("ones_made")
        y_seeded = sem("y_seeded")
        y_made = sem("y_made")
        y_stored = sem("y_stored")

        def exps(b, n, half):
            return b * (2 * N) + 2 * n + half + 1 + PRIME

        def adds(b, n):
            return b * (KV_HEADS * (STEPS - 1)) + (n // STEPS) * (STEPS - 1) + max(n % STEPS, 1) + PRIME

        def released(engine, b, i):
            if i < 0:
                b, i = b - 1, i + len(uses)
            kind, n, k = uses[i]
            if kind == "exp":
                engine.wait_ge(exp_done, exps(b, n, k))
            elif kind == "q":
                engine.wait_ge(q_stacked, b * (2 * KV_HEADS) + 2 * n + k + 3)
            else:
                engine.wait_ge(y_made, J * (b - 1) + 2 * k + 2 + PRIME)

        def add_step(engine, b, n, cols, added):
            s, acc = n % STEPS, sums[n // STEPS % 2]
            if s == 0:
                return
            engine.wait_ge(exp_done, exps(b, n, 1))
            if s == 1:
                engine.wait_ge(den_done, KV_HEADS * b + n // STEPS - 1 + PRIME)
                first = probs[:, (n - 1) % RING, cols]
            else:
                engine.wait_ge(added, adds(b, n - 1))
                first = acc[:, cols]
            engine.tensor_tensor(acc[:, cols], first, probs[:, n % RING, cols], ALU.add).then_inc(added, 1)

        with nc.Block() as block:

            @block.sync
            def _(sp):
                sp.dma_start(wo_raw[:, :, :], w_out).then_inc(wo_in, 16)
                sp.dma_start(y[:, :, :], x_blk[0]).then_inc(y_seeded, 16)
                with sp.Fori(1, BLOCKS) as b:
                    sp.wait_ge(y_made, J * b + PRIME)
                    sp.dma_start(y_blk[b - 1], y[:, :, :]).then_inc(y_stored, 16)
                    sp.wait_ge(y_stored, 16 * b)
                    sp.dma_start(y[:, :, :], x_blk[b]).then_inc(y_seeded, 16)
                sp.wait_ge(y_made, J * BLOCKS + PRIME)
                sp.dma_start(y_blk[BLOCKS - 1], y[:, :, :]).then_inc(y_stored, 16)
                sp.wait_ge(y_stored, 16 * BLOCKS)

            @block.gpsimd
            def _(pool):
                pool.sem_inc(pool_added, PRIME)
                pool.wait_ge(wo_hi_made, 1)
                pool.tensor_tensor(wo_lo[:, :, :], wo_raw[:, :, :], wo_hi[:, :, :].bitcast(F32),
                                   ALU.subtract).then_inc(wo_split, 1)
                cols = slice(DVE_COLS, WIDE)
                with pool.Fori(0, BLOCKS) as b:
                    for n in range(N):
                        add_step(pool, b, n, cols, pool_added)

            @block.scalar
            def _(act):
                for s in (exp_done, pv_saved, enc_hi_made):
                    act.sem_inc(s, PRIME)
                act.wait_ge(wo_in, 16)
                act.activation(wo_hi[:, :, :], wo_raw[:, :, :], ACT.Copy).then_inc(wo_hi_made, 1)

                def save_pv(b, g):
                    act.wait_ge(pv_done, b * N + (g + 1) * STEPS + PRIME)
                    act.wait_ge(enc_made, b * KV_HEADS + g + PRIME)
                    act.activation(pv_sb[:, :], pv[:, :], ACT.Copy).then_inc(pv_saved, 1)

                def enc_high(b, g):
                    act.wait_ge(enc_made, b * KV_HEADS + g + 1 + PRIME)
                    act.activation(enc_hi[:, g, :], enc[:, :], ACT.Copy).then_inc(enc_hi_made, 1)

                def stack_q(b, g, c):
                    i = place["q", g - 1, c] if g else c
                    act.wait_ge(q_turned, b * (2 * KV_HEADS) + 2 * g + c + 1)
                    out = q_stack[g % 2][:, :, 2 * c * P:2 * (c + 1) * P].rearrange("p h (j t) -> p j h t", t=P)
                    act.activation(out, slots[i % 3][:, :, :].rearrange("p j (h t) -> p j h t", t=P),
                                   ACT.Copy).then_inc(q_stacked, 1)

                for c in range(2):
                    stack_q(0, 0, c)
                with act.Fori(0, BLOCKS) as b:
                    for n in range(N):
                        g, s = divmod(n, STEPS)
                        if s in Q_AT:
                            c = Q_AT.index(s)
                            i = place["q", g, c]
                            act.wait_ge(q_turned, b * (2 * KV_HEADS) + 2 * g + c + 3)
                            out = q_stack[(g + 1) % 2][:, :, 2 * c * P:2 * (c + 1) * P].rearrange(
                                "p h (j t) -> p j h t", t=P)
                            act.activation(out, slots[i % 3][:, :, :].rearrange("p j (h t) -> p j h t", t=P),
                                           ACT.Copy).then_inc(q_stacked, 1)
                        for half in range(2):
                            act.wait_ge(qk_done, b * (2 * N) + 2 * n + half + 1)
                            if half == 0:
                                m = n - RING
                                act.wait_ge(pv_done, b * N + m + 1 + PRIME)
                                for added in (dve_added, pool_added):
                                    act.wait_ge(added, adds(b, m) if m >= 0 else adds(b - 1, m + N))
                            i = place["exp", n, half]
                            wide = probs[:, n % RING, half * 2 * BLOCK:(half + 1) * 2 * BLOCK]
                            act.activation(wide, slots[i % 3][:, :, :].rearrange("p h t -> p (h t)"),
                                           ACT.Exp, scale=SCALE).then_inc(exp_done, 1)
                        if s == 0:
                            if g:
                                save_pv(b, g - 1)
                            else:
                                with act.If(b > 0):
                                    save_pv(b - 1, KV_HEADS - 1)
                        if s == 7:
                            if g:
                                enc_high(b, g - 1)
                            else:
                                with act.If(b > 0):
                                    enc_high(b - 1, KV_HEADS - 1)
                save_pv(BLOCKS - 1, KV_HEADS - 1)
                enc_high(BLOCKS - 1, KV_HEADS - 1)

            @block.vector
            def _(dve):
                for s in (dve_added, inverted, enc_made, enc_split, y_made):
                    dve.sem_inc(s, PRIME)
                dve.memset(ones[:, :], 1.0).then_inc(ones_made, 1)

                def rows_q(b, g, unit):
                    src = q_all[:, bass.ds(b * J, J), g * P:(g + 1) * P].rearrange("p j (h d) -> p j h d", d=HEAD)
                    if not isinstance(unit, int) or unit:
                        dve.wait_ge(q_turned, 2 * unit)
                    for r in (0, 1):
                        last = dve.tensor_copy(q_rows[:, :, :, r, :], src)
                    last.then_inc(qhi_made, 1)
                    dve.wait_ge(qhi_made, unit + 1)
                    for r in (2, 3):
                        last = dve.tensor_tensor(q_rows[:, :, :, r, :], src, q_rows[:, :, :, 0, :].bitcast(F32),
                                                 ALU.subtract)
                    last.then_inc(q_rows_made, 1)

                def invert(b, g):
                    dve.wait_ge(den_done, b * KV_HEADS + g + 1 + PRIME)
                    dve.reciprocal(inverse[:, :], den[:, :]).then_inc(inverted, 1)

                def encode(b, g):
                    dve.wait_ge(inverted, b * KV_HEADS + g + 1 + PRIME)
                    dve.wait_ge(pv_saved, b * KV_HEADS + g + 1 + PRIME)
                    dve.wait_ge(enc_split, b * KV_HEADS + g + PRIME)
                    dve.tensor_tensor(enc[:, :], pv_sb[:, :], inverse[:, :], ALU.mult).then_inc(enc_made, 1)

                def enc_low(b, g):
                    dve.wait_ge(enc_hi_made, b * KV_HEADS + g + 1 + PRIME)
                    dve.tensor_tensor(enc_lo[:, g, :], enc[:, :], enc_hi[:, g, :].bitcast(F32),
                                      ALU.subtract).then_inc(enc_split, 1)

                def add_out(b, k, slot):
                    dve.wait_ge(y_seeded, 16 * b + 16)
                    dve.wait_ge(out_done, 2 * b + k + 1 + PRIME)
                    for j in range(2):
                        dve.tensor_tensor(y[:, 2 * k + j, :], y[:, 2 * k + j, :], slots[slot][:, j, :],
                                          ALU.add).then_inc(y_made, 1)

                rows_q(0, 0, 0)
                with dve.Fori(0, BLOCKS) as b:
                    for n in range(N):
                        g, s = divmod(n, STEPS)
                        add_step(dve, b, n, slice(0, DVE_COLS), dve_added)
                        if s == 1:
                            if g + 1 < KV_HEADS:
                                rows_q(b, g + 1, b * KV_HEADS + g + 1)
                            else:
                                rows_q((b + 1) % BLOCKS, 0, b * KV_HEADS + g + 1)
                        for at, do in ((3, invert), (5, encode), (9, enc_low)):
                            if s == at:
                                if g:
                                    do(b, g - 1)
                                else:
                                    with dve.If(b > 0):
                                        do(b - 1, KV_HEADS - 1)
                        if n + 1 in OUT_AT:
                            k = OUT_AT.index(n + 1)
                            with dve.If(b > 0):
                                add_out(b - 1, k, place["out", 0, k] % 3)
                for do in (invert, encode, enc_low):
                    do(BLOCKS - 1, KV_HEADS - 1)
                for k in range(2):
                    add_out(BLOCKS - 1, k, k)

            @block.tensor
            def _(pe):
                for s in (pv_done, den_done, out_done):
                    pe.sem_inc(s, PRIME)

                def turn_q(slot, c):
                    for j in range(2):
                        for h in range(GROUP):
                            last = pe.transpose(slots[slot][:, j, h * P:(h + 1) * P],
                                                q_rows[:, 2 * c + j, h].rearrange("p r d -> p (r d)").bitcast(F32),
                                                ident[:, :])
                    last.then_inc(q_turned, 1)

                def logits(b, n, half):
                    g, s = divmod(n, STEPS)
                    i = place["exp", n, half]
                    released(pe, b, i - 3)
                    if s == 0 and half == 0:
                        pe.wait_ge(q_stacked, b * (2 * KV_HEADS) + 2 * g + 2)
                    for h in range(2):
                        last = pe.matmul(slots[i % 3][:, h, :], k_stack[:, g, s * P:(s + 1) * P],
                                         q_stack[g % 2][:, 2 * half + h, :], start=True, stop=True)
                    last.then_inc(qk_done, 1)

                def values(b, n):
                    g, s = divmod(n, STEPS)
                    pe.wait_ge(exp_done, exps(b, n, 1))
                    if s == 0:
                        pe.wait_ge(pv_saved, b * KV_HEADS + g + PRIME)
                    for h in range(GROUP):
                        last = pe.matmul(pv[h * HEAD:(h + 1) * HEAD, :], v_all[:, s, g * HEAD:(g + 1) * HEAD],
                                         probs[:, n % RING, h * BLOCK:(h + 1) * BLOCK],
                                         start=(s == 0), stop=(s == STEPS - 1), tile_position=(0, h * HEAD))
                    last.then_inc(pv_done, 1)

                def denominators(b, g):
                    for added in (dve_added, pool_added):
                        pe.wait_ge(added, adds(b, (g + 1) * STEPS - 1))
                    pe.wait_ge(inverted, b * KV_HEADS + g + PRIME)
                    for h in range(GROUP):
                        last = pe.matmul(den[h * HEAD:(h + 1) * HEAD, :], ones[:, :],
                                         sums[g % 2][:, h * BLOCK:(h + 1) * BLOCK], start=True, stop=True,
                                         tile_position=(0, h * HEAD))
                    last.then_inc(den_done, 1)

                def project(b, k, slot):
                    pe.wait_ge(enc_split, (b + 1) * KV_HEADS + PRIME)
                    for j in range(2):
                        cols = slice((2 * k + j) * P, (2 * k + j + 1) * P)
                        for g in range(KV_HEADS):
                            for m, (e, w) in enumerate(((enc_hi, wo_hi), (enc_hi, wo_lo), (enc_lo, wo_hi))):
                                last = pe.matmul(slots[slot][:, j, :], e[:, g, cols], w[:, g, :],
                                                 start=(g == 0 and m == 0), stop=(g == KV_HEADS - 1 and m == 2))
                    last.then_inc(out_done, 1)

                pe.wait_ge(q_rows_made, 1)
                for c in range(2):
                    turn_q(c, c)
                pe.wait_ge(ones_made, 1)
                pe.wait_ge(wo_split, 1)
                with pe.Fori(0, BLOCKS) as b:
                    for n in range(N):
                        g, s = divmod(n, STEPS)
                        if s in Q_AT:
                            c = Q_AT.index(s)
                            i = place["q", g, c]
                            pe.wait_ge(q_rows_made, b * KV_HEADS + g + 2)
                            released(pe, b, i - 3)
                            turn_q(i % 3, c)
                        if n in OUT_AT:
                            k = OUT_AT.index(n)
                            i = place["out", 0, k]
                            with pe.If(b > 0):
                                released(pe, b, i - 3)
                                project(b - 1, k, i % 3)
                        logits(b, n, 0)
                        if n >= 2:
                            values(b, n - 2)
                        else:
                            with pe.If(b > 0):
                                values(b - 1, N + n - 2)
                        logits(b, n, 1)
                        if s == 3:
                            if g:
                                denominators(b, g - 1)
                            else:
                                with pe.If(b > 0):
                                    denominators(b - 1, KV_HEADS - 1)
                last = BLOCKS - 1
                for n in (N - 2, N - 1):
                    values(last, n)
                denominators(last, KV_HEADS - 1)
                for k in range(2):
                    if k == 0:
                        pe.wait_ge(exp_done, exps(last, N - 1, 1))
                        pe.wait_ge(q_stacked, 2 * KV_HEADS * BLOCKS + 2)
                    project(last, k, k)


def build_ffn(nc, new_sem, name, x_in, x_out, w_ffn, scales, down_scale, ident, neg_half):
    T, C = x_in.shape
    I_TILES = w_ffn.shape[0]
    K_TILES = C // P
    J = 4
    BLOCK = J * P
    BLOCKS = T // BLOCK
    GU = K_TILES * 2 * P
    LAG = 2
    x_blk = x_in.rearrange("(b j p) c -> b p j c", p=P, j=J)
    y_blk = x_out.rearrange("(b j p) c -> b p j c", p=P, j=J)

    with ExitStack() as ctx:
        def sb(n, shape, dt=F32):
            return ctx.enter_context(nc.sbuf_tensor(f"{name}_{n}", shape, dt))

        def sem(n):
            return new_sem(f"{name}_{n}")

        stage = sb("stage", [P, 2, GU + C])
        gu_hi = sb("gu_hi", [P, I_TILES, K_TILES, 2 * P], F32R)
        gu_lo = sb("gu_lo", [P, I_TILES, K_TILES, 2 * P], F32R)
        dn_hi = sb("dn_hi", [P, I_TILES, C], F32R)
        dn_lo = sb("dn_lo", [P, I_TILES, C], F32R)
        scale = sb("scale", [P, 2, I_TILES])
        ds_row = sb("ds_row", [P, C])
        x = sb("x", [P, J, C])
        y = sb("y", [P, J, C])
        u = sb("u", [P, J, C])
        u_hi = sb("u_hi", [P, K_TILES, BLOCK], F32R)
        u_lo = sb("u_lo", [P, K_TILES, BLOCK], F32R)
        act_g = sb("act_g", [P, BLOCK])
        h = sb("h", [P, BLOCK])
        h_hi = sb("h_hi", [P, 2, BLOCK], F32R)
        h_lo = sb("h_lo", [P, 2, BLOCK], F32R)
        stats = sb("stats", [P, J, 6])
        mv = sb("mv", [P, J, 2])
        veps = sb("veps", [P, J])
        rstd = sb("rstd", [P, J])
        gu_ps = ctx.enter_context(nc.psum_tensor(f"{name}_gu_ps", [P, 2, 2, BLOCK], F32))
        acc = ctx.enter_context(nc.psum_tensor(f"{name}_acc", [P, J, C], F32))

        consts_in = sem("consts_in")
        w_in = [sem(f"w_in{k}") for k in range(2)]
        w_scaled = sem("w_scaled")
        w_hi_made = sem("w_hi_made")
        w_split = sem("w_split")
        x_landed = sem("x_landed")
        y_seeded = sem("y_seeded")
        stats_made = sem("stats_made")
        stats_seen = sem("stats_seen")
        mean_made = sem("mean_made")
        veps_made = sem("veps_made")
        rstd_made = sem("rstd_made")
        u_made = sem("u_made")
        turned = sem("turned")
        uhi_made = sem("uhi_made")
        u_split = sem("u_split")
        gu_done = sem("gu_done")
        silu_done = sem("silu_done")
        h_made = sem("h_made")
        hhi_made = sem("hhi_made")
        h_split = sem("h_split")
        down_done = sem("down_done")
        y_made = sem("y_made")
        y_stored = sem("y_stored")

        def slot(i):
            return (i + 1) % 2

        with nc.Block() as block:

            @block.sync
            def _(sp):
                sp.dma_start(x[:, :, :], x_blk[0]).then_inc(x_landed, 16)
                sp.dma_start(scale[:, :, :], scales).then_inc(consts_in, 16)
                sp.dma_start(ds_row[:, :], down_scale.partition_broadcast(P)).then_inc(consts_in, 16)
                for i in range(I_TILES):
                    if i >= 2:
                        sp.wait_ge(w_split, i - 1)
                    sp.dma_start(stage[:, i % 2, :], w_ffn[i]).then_inc(w_in[i % 2], 16)
                    if i == 2:
                        sp.dma_start(y[:, :, :], x_blk[0]).then_inc(y_seeded, 16)
                        sp.wait_ge(u_made, J)
                        sp.dma_start(x[:, :, :], x_blk[1]).then_inc(x_landed, 16)
                def swap_y(b):
                    sp.wait_ge(y_made, b * J)
                    sp.dma_start(y_blk[b - 1], y[:, :, :]).then_inc(y_stored, 16)
                    sp.wait_ge(y_stored, b * 16)
                    sp.dma_start(y[:, :, :], x_blk[b]).then_inc(y_seeded, 16)

                with sp.Fori(1, BLOCKS - 1) as b:
                    swap_y(b)
                    sp.wait_ge(u_made, b * J + J)
                    sp.dma_start(x[:, :, :], x_blk[b + 1]).then_inc(x_landed, 16)
                swap_y(BLOCKS - 1)
                sp.wait_ge(y_made, BLOCKS * J)
                sp.dma_start(y_blk[BLOCKS - 1], y[:, :, :]).then_inc(y_stored, 16)
                sp.wait_ge(y_stored, 16 * BLOCKS)

            @block.gpsimd
            def _(pool):
                def rstd_block(b):
                    pool.wait_ge(veps_made, b + 1)
                    pool.tensor_tensor(rstd[:, :], veps[:, :], neg_half[:, 0:J], ALU.pow).then_inc(rstd_made, 1)

                rstd_block(0)
                pool.wait_ge(consts_in, 32)

                def w_scale(i):
                    pool.wait_ge(w_in[i % 2], 16 * (i // 2 + 1))
                    down = stage[:, i % 2, GU:GU + C]
                    pool.tensor_tensor(down, down, ds_row[:, :], ALU.mult).then_inc(w_scaled, 1)

                w_scale(0)
                for i in range(I_TILES):
                    if i + 1 < I_TILES:
                        w_scale(i + 1)
                    pool.wait_ge(w_hi_made, i + 1)
                    raw = stage[:, i % 2, :]
                    pool.tensor_tensor(gu_lo[:, i].rearrange("p k n -> p (k n)"), raw[:, 0:GU],
                                       gu_hi[:, i].rearrange("p k n -> p (k n)").bitcast(F32), ALU.subtract)
                    pool.tensor_tensor(dn_lo[:, i, :], raw[:, GU:GU + C], dn_hi[:, i, :].bitcast(F32),
                                       ALU.subtract).then_inc(w_split, 1)
                with pool.Fori(1, BLOCKS) as b:
                    rstd_block(b)

            @block.scalar
            def _(act):
                def u_high(b):
                    for k in range(K_TILES):
                        act.wait_ge(turned, b * K_TILES + k + 1)
                        act.activation(u_hi[:, k, :], gu_ps[:, k // 2, k % 2, :], ACT.Copy).then_inc(uhi_made, 1)

                def w_high(i):
                    act.wait_ge(w_scaled, i + 1)
                    act.activation(gu_hi[:, i].rearrange("p k n -> p (k n)"), stage[:, i % 2, 0:GU], ACT.Copy)
                    act.activation(dn_hi[:, i, :], stage[:, i % 2, GU:GU + C], ACT.Copy).then_inc(w_hi_made, 1)

                def body(b, first, last):
                    for i in range(I_TILES):
                        if first and i + 2 < I_TILES:
                            w_high(i + 2)
                        act.wait_ge(gu_done, b * I_TILES + i + 1)
                        act.activation(act_g[:, :], gu_ps[:, slot(i), 0, :], ACT.Silu,
                                       scale=scale[:, 0, i:i + 1]).then_inc(silu_done, 1)
                        act.wait_ge(h_made, b * I_TILES + i + 1)
                        if not first or i >= 2:
                            act.wait_ge(down_done, b * I_TILES + i - 1)
                        act.activation(h_hi[:, i % 2, :], h[:, :], ACT.Copy).then_inc(hhi_made, 1)
                    if not last:
                        u_high(b + 1)

                w_high(0)
                w_high(1)
                u_high(0)
                act.wait_ge(consts_in, 32)
                body(0, True, False)
                with act.Fori(1, BLOCKS - 1) as b:
                    body(b, False, False)
                body(BLOCKS - 1, False, True)

            @block.vector
            def _(dve):
                def layernorm(b):
                    dve.wait_ge(x_landed, b * 16 + 16)
                    for j in range(J):
                        dve.bn_stats(stats[:, j, :], x[:, j, :]).then_inc(stats_made, 1)
                    dve.wait_ge(stats_made, b * J + J)
                    dve.sem_inc(stats_seen, 1)
                    for j in range(J):
                        dve.bn_aggr(mv[:, j, :], stats[:, j, :]).then_inc(mean_made, 1)
                    dve.wait_ge(mean_made, b * J + J)
                    dve.tensor_scalar(veps[:, :], mv[:, :, 1], LN_EPS, None, ALU.add).then_inc(veps_made, 1)
                    dve.wait_ge(rstd_made, b + 1)
                    for j in range(J):
                        dve.tensor_scalar(u[:, j, :], x[:, j, :], mv[:, j, 0:1], rstd[:, j:j + 1],
                                          ALU.subtract, ALU.mult).then_inc(u_made, 1)

                def u_low(b):
                    for k in range(K_TILES):
                        dve.wait_ge(uhi_made, b * K_TILES + k + 1)
                        dve.tensor_tensor(u_lo[:, k, :], gu_ps[:, k // 2, k % 2, :],
                                          u_hi[:, k, :].bitcast(F32), ALU.subtract).then_inc(u_split, 1)

                def body(b, first, last):
                    for i in range(I_TILES):
                        dve.wait_ge(silu_done, b * I_TILES + i + 1)
                        if not first or i >= 1:
                            dve.wait_ge(h_split, b * I_TILES + i)
                        dve.scalar_tensor_tensor(out=h[:, :], in0=gu_ps[:, slot(i), 1, :],
                                                 scalar=scale[:, 1, i:i + 1], in1=act_g[:, :],
                                                 op0=ALU.mult, op1=ALU.mult).then_inc(h_made, 1)
                        dve.wait_ge(hhi_made, b * I_TILES + i + 1)
                        dve.tensor_tensor(h_lo[:, i % 2, :], h[:, :], h_hi[:, i % 2, :].bitcast(F32),
                                          ALU.subtract).then_inc(h_split, 1)
                        if i == 8 and not last:
                            layernorm(b + 1)
                    if not last:
                        u_low(b + 1)
                    dve.wait_ge(y_seeded, b * 16 + 16)
                    dve.wait_ge(down_done, b * I_TILES + I_TILES)
                    for j in range(J):
                        dve.tensor_tensor(y[:, j, :], y[:, j, :], acc[:, j, :], ALU.add).then_inc(y_made, 1)

                layernorm(0)
                u_low(0)
                dve.wait_ge(consts_in, 32)
                body(0, True, False)
                with dve.Fori(1, BLOCKS - 1) as b:
                    body(b, False, False)
                body(BLOCKS - 1, False, True)

            @block.tensor
            def _(pe):
                def turn(b):
                    for k in range(K_TILES):
                        for j in range(J):
                            if k == 0:
                                pe.wait_ge(u_made, b * J + j + 1)
                            last = pe.transpose(gu_ps[:, k // 2, k % 2, j * P:(j + 1) * P],
                                                u[:, j, k * P:(k + 1) * P], ident[:, :])
                        last.then_inc(turned, 1)

                def gate_up(b, i, first):
                    if i == 0:
                        pe.wait_ge(u_split, b * K_TILES + K_TILES)
                    if not (first and i < 2):
                        pe.wait_ge(h_made, b * I_TILES + i - 1)
                    if first:
                        pe.wait_ge(w_split, i + 1)
                    for half in range(2):
                        for k in range(K_TILES):
                            w_hi = gu_hi[:, i, k, half * P:(half + 1) * P]
                            w_lo = gu_lo[:, i, k, half * P:(half + 1) * P]
                            for w, v in ((w_hi, u_hi), (w_hi, u_lo), (w_lo, u_hi)):
                                last = pe.matmul(gu_ps[:, slot(i), half, :], w, v[:, k, :],
                                                 start=(k == 0 and v is u_hi and w is w_hi),
                                                 stop=(k == K_TILES - 1 and w is w_lo))
                    last.then_inc(gu_done, 1)

                def down(b, i, first):
                    pe.wait_ge(h_split, b * I_TILES + i + 1)
                    if i == 0 and not first:
                        pe.wait_ge(y_made, b * J)
                    for j in range(J):
                        cols = slice(j * P, (j + 1) * P)
                        for n, (a, w) in enumerate(((h_hi, dn_hi), (h_hi, dn_lo), (h_lo, dn_hi))):
                            last = pe.matmul(acc[:, j, :], a[:, i % 2, cols], w[:, i, :],
                                             start=(i == 0 and n == 0),
                                             stop=(i == I_TILES - 1 and n == 2))
                    last.then_inc(down_done, 1)

                def body(b, first, last):
                    for i in range(I_TILES):
                        gate_up(b, i, first)
                        if i >= LAG:
                            down(b, i - LAG, first)
                    if not last:
                        pe.wait_ge(h_made, b * I_TILES + I_TILES)
                        turn(b + 1)
                    for i in range(I_TILES - LAG, I_TILES):
                        down(b, i, first)

                turn(0)
                body(0, True, False)
                with pe.Fori(1, BLOCKS - 1) as b:
                    body(b, False, False)
                body(BLOCKS - 1, False, True)


def build_ssm(nc, new_sem, x_in, x_out, w_all, conv, per_head, norm_w, ident, neg_half):
    T, C = x_in.shape
    K_TILES = C // P
    J = 4
    BLOCK = J * P
    BLOCKS = T // BLOCK
    TILES = T // P
    INNER = SSM_HEADS * SSM_HEAD
    X_TILES = INNER // P
    CONV_TILES = X_TILES + 1
    PART = 4
    PARTS = SSM_HEADS // PART
    LOG_FLOOR = -110.0
    LOG_RATE_MAX = 80.0
    W_BC = 0
    W_X = W_BC + K_TILES * P
    W_GATE = W_X + X_TILES * K_TILES * P
    W_OUT = W_GATE + 2 * K_TILES * 512
    W_COLS = W_OUT + X_TILES * C
    x_tile = x_in.rearrange("(t p) c -> t p c", p=P)
    y_tile = x_out.rearrange("(t p) c -> t p c", p=P)
    x_blk = x_in.rearrange("(b j p) c -> b p j c", p=P, j=J)

    pieces = [(W_BC, K_TILES * P)] + [(a, 1024) for a in range(W_X, W_COLS, 1024)]
    first_gate_piece = 1 + (W_GATE - W_X) // 1024
    first_out_piece = 1 + (W_OUT - W_X) // 1024

    order = [("turn", j) for j in range(J)] + [("conv", 0), ("conv", 1), ("out", -1)]
    for n in range(2, CONV_TILES + 2):
        if n < CONV_TILES:
            order.append(("conv", n))
        order.append(("tok", n - 2))
    order += [("gate", 0, 0), ("gate", 0, 1), ("decay", 0)]
    for q in range(J):
        order.append(("cb", q))
        if q:
            order += [("gate", q, 0), ("gate", q, 1), ("out", q - 1)]
    if len(order) % 2:
        order.append(None)
    at = {use: i for i, use in enumerate(order) if use}

    with ExitStack() as ctx:
        def sb(n, shape, dt=F32):
            return ctx.enter_context(nc.sbuf_tensor(f"ss_{n}", shape, dt))

        def sem(n):
            return new_sem(f"ss_{n}")

        w_hi = sb("w_hi", [P, W_COLS], F32R)
        w_lo = sb("w_lo", [P, W_COLS], F32R)
        conv_sb = sb("conv", [P, CONV_TILES, TAPS + 1])
        heads_sb = sb("heads", [P, 2, SSM_HEADS])
        rate = sb("rate", [P, SSM_HEADS])
        norm_sb = sb("norm", [P, X_TILES])
        upto = sb("upto", [P, P])
        beyond = sb("beyond", [P, P])
        ones = sb("ones", [P, P])
        u = sb("u", [P, J, C])
        u_hi = sb("u_hi", [P, J, C], F32R)
        u_lo = sb("u_lo", [P, J, C], F32R)
        res = sb("res", [P, 2, C])
        line = [sb(f"line{k}", [P, TAPS - 1 + BLOCK]) for k in range(2)]
        past = sb("past", [P, CONV_TILES, TAPS - 1])
        mixed = [sb(f"mixed{k}", [P, BLOCK]) for k in range(2)]
        bc = sb("bc", [P, BLOCK])
        c_rows = sb("c_rows", [STATE, BLOCK])
        x_tok = sb("x_tok", [P, J, INNER])
        bc_tok = sb("bc_tok", [P, J, P])
        small = [sb(f"dt_{n}", [P, J, SSM_HEADS]) for n in range(9)]
        dt_abs, dt_exp, dt_one, dt_log, dt_gap, dt_inv, dt_tail, dt, la = small
        decay = sb("decay", [P, 3, J * SSM_HEADS])
        spread = [sb(f"spread{k}", [P, PART, P]) for k in range(2)]
        mix = sb("mix", [P, SSM_HEADS, P])
        cb = sb("cb", [P, P])
        dtx = sb("dtx", [P, INNER])
        tail_x = sb("tail_x", [P, INNER])
        gate = sb("gate", [P, INNER])
        y = sb("y", [P, INNER])
        y_hi = sb("y_hi", [P, INNER], F32R)
        y_lo = sb("y_lo", [P, INNER], F32R)
        state = sb("state", [STATE, INNER])
        stats = sb("stats", [P, J, 6])
        mv = sb("mv", [P, J, 2])
        veps = sb("veps", [P, J])
        rstd = sb("rstd", [P, J])
        ssq = sb("ssq", [P, J])
        geps = sb("geps", [P, J])
        gnorm = sb("gnorm", [P, J])
        stage = [mix[:, 8 * k:8 * k + 8, :].rearrange("p h t -> p (h t)") for k in range(2)]

        proj = [ctx.enter_context(nc.psum_tensor(f"ss_proj{k}", [P, BLOCK], F32)) for k in range(2)]
        seg = [ctx.enter_context(nc.psum_tensor(f"ss_seg{k}", [P, PART * P], F32)) for k in range(2)]
        inside = ctx.enter_context(nc.psum_tensor("ss_inside", [P, INNER], F32))
        across = ctx.enter_context(nc.psum_tensor("ss_across", [P, INNER], F32))

        PRIME = 16
        primed = {}

        def primed_sem(n, engine):
            s = sem(n)
            primed.setdefault(engine, []).append(s)
            return s

        consts_in = sem("consts_in")
        norm_in = sem("norm_in")
        w_in = [sem(f"w_in{k}") for k in range(2)]
        w_scaled = sem("w_scaled")
        w_hi_made = sem("w_hi_made")
        w_split = sem("w_split")
        ones_made = sem("ones_made")
        masks_made = sem("masks_made")
        rate_capped = sem("rate_capped")
        rate_made = sem("rate_made")
        state_zeroed = sem("state_zeroed")
        x_landed = sem("x_landed")
        res_landed = [sem(f"res_landed{k}") for k in range(2)]
        stats_made = sem("stats_made")
        stats_seen = sem("stats_seen")
        mean_made = sem("mean_made")
        veps_made = sem("veps_made")
        rstd_made = sem("rstd_made")
        u_made = sem("u_made")
        turned = primed_sem("turned", "pe")
        uhi_made = sem("uhi_made")
        u_split = primed_sem("u_split", "dve")
        proj_done = sem("proj_done")
        filled = primed_sem("filled", "act")
        past_in = sem("past_in")
        mixing = sem("mixing")
        mixed_made = primed_sem("mixed_made", "dve")
        silu_made = primed_sem("silu_made", "act")
        rows_turned = primed_sem("rows_turned", "pe")
        tok_stored = primed_sem("tok_stored", "act")
        abs_made = sem("abs_made")
        exp_made = sem("exp_made")
        one_made = sem("one_made")
        log_made = sem("log_made")
        dt_step = sem("dt_step")
        la_made = sem("la_made")
        sums_done = sem("sums_done")
        decay_made = primed_sem("decay_made", "act")
        spread_made = sem("spread_made")
        seg_done = primed_sem("seg_done", "pe")
        seg_exp = primed_sem("seg_exp", "act")
        cb_done = primed_sem("cb_done", "pe")
        cb_masked = primed_sem("cb_masked", "dve")
        mix_made = primed_sem("mix_made", "dve")
        dtx_made = primed_sem("dtx_made", "dve")
        tail_made = primed_sem("tail_made", "pool")
        skip_made = primed_sem("skip_made", "pool")
        gate_done = sem("gate_done")
        gate_made = primed_sem("gate_made", "act")
        across_done = primed_sem("across_done", "pe")
        across_read = primed_sem("across_read", "dve")
        inside_done = primed_sem("inside_done", "pe")
        inside_read = sem("inside_read")
        gated = primed_sem("gated", "dve")
        state_done = primed_sem("state_done", "pe")
        state_decayed = sem("state_decayed")
        state_made = primed_sem("state_made", "dve")
        squared = primed_sem("squared", "act")
        geps_made = sem("geps_made")
        gnorm_made = primed_sem("gnorm_made", "pool")
        y_turned = primed_sem("y_turned", "pe")
        yhi_made = primed_sem("yhi_made", "act")
        y_split = primed_sem("y_split", "dve")
        out_done = primed_sem("out_done", "pe")
        y_made = primed_sem("y_made", "dve")
        y_stored = [sem(f"y_stored{k}") for k in range(2)]

        def prime(engine, name):
            for s in primed[name]:
                engine.sem_inc(s, PRIME)

        def released(engine, b, i):
            if i < 0:
                b, i = b - 1, i + len(order)
            use = order[i]
            if use is None:
                return released(engine, b, i - 2)
            kind, n = use[:2]
            if kind == "turn":
                engine.wait_ge(u_split, J * b + n + 1 + PRIME)
            elif kind == "conv":
                engine.wait_ge(filled, CONV_TILES * b + n + 1 + PRIME)
            elif kind == "tok":
                engine.wait_ge(tok_stored, CONV_TILES * b + n + 1 + PRIME)
            elif kind == "decay":
                engine.wait_ge(decay_made, b + 1 + PRIME)
            elif kind == "gate":
                engine.wait_ge(gate_made, 2 * (J * b + n) + use[2] + 1 + PRIME)
            elif kind == "cb":
                engine.wait_ge(cb_masked, J * b + n + 1 + PRIME)
            else:
                engine.wait_ge(y_made, J * b + n + 1 + PRIME)

        def by_head(ap, width=SSM_HEAD):
            return ap.rearrange("p (h d) -> p h d", d=width)

        def split3(a_hi, a_lo):
            return ((a_hi, w_hi), (a_hi, w_lo), (a_lo, w_hi))

        with nc.Block() as block:

            @block.sync
            def _(sp):
                sp.dma_start(u[:, :, :], x_blk[0]).then_inc(x_landed, 16)
                sp.dma_start(conv_sb[:, :, :], conv).then_inc(consts_in, 16)
                sp.dma_start(heads_sb[:, :, :], per_head.partition_broadcast(P)).then_inc(consts_in, 16)
                sp.dma_start(norm_sb[:, :], norm_w).then_inc(norm_in, 16)
                for n, (a, size) in enumerate(pieces):
                    if n >= 2:
                        sp.wait_ge(w_split, n - 1)
                    sp.dma_start(stage[n % 2][:, 0:size], w_all[:, a:a + size]).then_inc(w_in[n % 2], 16)
                for k in range(2):
                    sp.dma_start(res[:, k, :], x_tile[k]).then_inc(res_landed[k], 16)
                with sp.Fori(0, BLOCKS) as b:
                    with sp.If(b < BLOCKS - 1):
                        sp.wait_ge(turned, J * b + J + PRIME)
                        sp.dma_start(u[:, :, :], x_blk[(b + 1) % BLOCKS]).then_inc(x_landed, 16)
                    for q in range(J):
                        k, c = q % 2, J * b + q

                        def refill():
                            sp.wait_ge(y_stored[k], 16 * (2 * b + q // 2 + 1))
                            sp.dma_start(res[:, k, :], x_tile[(c + 2) % TILES]).then_inc(res_landed[k], 16)

                        sp.wait_ge(y_made, c + 1 + PRIME)
                        sp.dma_start(y_tile[c], res[:, k, :]).then_inc(y_stored[k], 16)
                        if q < J - 2:
                            refill()
                        else:
                            with sp.If(b < BLOCKS - 1):
                                refill()
                for k in range(2):
                    sp.wait_ge(y_stored[k], 16 * BLOCKS * J // 2)

            @block.gpsimd
            def _(pool):
                prime(pool, "pool")
                for m in (upto, beyond, ones):
                    last = pool.memset(m[:, :], 1.0)
                last.then_inc(ones_made, 1)
                pool.wait_ge(ones_made, 1)
                pool.affine_select(out=upto[:, :], in_=upto[:, :], compare_op=ALU.is_ge, fill=0.0, base=0,
                                   pattern=[[1, P]], channel_multiplier=-1).then_inc(masks_made, 1)
                pool.affine_select(out=beyond[:, :], in_=beyond[:, :], compare_op=ALU.is_ge, fill=0.0, base=-1,
                                   pattern=[[-1, P]], channel_multiplier=1).then_inc(masks_made, 1)
                pool.wait_ge(veps_made, 1)
                pool.tensor_tensor(rstd[:, :], veps[:, :], neg_half[:, 0:J], ALU.pow).then_inc(rstd_made, 1)
                pool.wait_ge(norm_in, 16)

                def scale_out(n):
                    if n < first_out_piece or n >= len(pieces):
                        return
                    pool.wait_ge(w_in[n % 2], 16 * (n // 2 + 1))
                    t = 2 * (n - first_out_piece)
                    rows = stage[n % 2].rearrange("p (c n) -> p c n", n=C)
                    pool.tensor_tensor(rows, rows, norm_sb[:, t:t + 2].unsqueeze(2).to_broadcast([P, 2, C]),
                                       ALU.mult).then_inc(w_scaled, 1)

                pool.wait_ge(masks_made, 2)
                pool.wait_ge(consts_in, 32)
                for n, (a, size) in enumerate(pieces):
                    scale_out(n + 1)
                    pool.wait_ge(w_hi_made, n + 1)
                    pool.tensor_tensor(w_lo[:, a:a + size], stage[n % 2][:, 0:size],
                                       w_hi[:, a:a + size].bitcast(F32), ALU.subtract).then_inc(w_split, 1)

                def gate_rms(b, q):
                    pool.wait_ge(geps_made, J * b + q + 1)
                    pool.tensor_tensor(gnorm[:, q:q + 1], geps[:, q:q + 1], neg_half[:, 0:1],
                                       ALU.pow).then_inc(gnorm_made, 1)

                with pool.Fori(0, BLOCKS) as b:
                    with pool.If(b > 0):
                        gate_rms(b - 1, J - 1)
                    pool.wait_ge(la_made, b + 1)
                    for q in range(J):
                        c = J * b + q
                        for p in range(PARTS):
                            i = PARTS * q + p
                            pool.wait_ge(seg_done, J * PARTS * b + i - 1 + PRIME)
                            pool.tensor_tensor(
                                spread[i % 2][:, :, :], upto[:, :].unsqueeze(1).to_broadcast([P, PART, P]),
                                la[:, q, p * PART:(p + 1) * PART].unsqueeze(2).to_broadcast([P, PART, P]),
                                ALU.mult).then_inc(spread_made, 1)
                        if q:
                            gate_rms(b, q - 1)
                        pool.wait_ge(gated, c + PRIME)
                        pool.wait_ge(y_turned, c + PRIME)
                        pool.wait_ge(squared, c + PRIME)
                        if q == 0:
                            pool.wait_ge(tok_stored, CONV_TILES * (b + 1) + PRIME)
                        pool.tensor_tensor(by_head(y[:, :]), by_head(x_tok[:, q, :]),
                                           heads_sb[:, 1, :].unsqueeze(2).to_broadcast([P, SSM_HEADS, SSM_HEAD]),
                                           ALU.mult).then_inc(skip_made, 1)
                        pool.wait_ge(dtx_made, c + 1 + PRIME)
                        pool.wait_ge(decay_made, b + 1 + PRIME)
                        pool.wait_ge(state_done, c + PRIME)
                        pool.tensor_tensor(
                            by_head(tail_x[:, :]), by_head(dtx[:, :]),
                            decay[:, 1, q * SSM_HEADS:(q + 1) * SSM_HEADS].unsqueeze(2).to_broadcast(
                                [P, SSM_HEADS, SSM_HEAD]), ALU.mult).then_inc(tail_made, 1)
                        if q == 2:
                            with pool.If(b < BLOCKS - 1):
                                pool.wait_ge(veps_made, b + 2)
                                pool.tensor_tensor(rstd[:, :], veps[:, :], neg_half[:, 0:J],
                                                   ALU.pow).then_inc(rstd_made, 1)
                gate_rms(BLOCKS - 1, J - 1)

            @block.scalar
            def _(act):
                prime(act, "act")

                def w_high(n):
                    a, size = pieces[n]
                    act.wait_ge(w_in[n % 2], 16 * (n // 2 + 1))
                    if n >= first_out_piece:
                        act.wait_ge(w_scaled, n - first_out_piece + 1)
                    act.activation(w_hi[:, a:a + size], stage[n % 2][:, 0:size], ACT.Copy).then_inc(w_hi_made, 1)

                def turn_y(b, q):
                    c = J * b + q
                    act.wait_ge(y_turned, c + 1 + PRIME)
                    act.wait_ge(out_done, c + PRIME)
                    act.activation(y_hi[:, :], inside[:, :], ACT.Copy).then_inc(yhi_made, 1)

                def square_y(b, q):
                    c = J * b + q
                    act.wait_ge(gated, c + 1 + PRIME)
                    act.activation(gate[:, :], y[:, :], ACT.Square, accum_out=ssq[:, q:q + 1]).then_inc(squared, 1)

                def fill(b, n):
                    act.wait_ge(proj_done, CONV_TILES * b + n + 1)
                    act.wait_ge(mixed_made, CONV_TILES * b + n - 1 + PRIME)
                    act.activation(line[n % 2][:, TAPS - 1:], proj[at["conv", n] % 2][:, :],
                                   ACT.Copy).then_inc(filled, 1)

                def silu(b, n):
                    act.wait_ge(mixed_made, CONV_TILES * b + n + 1 + PRIME)
                    if n:
                        act.activation(mixed[n % 2][:, :], mixed[n % 2][:, :], ACT.Silu).then_inc(silu_made, 1)
                        return
                    act.wait_ge(cb_done, J * b + PRIME)
                    act.wait_ge(across_done, J * b + PRIME)
                    act.activation(bc[0:DT_ROW, :], mixed[0][0:DT_ROW, :], ACT.Silu)
                    act.activation(bc[DT_ROW:P, :], mixed[0][DT_ROW:P, :], ACT.Copy)
                    act.activation(c_rows[:, :], mixed[0][C_ROW:C_ROW + STATE, :], ACT.Silu).then_inc(silu_made, 1)

                def store_tok(b, n):
                    act.wait_ge(rows_turned, CONV_TILES * b + n + 1 + PRIME)
                    bank = proj[at["tok", n] % 2][:, :].rearrange("p (q c) -> p q c", c=P)
                    if n == 0:
                        act.wait_ge(state_done, J * b + PRIME)
                        act.activation(bc_tok[:, :, :], bank, ACT.Copy).then_inc(tok_stored, 1)
                        return
                    if n == 1:
                        act.wait_ge(dtx_made, J * b + PRIME)
                        act.wait_ge(skip_made, J * b + PRIME)
                    act.activation(x_tok[:, :, (n - 1) * P:n * P], bank, ACT.Copy).then_inc(tok_stored, 1)

                def open_gate(b, q):
                    for half in range(2):
                        act.wait_ge(gate_done, 2 * (J * b + q) + half + 1)
                        if half == 0:
                            act.wait_ge(squared, J * b + q + PRIME)
                        act.activation(gate[:, half * 512:(half + 1) * 512],
                                       proj[at["gate", q, half] % 2][:, :], ACT.Silu).then_inc(gate_made, 1)

                w_high(0)
                w_high(1)
                act.wait_ge(rate_capped, 1)
                act.activation(rate[:, :], rate[:, :], ACT.Exp).then_inc(rate_made, 1)
                w_high(2)
                pending = list(range(3, len(pieces)))
                with act.Fori(0, BLOCKS) as b:
                    for j in range(J):
                        act.wait_ge(turned, J * b + j + 1 + PRIME)
                        act.wait_ge(gate_made, 2 * J * b + PRIME)
                        act.activation(u_hi[:, j, :], proj[at["turn", j] % 2][:, :], ACT.Copy).then_inc(uhi_made, 1)
                    with act.If(b > 0):
                        square_y(b - 1, J - 1)
                        turn_y(b - 1, J - 1)
                    for n in range(CONV_TILES + 2):
                        if n and pending:
                            with act.If(b < 1):
                                w_high(pending.pop(0))
                        if n < CONV_TILES:
                            fill(b, n)
                        if 1 <= n <= CONV_TILES:
                            silu(b, n - 1)
                        if n >= 2:
                            store_tok(b, n - 2)
                    act.activation(dt_abs[:, :, :], bc_tok[:, :, DT_ROW:DT_ROW + SSM_HEADS], ACT.Abs).then_inc(abs_made, 1)
                    open_gate(b, 0)
                    act.wait_ge(abs_made, b + 1)
                    act.activation(dt_exp[:, :, :], dt_abs[:, :, :], ACT.Exp, scale=-1.0).then_inc(exp_made, 1)
                    act.wait_ge(one_made, b + 1)
                    act.activation(dt_log[:, :, :], dt_one[:, :, :], ACT.Ln).then_inc(log_made, 1)
                    act.wait_ge(sums_done, b + 1)
                    act.wait_ge(state_made, J * b + PRIME)
                    act.wait_ge(across_read, J * b + PRIME)
                    act.wait_ge(tail_made, J * b + PRIME)
                    act.activation(decay[:, :, :].rearrange("p a n -> p (a n)"),
                                   proj[at["decay", 0] % 2][:, 0:3 * J * SSM_HEADS], ACT.Exp).then_inc(decay_made, 1)
                    for q in range(J):
                        for p in range(PARTS):
                            i = PARTS * q + p
                            act.wait_ge(seg_done, J * PARTS * b + i + 1 + PRIME)
                            if p == 0:
                                act.wait_ge(w_split, len(pieces))
                                act.wait_ge(inside_done, J * b + q + PRIME)
                            act.activation(mix[:, p * PART:(p + 1) * PART, :].rearrange("p h t -> p (h t)"),
                                           seg[i % 2][:, :], ACT.Exp).then_inc(seg_exp, 1)
                            if p == 1 and q:
                                square_y(b, q - 1)
                                open_gate(b, q)
                                turn_y(b, q - 1)
                square_y(BLOCKS - 1, J - 1)
                turn_y(BLOCKS - 1, J - 1)

            @block.vector
            def _(dve):
                prime(dve, "dve")

                def normalize(b):
                    dve.wait_ge(x_landed, b * 16 + 16)
                    for j in range(J):
                        dve.bn_stats(stats[:, j, :], u[:, j, :]).then_inc(stats_made, 1)
                    dve.wait_ge(stats_made, b * J + J)
                    dve.sem_inc(stats_seen, 1)
                    for j in range(J):
                        dve.bn_aggr(mv[:, j, :], stats[:, j, :]).then_inc(mean_made, 1)
                    dve.wait_ge(mean_made, b * J + J)
                    dve.tensor_scalar(veps[:, :], mv[:, :, 1], LN_EPS, None, ALU.add).then_inc(veps_made, 1)

                def apply_norm(b):
                    dve.wait_ge(rstd_made, b + 1)
                    for j in range(J):
                        dve.tensor_scalar(u[:, j, :], u[:, j, :], mv[:, j, 0:1], rstd[:, j:j + 1],
                                          ALU.subtract, ALU.mult).then_inc(u_made, 1)

                def y_low(b, q):
                    dve.wait_ge(yhi_made, J * b + q + 1 + PRIME)
                    dve.tensor_tensor(y_lo[:, :], inside[:, :], y_hi[:, :].bitcast(F32),
                                      ALU.subtract).then_inc(y_split, 1)

                def gate_eps(b, q):
                    dve.wait_ge(squared, J * b + q + 1 + PRIME)
                    dve.tensor_scalar(geps[:, q:q + 1], ssq[:, q:q + 1], 1.0 / INNER, GATE_EPS,
                                      ALU.mult, ALU.add).then_inc(geps_made, 1)

                def add_out(b, q):
                    c = J * b + q
                    dve.wait_ge(out_done, c + 1 + PRIME)
                    dve.wait_ge(gnorm_made, c + 1 + PRIME)
                    k = q % 2
                    dve.wait_ge(res_landed[k], 16 * (2 * b + q // 2 + 1))
                    dve.scalar_tensor_tensor(out=res[:, k, :], in0=proj[at["out", q if q < J - 1 else -1] % 2][:, :],
                                             scalar=gnorm[:, q:q + 1], in1=res[:, k, :], op0=ALU.mult,
                                             op1=ALU.add).then_inc(y_made, 1)

                def convolve(b, n):
                    i = CONV_TILES * b + n
                    src, dst = line[n % 2], mixed[n % 2]
                    dve.wait_ge(filled, i + 1 + PRIME)
                    dve.tensor_copy(src[:, 0:TAPS - 1], past[:, n, :]).then_inc(past_in, 1)
                    dve.wait_ge(past_in, i + 1)
                    dve.wait_ge(silu_made, i - 1 + PRIME)
                    dve.wait_ge(rows_turned, i - 1 + PRIME)
                    dve.tensor_scalar(dst[:, :], src[:, 0:BLOCK], conv_sb[:, n, 0:1], conv_sb[:, n, TAPS:TAPS + 1],
                                      ALU.mult, ALU.add).then_inc(mixing, 1)
                    dve.tensor_copy(past[:, n, :], src[:, BLOCK:BLOCK + TAPS - 1])
                    for k in range(1, TAPS):
                        dve.wait_ge(mixing, (TAPS - 1) * i + k)
                        ins = dve.scalar_tensor_tensor(out=dst[:, :], in0=src[:, k:k + BLOCK],
                                                       scalar=conv_sb[:, n, k:k + 1], in1=dst[:, :],
                                                       op0=ALU.mult, op1=ALU.add)
                        ins.then_inc(mixing if k < TAPS - 1 else mixed_made, 1)

                def time_steps(b):
                    raw = bc_tok[:, :, DT_ROW:DT_ROW + SSM_HEADS]
                    made = 0

                    def chain(ins):
                        nonlocal made
                        made += 1
                        ins.then_inc(dt_step, 1)
                        dve.wait_ge(dt_step, 9 * b + made)

                    dve.wait_ge(exp_made, b + 1)
                    dve.tensor_scalar(dt_one[:, :, :], dt_exp[:, :, :], 1.0, None, ALU.add).then_inc(one_made, 1)
                    dve.wait_ge(one_made, b + 1)
                    chain(dve.tensor_scalar(dt_gap[:, :, :], dt_one[:, :, :], 1.0, None, ALU.subtract))
                    chain(dve.tensor_scalar(dt_inv[:, :, :], dt_gap[:, :, :], 2.0 ** -24, None, ALU.max))
                    chain(dve.reciprocal(dt_inv[:, :, :], dt_inv[:, :, :]))
                    chain(dve.tensor_tensor(dt_inv[:, :, :], dt_inv[:, :, :], dt_exp[:, :, :], ALU.mult))
                    chain(dve.scalar_tensor_tensor(out=dt_tail[:, :, :], in0=dt_gap[:, :, :], scalar=0.0,
                                                   in1=dt_exp[:, :, :], op0=ALU.is_equal, op1=ALU.mult))
                    dve.wait_ge(log_made, b + 1)
                    chain(dve.tensor_tensor(dt_gap[:, :, :], dt_log[:, :, :], dt_inv[:, :, :], ALU.mult))
                    chain(dve.tensor_tensor(dt_gap[:, :, :], dt_gap[:, :, :], dt_tail[:, :, :], ALU.add))
                    chain(dve.scalar_tensor_tensor(out=dt[:, :, :], in0=raw, scalar=0.0, in1=dt_gap[:, :, :],
                                                   op0=ALU.max, op1=ALU.add))
                    dve.wait_ge(seg_done, J * PARTS * b + PRIME)
                    chain(dve.tensor_tensor(la[:, :, :], dt[:, :, :],
                                            rate[:, :].unsqueeze(1).to_broadcast([P, J, SSM_HEADS]), ALU.mult))
                    dve.tensor_scalar(la[:, :, :], la[:, :, :], -1.0, LOG_FLOOR, ALU.mult,
                                      ALU.max).then_inc(la_made, 1)

                def chunk(b, q):
                    c = J * b + q
                    heads = slice(q * SSM_HEADS, (q + 1) * SSM_HEADS)
                    if q == 0:
                        dve.wait_ge(tok_stored, CONV_TILES * (b + 1) + PRIME)
                    dve.wait_ge(inside_done, c + PRIME)
                    dve.wait_ge(tail_made, c + PRIME)
                    dve.tensor_tensor(by_head(dtx[:, :]), by_head(x_tok[:, q, :]),
                                      dt[:, q, :].unsqueeze(2).to_broadcast([P, SSM_HEADS, SSM_HEAD]),
                                      ALU.mult).then_inc(dtx_made, 1)
                    dve.wait_ge(cb_done, c + 1 + PRIME)
                    dve.tensor_tensor(cb[:, :], proj[at["cb", q] % 2][:, 0:P], upto[:, :],
                                      ALU.mult).then_inc(cb_masked, 1)
                    if q:
                        gate_eps(b, q - 1)
                    dve.wait_ge(cb_masked, c + 1 + PRIME)
                    for p in range(PARTS):
                        dve.wait_ge(seg_exp, PARTS * c + p + 1 + PRIME)
                        part = mix[:, p * PART:(p + 1) * PART, :]
                        dve.tensor_tensor(part, part, cb[:, :].unsqueeze(1).to_broadcast([P, PART, P]),
                                          ALU.mult).then_inc(mix_made, 1)
                        if p == 1 and q:
                            y_low(b, q - 1)
                    if q:
                        add_out(b, q - 1)
                    dve.wait_ge(across_done, c + 1 + PRIME)
                    dve.wait_ge(skip_made, c + 1 + PRIME)
                    dve.wait_ge(decay_made, b + 1 + PRIME)
                    for h in range(SSM_HEADS):
                        cols = slice(h * SSM_HEAD, (h + 1) * SSM_HEAD)
                        i = q * SSM_HEADS + h
                        last = dve.scalar_tensor_tensor(out=y[:, cols], in0=across[:, cols],
                                                        scalar=decay[:, 0, i:i + 1], in1=y[:, cols],
                                                        op0=ALU.mult, op1=ALU.add)
                    last.then_inc(across_read, 1)
                    dve.wait_ge(state_made, c + PRIME)
                    dve.tensor_tensor(by_head(state[:, :]), by_head(state[:, :]),
                                      decay[0:STATE, 2, heads].unsqueeze(2).to_broadcast(
                                          [STATE, SSM_HEADS, SSM_HEAD]), ALU.mult).then_inc(state_decayed, 1)
                    dve.wait_ge(inside_done, c + 1 + PRIME)
                    dve.wait_ge(across_read, c + 1 + PRIME)
                    dve.tensor_tensor(y[:, :], y[:, :], inside[:, :], ALU.add).then_inc(inside_read, 1)
                    dve.wait_ge(inside_read, c + 1)
                    dve.wait_ge(gate_made, 2 * c + 2 + PRIME)
                    dve.tensor_tensor(y[:, :], y[:, :], gate[:, :], ALU.mult).then_inc(gated, 1)
                    dve.wait_ge(state_decayed, c + 1)
                    dve.wait_ge(state_done, c + 1 + PRIME)
                    dve.tensor_tensor(state[:, :], state[:, :], across[0:STATE, :], ALU.add).then_inc(state_made, 1)

                dve.memset(state[:, :], 0.0).then_inc(state_zeroed, 1)
                dve.memset(past[:, :, :], 0.0).then_inc(state_zeroed, 1)
                dve.wait_ge(consts_in, 32)
                dve.tensor_scalar(rate[:, :], heads_sb[:, 0, :], LOG_RATE_MAX, None, ALU.min).then_inc(rate_capped, 1)
                normalize(0)
                apply_norm(0)
                dve.wait_ge(state_zeroed, 2)
                dve.wait_ge(rate_made, 1)
                dve.wait_ge(masks_made, 2)
                with dve.Fori(0, BLOCKS) as b:
                    for j in range(J):
                        dve.wait_ge(uhi_made, J * b + j + 1)
                        dve.tensor_tensor(u_lo[:, j, :], proj[at["turn", j] % 2][:, :], u_hi[:, j, :].bitcast(F32),
                                          ALU.subtract).then_inc(u_split, 1)
                    with dve.If(b > 0):
                        gate_eps(b - 1, J - 1)
                        y_low(b - 1, J - 1)
                    convolve(b, 0)
                    convolve(b, 1)
                    with dve.If(b > 0):
                        add_out(b - 1, J - 1)
                    for n in range(2, CONV_TILES):
                        convolve(b, n)
                    time_steps(b)
                    for q in range(J):
                        chunk(b, q)
                        if q == 1:
                            with dve.If(b < BLOCKS - 1):
                                normalize(b + 1)
                        if q == J - 1:
                            with dve.If(b < BLOCKS - 1):
                                apply_norm(b + 1)
                gate_eps(BLOCKS - 1, J - 1)
                y_low(BLOCKS - 1, J - 1)
                add_out(BLOCKS - 1, J - 1)

            @block.tensor
            def _(pe):
                prime(pe, "pe")

                def bank(b, use):
                    i = at[use]
                    released(pe, b, i - 2)
                    return proj[i % 2]

                def convolved(b, n):
                    dst = bank(b, ("conv", n))
                    pe.wait_ge(w_split, 1 if n == 0 else 2 + (n - 1) // 2)
                    for k in range(K_TILES):
                        a = W_BC + k * P if n == 0 else W_X + ((n - 1) * K_TILES + k) * P
                        cols = slice(k * P, (k + 1) * P)
                        for m, (w, v) in enumerate(((w_hi, u_hi), (w_hi, u_lo), (w_lo, u_hi))):
                            last = pe.matmul(dst[:, :], w[:, a:a + P], v[:, :, cols],
                                             start=(k == 0 and m == 0), stop=(k == K_TILES - 1 and m == 2))
                    last.then_inc(proj_done, 1)

                def rows(b, n):
                    dst = bank(b, ("tok", n))
                    pe.wait_ge(silu_made, CONV_TILES * b + n + 1 + PRIME)
                    src = mixed[n % 2] if n else bc
                    for q in range(J):
                        last = pe.transpose(dst[:, q * P:(q + 1) * P], src[:, q * P:(q + 1) * P], ident[:, :])
                    last.then_inc(rows_turned, 1)

                def gate_half(b, q, half):
                    dst = bank(b, ("gate", q, half))
                    pe.wait_ge(w_split, first_gate_piece + 2 * half + 2)
                    for k in range(K_TILES):
                        cols = slice(k * P, (k + 1) * P)
                        a = W_GATE + (half * K_TILES + k) * 512
                        for m, (v, w) in enumerate(split3(u_hi, u_lo)):
                            last = pe.matmul(dst[:, :], v[:, q, cols], w[:, a:a + 512],
                                             start=(k == 0 and m == 0), stop=(k == K_TILES - 1 and m == 2))
                    last.then_inc(gate_done, 1)

                def turn_y(b, q):
                    pe.wait_ge(gated, J * b + q + 1 + PRIME)
                    for t in range(X_TILES):
                        last = pe.transpose(inside[:, t * P:(t + 1) * P], y[:, t * P:(t + 1) * P], ident[:, :])
                    last.then_inc(y_turned, 1)

                def project(b, q, use):
                    src_block = b if use[1] >= 0 else b - 1
                    if isinstance(b, int):
                        i = at[use]
                        released(pe, b - 1, max(n for n, o in enumerate(order) if o and n % 2 == i % 2))
                        dst = proj[i % 2]
                    else:
                        dst = bank(b, use)
                    pe.wait_ge(w_split, len(pieces))
                    pe.wait_ge(y_split, J * src_block + q + 1 + PRIME)
                    for t in range(X_TILES):
                        cols = slice(t * P, (t + 1) * P)
                        a = W_OUT + t * C
                        for m, (v, w) in enumerate(split3(y_hi, y_lo)):
                            last = pe.matmul(dst[:, :], v[:, cols], w[:, a:a + C],
                                             start=(t == 0 and m == 0), stop=(t == X_TILES - 1 and m == 2))
                    last.then_inc(out_done, 1)

                def decays(b):
                    dst = bank(b, ("decay", 0))
                    pe.wait_ge(la_made, b + 1)
                    for m, mask in enumerate((upto, beyond, ones)):
                        last = pe.matmul(dst[:, m * J * SSM_HEADS:(m + 1) * J * SSM_HEADS], mask[:, :],
                                         la[:, :, :], start=True, stop=True)
                    last.then_inc(sums_done, 1)

                def segment(b, q, p):
                    i = PARTS * q + p
                    pe.wait_ge(spread_made, J * PARTS * b + i + 1)
                    pe.wait_ge(seg_exp, J * PARTS * b + i - 1 + PRIME)
                    pe.matmul(seg[i % 2][:, :], beyond[:, :], spread[i % 2][:, :, :].rearrange("p h t -> p (h t)"),
                              start=True, stop=True).then_inc(seg_done, 1)

                def products(b, q):
                    dst = bank(b, ("cb", q))
                    cols = slice(q * P, (q + 1) * P)
                    pe.matmul(dst[:, 0:P], bc[B_ROW:B_ROW + STATE, cols], c_rows[:, cols],
                              start=True, stop=True).then_inc(cb_done, 1)

                def from_state(b, q):
                    c = J * b + q
                    pe.wait_ge(state_made, c + PRIME)
                    for half in range(2):
                        cols = slice(half * 512, (half + 1) * 512)
                        last = pe.matmul(across[:, cols], c_rows[:, q * P:(q + 1) * P], state[:, cols],
                                         start=True, stop=True)
                    last.then_inc(across_done, 1)

                def from_chunk(b, q):
                    c = J * b + q
                    pe.wait_ge(y_split, c + PRIME)
                    pe.wait_ge(dtx_made, c + 1 + PRIME)
                    for h in range(SSM_HEADS):
                        if h % PART == 0:
                            pe.wait_ge(mix_made, PARTS * c + h // PART + 1 + PRIME)
                        cols = slice(h * SSM_HEAD, (h + 1) * SSM_HEAD)
                        last = pe.matmul(inside[:, cols], mix[:, h, :], dtx[:, cols], start=True, stop=True)
                    last.then_inc(inside_done, 1)

                def to_state(b, q):
                    c = J * b + q
                    pe.wait_ge(across_read, c + 1 + PRIME)
                    pe.wait_ge(tail_made, c + 1 + PRIME)
                    for half in range(2):
                        cols = slice(half * 512, (half + 1) * 512)
                        last = pe.matmul(across[0:STATE, cols], bc_tok[:, q, B_ROW:B_ROW + STATE],
                                         tail_x[:, cols], start=True, stop=True)
                    last.then_inc(state_done, 1)

                pe.wait_ge(masks_made, 2)
                with pe.Fori(0, BLOCKS) as b:
                    for j in range(J):
                        dst = bank(b, ("turn", j))
                        pe.wait_ge(u_made, J * b + j + 1)
                        for k in range(K_TILES):
                            last = pe.transpose(dst[:, k * P:(k + 1) * P], u[:, j, k * P:(k + 1) * P], ident[:, :])
                        last.then_inc(turned, 1)
                    with pe.If(b > 0):
                        turn_y(b - 1, J - 1)
                    pe.wait_ge(u_split, J * b + J + PRIME)
                    convolved(b, 0)
                    convolved(b, 1)
                    with pe.If(b > 0):
                        project(b, J - 1, ("out", -1))
                    for n in range(2, CONV_TILES + 2):
                        if n < CONV_TILES:
                            convolved(b, n)
                        rows(b, n - 2)
                    for half in range(2):
                        gate_half(b, 0, half)
                    decays(b)
                    for q in range(J):
                        products(b, q)
                        segment(b, q, 0)
                        segment(b, q, 1)
                        if q:
                            gate_half(b, q, 0)
                            gate_half(b, q, 1)
                            turn_y(b, q - 1)
                        segment(b, q, 2)
                        segment(b, q, 3)
                        if q:
                            project(b, q - 1, ("out", q - 1))
                        from_state(b, q)
                        from_chunk(b, q)
                        to_state(b, q)
                turn_y(BLOCKS - 1, J - 1)
                project(BLOCKS, J - 1, ("out", -1))


def build_program(nc, x, w_qkv, w_out, rope, w_ssm, conv, per_head, norm_w, w_ffn, ffn_scales,
                  down_scale, eye, out):
    T, C = x.shape
    K_TILES = C // P
    after = [nc.dram_tensor(f"x_after_{n}", [T, C], F32, kind="Internal").ap()
             for n in ("attention", "ffn", "ssm")]
    with ExitStack() as ctx:
        ident = ctx.enter_context(nc.sbuf_tensor("ident", [P, P], F32))
        neg_half = ctx.enter_context(nc.sbuf_tensor("neg_half", [P, 4], F32))

        def new_sem(name):
            return ctx.enter_context(nc.semaphore(name))

        ident_in = new_sem("ident_in")
        with nc.Block() as block:
            @block.sync
            def _(sp):
                sp.dma_start(ident[:, :], eye).then_inc(ident_in, 16)
                sp.wait_ge(ident_in, 16)

            @block.vector
            def _(dve):
                dve.memset(neg_half[:, :], -0.5)

        with ExitStack() as attention:
            q_all = attention.enter_context(nc.sbuf_tensor("q_all", [P, T // P, HEADS * HEAD], F32))
            k_stack = attention.enter_context(nc.sbuf_tensor("k_stack", [P, KV_HEADS, T], F32R))
            v_all = attention.enter_context(nc.sbuf_tensor("v_all", [P, T // P, KV_HEADS * HEAD], F32))
            build_qkv(nc, new_sem, x, w_qkv, rope, ident, neg_half, q_all, k_stack, v_all)
            build_attention(nc, new_sem, x, after[0], w_out, ident, q_all, k_stack, v_all)
        with ExitStack() as passing:
            own = []

            def own_sem(name):
                own.append(passing.enter_context(nc.semaphore(name)))
                return own[-1]

            build_ffn(nc, own_sem, "f1", after[0], after[1], w_ffn, ffn_scales, down_scale, ident, neg_half)
            with nc.Block() as block:
                @block.sync
                def _(sp):
                    for s in own:
                        sp.sem_clear(s)
        build_ssm(nc, new_sem, after[1], after[2], w_ssm, conv, per_head, norm_w, ident, neg_half)
        build_ffn(nc, new_sem, "f2", after[2], out, w_ffn, ffn_scales, down_scale, ident, neg_half)




def kernel(**inputs):
    import numpy as np
    import concourse.bacc as _bacc
    from concourse import mybir as _mybir
    from concourse.bass_utils import run_bass_kernel_spmd as _run

    f32 = np.float32
    a = {name.removeprefix("L0_"): np.asarray(value) for name, value in inputs.items()}
    _, T, C = a["attn_a_x"].shape
    K = C // P

    def rows_in_tiles(w):
        return w.reshape(-1, P, w.shape[1]).transpose(1, 0, 2)

    fraction = np.arange(0, HEAD, 2, dtype=f32) / f32(HEAD)
    inv_freq = (f32(1.0) / f32(10000.0) ** fraction).astype(f32)
    angle = np.arange(T, dtype=f32)[:, None] * inv_freq[None, :]
    cos, sin = np.cos(angle), np.sin(angle)
    rope = np.stack([np.concatenate([cos, cos], -1), np.concatenate([-sin, sin], -1)], 1)
    rope = rope.reshape(T // P, P, 2, HEAD).transpose(1, 0, 2, 3)

    w_qkv = np.concatenate([a["attn_a_q_kernel"], a["attn_a_k_kernel"], a["attn_a_v_kernel"]], 1)

    inner = SSM_HEADS * SSM_HEAD
    w_in = a["attn_b_W_in"]
    w_gate, w_x = w_in[:, 0:inner], w_in[:, inner:2 * inner]
    rest = w_in[:, 2 * inner:]
    w_bc = np.zeros((C, P), f32)
    w_bc[:, B_ROW:B_ROW + STATE] = rest[:, 0:STATE]
    w_bc[:, C_ROW:C_ROW + STATE] = rest[:, STATE:2 * STATE]
    w_bc[:, DT_ROW:DT_ROW + SSM_HEADS] = rest[:, 2 * STATE:]
    w_ssm = np.concatenate([
        rows_in_tiles(w_bc).reshape(P, -1),
        w_x.reshape(K, P, inner // P, P).transpose(1, 2, 0, 3).reshape(P, -1),
        w_gate.reshape(K, P, 2, inner // 2).transpose(1, 2, 0, 3).reshape(P, -1),
        rows_in_tiles(a["attn_b_W_out"]).reshape(P, -1)], 1)
    taps, bias = a["attn_b_conv_w"], a["attn_b_conv_b"]
    conv = np.zeros((P, 1 + inner // P, TAPS + 1), f32)
    conv[:, 1:, 0:TAPS] = taps[0:inner].reshape(-1, P, TAPS).transpose(1, 0, 2)
    conv[:, 1:, TAPS] = bias[0:inner].reshape(-1, P).T
    for row, start in ((B_ROW, inner), (C_ROW, inner + STATE)):
        conv[row:row + STATE, 0, 0:TAPS] = taps[start:start + STATE]
        conv[row:row + STATE, 0, TAPS] = bias[start:start + STATE]
    conv[DT_ROW:DT_ROW + SSM_HEADS, 0, TAPS - 1] = 1.0
    conv[DT_ROW:DT_ROW + SSM_HEADS, 0, TAPS] = a["attn_b_dt_bias"]
    per_head = np.stack([a["attn_b_A_log"], a["attn_b_D_skip"]])

    gate_w, up_w, down_w = a["ffn_gate_w"], a["ffn_up_w"], a["ffn_down_w"]
    I = gate_w.shape[0] // P
    gate_up = np.stack([gate_w.T.reshape(K, P, I, P), up_w.T.reshape(K, P, I, P)], 3)
    gate_up = gate_up.transpose(2, 1, 0, 3, 4).reshape(I, P, -1)
    w_ffn = np.concatenate([gate_up, down_w.T.reshape(I, P, C)], 2)
    ffn_scales = np.stack([a["ffn_gate_s"].reshape(I, P).T, a["ffn_up_s"].reshape(I, P).T], 1)

    arrays = {
        "x": a["attn_a_x"][0], "w_qkv": rows_in_tiles(w_qkv), "w_out": rows_in_tiles(a["attn_a_out_kernel"]),
        "rope": rope, "w_ssm": w_ssm, "conv": conv, "per_head": per_head,
        "norm_w": a["attn_b_norm_w"].reshape(-1, P).T, "w_ffn": w_ffn, "ffn_scales": ffn_scales,
        "down_scale": a["ffn_down_s"], "eye": np.eye(P, dtype=f32)}
    arrays = {n: np.ascontiguousarray(v) for n, v in arrays.items()}

    nc = _bacc.Bacc("TRN2", target_bir_lowering=False, num_devices=1)
    args = [nc.dram_tensor(n, v.shape, _mybir.dt.from_np(v.dtype), kind="ExternalInput").ap()
            for n, v in arrays.items()]
    args.append(nc.dram_tensor("out", [T, C], _mybir.dt.from_np(np.dtype(f32)), kind="ExternalOutput").ap())
    build_program(nc, *args)
    r = _run(nc, [arrays], core_ids=[0])
    return r.results[0]["out"].reshape(1, T, C)
```

```python
from contextlib import ExitStack

import concourse.bass as bass
from concourse import mybir

F32 = mybir.dt.float32
F32R = mybir.dt.float32r
ALU = mybir.AluOpType
ACT = mybir.ActivationFunctionType
AX = mybir.AxisListType

P = 128
LN_EPS = 1e-5
RMS_EPS = 1e-6
GATE_EPS = 1e-5

HEADS = 16
KV_HEADS = 4
GROUP = HEADS // KV_HEADS
HEAD = 32

SSM_HEADS = 16
SSM_HEAD = 64
STATE = 16
TAPS = 4
B_ROW, C_ROW, DT_ROW = 0, 32, 64


def build_qkv(nc, new_sem, x_in, w_qkv, rope, ident, neg_half, q_all, k_stack, v_all):
    T, C = x_in.shape
    K_TILES = C // P
    TILES = T // P
    QC, KC = HEADS * HEAD, KV_HEADS * HEAD
    N = QC + 2 * KC
    QK = QC + KC
    HALF = HEAD // 2
    x_tile = x_in.rearrange("(t p) c -> t p c", p=P)

    with ExitStack() as ctx:
        def sb(n, shape, dt=F32):
            return ctx.enter_context(nc.sbuf_tensor(f"qkv_{n}", shape, dt))

        def sem(n):
            return new_sem(f"qkv_{n}")

        def pair(n, shape, dt=F32):
            return [sb(f"{n}{k}", shape, dt) for k in range(2)]

        w_raw = sb("w_raw", [P, K_TILES, N])
        w_hi = sb("w_hi", [P, K_TILES, N], F32R)
        w_lo = sb("w_lo", [P, K_TILES, N], F32R)
        rope_sb = sb("rope", [P, TILES, 2, HEAD])
        x = pair("x", [P, C])
        u = pair("u", [P, C])
        u_hi = pair("u_hi", [P, C], F32R)
        u_lo = pair("u_lo", [P, C], F32R)
        stats = pair("stats", [P, 6])
        mv = pair("mv", [P, 2])
        veps = pair("veps", [P, 1])
        rstd = pair("rstd", [P, 1])
        square = pair("square", [P, QK])
        ssq = pair("ssq", [P, 2])
        qeps = pair("qeps", [P, 2])
        qk_rms = pair("qk_rms", [P, 2])
        normed = pair("normed", [P, QK])
        by_cos = pair("by_cos", [P, QK])
        by_sin = pair("by_sin", [P, QK])
        k_rot = pair("k_rot", [P, KC])
        k_rows = pair("k_rows", [P, KV_HEADS, 4, HEAD], F32R)

        def bank(n, cols):
            return [ctx.enter_context(nc.psum_tensor(f"qkv_{n}{k}", [P, cols], F32)) for k in range(2)]

        turn_ps = bank("turn_ps", 512)
        proj = bank("proj", 1024)
        k_ps = bank("k_ps", 512)

        w_in = sem("w_in")
        rope_in = sem("rope_in")
        w_hi_made = sem("w_hi_made")
        w_split = sem("w_split")
        x_landed = [sem(f"x_landed{k}") for k in range(2)]
        stats_made = sem("stats_made")
        stats_seen = sem("stats_seen")
        mean_made = sem("mean_made")
        veps_made = sem("veps_made")
        rstd_made = sem("rstd_made")
        u_made = sem("u_made")
        turned = sem("turned")
        uhi_made = sem("uhi_made")
        u_split = sem("u_split")
        proj_done = sem("proj_done")
        squares_made = sem("squares_made")
        qeps_made = sem("qeps_made")
        qk_rms_made = sem("qk_rms_made")
        normed_made = sem("normed_made")
        v_copied = sem("v_copied")
        cos_made = sem("cos_made")
        sin_made = sem("sin_made")
        q_made = sem("q_made")
        k_made = sem("k_made")
        khi_made = sem("khi_made")
        k_rows_made = sem("k_rows_made")
        k_turned = sem("k_turned")
        k_stored = sem("k_stored")

        LAGS = 4
        FIRST, LAST = 3, TILES // 2 - 1

        def steps(step):
            def run(engine):
                for t in range(2 * FIRST):
                    step(t // 2, t % 2, t)
                with engine.Fori(FIRST, LAST) as m:
                    for k in range(2):
                        step(m, k, 2 * m + k)
                for t in range(2 * LAST, TILES + LAGS):
                    step(t // 2, t % 2, t)
            return run

        def has(t, lag):
            return not isinstance(t, int) or 0 <= t - lag < TILES

        def freed(engine, signal, count):
            if not isinstance(count, int) or count > 0:
                engine.wait_ge(signal, count)

        def tile_of(tensor, t):
            return tensor[:, t] if isinstance(t, int) else tensor[:, bass.ds(t, 1)].squeeze(1)

        with nc.Block() as block:

            @block.sync
            def _(sp):
                sp.dma_start(x[0][:, :], x_tile[0]).then_inc(x_landed[0], 16)
                for c in range(K_TILES):
                    sp.dma_start(w_raw[:, c, :], w_qkv[:, c, :]).then_inc(w_in, 16)
                sp.dma_start(x[1][:, :], x_tile[1]).then_inc(x_landed[1], 16)
                sp.dma_start(rope_sb[:, :, :, :], rope).then_inc(rope_in, 16)
                with sp.Fori(1, TILES // 2) as m:
                    for k in range(2):
                        sp.wait_ge(u_made, 2 * m + k - 1)
                        sp.dma_start(x[k][:, :], x_tile[2 * m + k]).then_inc(x_landed[k], 16)

            @block.gpsimd
            def _(pool):
                def rstd_tile(t, k):
                    pool.wait_ge(veps_made, t + 1)
                    pool.tensor_tensor(rstd[k][:, :], veps[k][:, :], neg_half[:, 0:1],
                                       ALU.pow).then_inc(rstd_made, 1)

                def step(m, k, t):
                    if has(t, -1):
                        rstd_tile(t + 1, 1 - k)
                    if has(t, 2):
                        pool.wait_ge(qeps_made, t - 1)
                        pool.tensor_tensor(qk_rms[k][:, :], qeps[k][:, :], neg_half[:, 0:2],
                                           ALU.pow).then_inc(qk_rms_made, 1)
                        pool.wait_ge(normed_made, t - 1)
                        freed(pool, k_made, t - 3)
                        src = normed[k][:, :].rearrange("p (h s d) -> p h s d", s=2, d=HALF)
                        dst = by_sin[k][:, :].rearrange("p (h s d) -> p h s d", s=2, d=HALF)
                        sin = tile_of(rope_sb, t - 2)[:, 1, :]
                        for s in range(2):
                            last = pool.tensor_tensor(
                                dst[:, :, s, :], src[:, :, 1 - s, :],
                                sin[:, s * HALF:(s + 1) * HALF].unsqueeze(1).to_broadcast([P, QK // HEAD, HALF]),
                                ALU.mult)
                        last.then_inc(sin_made, 1)

                rstd_tile(0, 0)
                pool.wait_ge(w_hi_made, 1)
                pool.tensor_tensor(w_lo[:, :, :], w_raw[:, :, :], w_hi[:, :, :].bitcast(F32),
                                   ALU.subtract).then_inc(w_split, 1)
                pool.wait_ge(rope_in, 16)
                steps(step)(pool)

            @block.scalar
            def _(act):
                act.wait_ge(w_in, 16 * K_TILES)
                act.activation(w_hi[:, :, :], w_raw[:, :, :], ACT.Copy).then_inc(w_hi_made, 1)

                def step(m, k, t):
                    if has(t, 2):
                        act.wait_ge(proj_done, t - 1)
                        freed(act, squares_made, t - 3)
                        act.activation(square[k][:, 0:QC], proj[k][:, 0:QC], ACT.Square, accum_out=ssq[k][:, 0:1])
                        act.activation(square[k][:, QC:QK], proj[k][:, QC:QK], ACT.Square,
                                       accum_out=ssq[k][:, 1:2]).then_inc(squares_made, 1)
                    if has(t, 0):
                        act.wait_ge(turned, t + 1)
                        freed(act, proj_done, t - 1)
                        act.activation(u_hi[k][:, :], turn_ps[k][:, :], ACT.Copy).then_inc(uhi_made, 1)
                    if has(t, 2):
                        act.wait_ge(qk_rms_made, t - 1)
                        freed(act, sin_made, t - 3)
                        freed(act, cos_made, t - 3)
                        act.activation(normed[k][:, 0:QC], proj[k][:, 0:QC], ACT.Copy, scale=qk_rms[k][:, 0:1])
                        act.activation(normed[k][:, QC:QK], proj[k][:, QC:QK], ACT.Copy,
                                       scale=qk_rms[k][:, 1:2]).then_inc(normed_made, 1)
                        act.activation(tile_of(v_all, t - 2), proj[k][:, QK:N], ACT.Copy).then_inc(v_copied, 1)
                    if has(t, 4):
                        act.wait_ge(k_turned, t - 3)
                        act.activation(k_stack[:, :, bass.ds((t - 4) * P, P)],
                                       k_ps[k][:, :].rearrange("p (g s) -> p g s", g=KV_HEADS),
                                       ACT.Copy).then_inc(k_stored, 1)

                steps(step)(act)

            @block.vector
            def _(dve):
                def stats_tile(t, k, landed):
                    dve.wait_ge(x_landed[k], 16 * landed)
                    dve.bn_stats(stats[k][:, :], x[k][:, :]).then_inc(stats_made, 1)
                    dve.wait_ge(stats_made, t + 1)
                    dve.sem_inc(stats_seen, 1)
                    dve.bn_aggr(mv[k][:, :], stats[k][:, :]).then_inc(mean_made, 1)
                    dve.wait_ge(mean_made, t + 1)
                    dve.tensor_scalar(veps[k][:, :], mv[k][:, 1:2], LN_EPS, None, ALU.add).then_inc(veps_made, 1)

                def step(m, k, t):
                    if has(t, 0):
                        dve.wait_ge(rstd_made, t + 1)
                        freed(dve, turned, t - 1)
                        dve.tensor_scalar(u[k][:, :], x[k][:, :], mv[k][:, 0:1], rstd[k][:, 0:1],
                                          ALU.subtract, ALU.mult).then_inc(u_made, 1)
                    if has(t, -1):
                        stats_tile(t + 1, 1 - k, m + 1 + k)
                    if has(t, 2):
                        dve.wait_ge(squares_made, t - 1)
                        dve.tensor_scalar(qeps[k][:, 0:1], ssq[k][:, 0:1], 1.0 / QC, RMS_EPS, ALU.mult, ALU.add)
                        dve.tensor_scalar(qeps[k][:, 1:2], ssq[k][:, 1:2], 1.0 / KC, RMS_EPS, ALU.mult,
                                          ALU.add).then_inc(qeps_made, 1)
                    if has(t, 3):
                        dve.wait_ge(sin_made, t - 2)
                        dve.wait_ge(cos_made, t - 2)
                        dve.tensor_tensor(k_rot[1 - k][:, :], by_cos[1 - k][:, QC:QK], by_sin[1 - k][:, QC:QK],
                                          ALU.add)
                        dve.tensor_tensor(tile_of(q_all, t - 3), by_cos[1 - k][:, 0:QC], by_sin[1 - k][:, 0:QC],
                                          ALU.add).then_inc(k_made, 1)
                    if has(t, 0):
                        dve.wait_ge(uhi_made, t + 1)
                        dve.tensor_tensor(u_lo[k][:, :], turn_ps[k][:, :], u_hi[k][:, :].bitcast(F32),
                                          ALU.subtract).then_inc(u_split, 1)
                    if has(t, 3):
                        dve.wait_ge(k_made, t - 2)
                        freed(dve, k_turned, t - 4)
                        rot = k_rot[1 - k][:, :].rearrange("p (g d) -> p g d", d=HEAD)
                        rows = k_rows[1 - k]
                        for r in (0, 2):
                            last = dve.tensor_copy(rows[:, :, r, :], rot)
                        last.then_inc(khi_made, 1)
                        dve.wait_ge(khi_made, t - 2)
                        for r in (1, 3):
                            last = dve.tensor_tensor(rows[:, :, r, :], rot, rows[:, :, 0, :].bitcast(F32),
                                                     ALU.subtract)
                        last.then_inc(k_rows_made, 1)
                    if has(t, 2):
                        dve.wait_ge(normed_made, t - 1)
                        dve.tensor_tensor(
                            by_cos[k][:, :].rearrange("p (h d) -> p h d", d=HEAD),
                            normed[k][:, :].rearrange("p (h d) -> p h d", d=HEAD),
                            tile_of(rope_sb, t - 2)[:, 0, :].unsqueeze(1).to_broadcast([P, QK // HEAD, HEAD]),
                            ALU.mult).then_inc(cos_made, 1)

                stats_tile(0, 0, 1)
                dve.wait_ge(rope_in, 16)
                steps(step)(dve)

            @block.tensor
            def _(pe):
                def step(m, k, t):
                    if has(t, 0):
                        pe.wait_ge(u_made, t + 1)
                        freed(pe, u_split, t - 1)
                        for c in range(K_TILES):
                            last = pe.transpose(turn_ps[k][:, c * P:(c + 1) * P], u[k][:, c * P:(c + 1) * P],
                                                ident[:, :])
                        last.then_inc(turned, 1)
                    if has(t, 1):
                        j = 1 - k
                        pe.wait_ge(u_split, t)
                        if isinstance(t, int) and t == 1:
                            pe.wait_ge(w_split, 1)
                        freed(pe, v_copied, t - 2)
                        for a, b in ((0, QC), (QC, N)):
                            for c in range(K_TILES):
                                cols = slice(c * P, (c + 1) * P)
                                for n, (v, w) in enumerate(((u_hi, w_hi), (u_hi, w_lo), (u_lo, w_hi))):
                                    last = pe.matmul(proj[j][:, a:b], v[j][:, cols], w[:, c, a:b],
                                                     start=(c == 0 and n == 0),
                                                     stop=(c == K_TILES - 1 and n == 2))
                        last.then_inc(proj_done, 1)
                    if has(t, 4):
                        pe.wait_ge(k_rows_made, t - 3)
                        freed(pe, k_stored, t - 5)
                        for g in range(KV_HEADS):
                            last = pe.transpose(k_ps[k][:, g * P:(g + 1) * P],
                                                k_rows[k][:, g].rearrange("p r d -> p (r d)").bitcast(F32),
                                                ident[:, :])
                        last.then_inc(k_turned, 1)

                steps(step)(pe)


def build_attention(nc, new_sem, x_in, x_out, w_out, ident, q_all, k_stack, v_all):
    T, C = x_in.shape
    TILES = T // P
    J = 4
    BLOCK = J * P
    BLOCKS = T // BLOCK
    STEPS = TILES
    N = KV_HEADS * STEPS
    WIDE = GROUP * BLOCK
    RING = 4
    DVE_COLS = 1280
    SCALE = float(HEAD) ** -0.5
    x_blk = x_in.rearrange("(b j p) c -> b p j c", p=P, j=J)
    y_blk = x_out.rearrange("(b j p) c -> b p j c", p=P, j=J)

    Q_AT = (6, 8)
    OUT_AT = (12, 14)
    uses = []
    for n in range(N):
        if n % STEPS in Q_AT:
            uses.append(("q", n // STEPS, Q_AT.index(n % STEPS)))
        if n in OUT_AT:
            uses.append(("out", 0, OUT_AT.index(n)))
        uses += [("exp", n, 0), ("exp", n, 1)]
    assert len(uses) % 3 == 0
    place = {use: i for i, use in enumerate(uses)}

    with ExitStack() as ctx:
        def sb(n, shape, dt=F32):
            return ctx.enter_context(nc.sbuf_tensor(f"at_{n}", shape, dt))

        def sem(n):
            return new_sem(f"at_{n}")

        wo_raw = sb("wo_raw", [P, KV_HEADS, C])
        wo_hi = sb("wo_hi", [P, KV_HEADS, C], F32R)
        wo_lo = sb("wo_lo", [P, KV_HEADS, C], F32R)
        ones = sb("ones", [P, HEAD])
        q_rows = sb("q_rows", [P, J, GROUP, 4, HEAD], F32R)
        q_stack = [sb(f"q_stack{k}", [P, GROUP, BLOCK], F32R) for k in range(2)]
        probs = sb("probs", [P, RING, WIDE])
        sums = [sb(f"sums{k}", [P, WIDE]) for k in range(2)]
        pv_sb = sb("pv_sb", [P, BLOCK])
        inverse = sb("inverse", [P, BLOCK])
        enc = sb("enc", [P, BLOCK])
        enc_hi = sb("enc_hi", [P, KV_HEADS, BLOCK], F32R)
        enc_lo = sb("enc_lo", [P, KV_HEADS, BLOCK], F32R)
        y = sb("y", [P, J, C])
        slots = [ctx.enter_context(nc.psum_tensor(f"at_slot{k}", [P, 2, BLOCK], F32)) for k in range(3)]
        pv = ctx.enter_context(nc.psum_tensor("at_pv", [P, BLOCK], F32))
        den = ctx.enter_context(nc.psum_tensor("at_den", [P, BLOCK], F32))

        PRIME = 4
        qk_done = sem("qk_done")
        exp_done = sem("exp_done")
        pv_done = sem("pv_done")
        dve_added = sem("dve_added")
        pool_added = sem("pool_added")
        den_done = sem("den_done")
        inverted = sem("inverted")
        pv_saved = sem("pv_saved")
        enc_made = sem("enc_made")
        enc_hi_made = sem("enc_hi_made")
        enc_split = sem("enc_split")
        out_done = sem("out_done")
        qhi_made = sem("qhi_made")
        q_rows_made = sem("q_rows_made")
        q_turned = sem("q_turned")
        q_stacked = sem("q_stacked")
        wo_in = sem("wo_in")
        wo_hi_made = sem("wo_hi_made")
        wo_split = sem("wo_split")
        ones_made = sem("ones_made")
        y_seeded = sem("y_seeded")
        y_made = sem("y_made")
        y_stored = sem("y_stored")

        def exps(b, n, half):
            return b * (2 * N) + 2 * n + half + 1 + PRIME

        def adds(b, n):
            return b * (KV_HEADS * (STEPS - 1)) + (n // STEPS) * (STEPS - 1) + max(n % STEPS, 1) + PRIME

        def released(engine, b, i):
            if i < 0:
                b, i = b - 1, i + len(uses)
            kind, n, k = uses[i]
            if kind == "exp":
                engine.wait_ge(exp_done, exps(b, n, k))
            elif kind == "q":
                engine.wait_ge(q_stacked, b * (2 * KV_HEADS) + 2 * n + k + 3)
            else:
                engine.wait_ge(y_made, J * (b - 1) + 2 * k + 2 + PRIME)

        def add_step(engine, b, n, cols, added):
            s, acc = n % STEPS, sums[n // STEPS % 2]
            if s == 0:
                return
            engine.wait_ge(exp_done, exps(b, n, 1))
            if s == 1:
                engine.wait_ge(den_done, KV_HEADS * b + n // STEPS - 1 + PRIME)
                first = probs[:, (n - 1) % RING, cols]
            else:
                engine.wait_ge(added, adds(b, n - 1))
                first = acc[:, cols]
            engine.tensor_tensor(acc[:, cols], first, probs[:, n % RING, cols], ALU.add).then_inc(added, 1)

        with nc.Block() as block:

            @block.sync
            def _(sp):
                sp.dma_start(wo_raw[:, :, :], w_out).then_inc(wo_in, 16)
                sp.dma_start(y[:, :, :], x_blk[0]).then_inc(y_seeded, 16)
                with sp.Fori(1, BLOCKS) as b:
                    sp.wait_ge(y_made, J * b + PRIME)
                    sp.dma_start(y_blk[b - 1], y[:, :, :]).then_inc(y_stored, 16)
                    sp.wait_ge(y_stored, 16 * b)
                    sp.dma_start(y[:, :, :], x_blk[b]).then_inc(y_seeded, 16)
                sp.wait_ge(y_made, J * BLOCKS + PRIME)
                sp.dma_start(y_blk[BLOCKS - 1], y[:, :, :]).then_inc(y_stored, 16)
                sp.wait_ge(y_stored, 16 * BLOCKS)

            @block.gpsimd
            def _(pool):
                pool.sem_inc(pool_added, PRIME)
                pool.wait_ge(wo_hi_made, 1)
                pool.tensor_tensor(wo_lo[:, :, :], wo_raw[:, :, :], wo_hi[:, :, :].bitcast(F32),
                                   ALU.subtract).then_inc(wo_split, 1)
                cols = slice(DVE_COLS, WIDE)
                with pool.Fori(0, BLOCKS) as b:
                    for n in range(N):
                        add_step(pool, b, n, cols, pool_added)

            @block.scalar
            def _(act):
                for s in (exp_done, pv_saved, enc_hi_made):
                    act.sem_inc(s, PRIME)
                act.wait_ge(wo_in, 16)
                act.activation(wo_hi[:, :, :], wo_raw[:, :, :], ACT.Copy).then_inc(wo_hi_made, 1)

                def save_pv(b, g):
                    act.wait_ge(pv_done, b * N + (g + 1) * STEPS + PRIME)
                    act.wait_ge(enc_made, b * KV_HEADS + g + PRIME)
                    act.activation(pv_sb[:, :], pv[:, :], ACT.Copy).then_inc(pv_saved, 1)

                def enc_high(b, g):
                    act.wait_ge(enc_made, b * KV_HEADS + g + 1 + PRIME)
                    act.activation(enc_hi[:, g, :], enc[:, :], ACT.Copy).then_inc(enc_hi_made, 1)

                def stack_q(b, g, c):
                    i = place["q", g - 1, c] if g else c
                    act.wait_ge(q_turned, b * (2 * KV_HEADS) + 2 * g + c + 1)
                    out = q_stack[g % 2][:, :, 2 * c * P:2 * (c + 1) * P].rearrange("p h (j t) -> p j h t", t=P)
                    act.activation(out, slots[i % 3][:, :, :].rearrange("p j (h t) -> p j h t", t=P),
                                   ACT.Copy).then_inc(q_stacked, 1)

                for c in range(2):
                    stack_q(0, 0, c)
                with act.Fori(0, BLOCKS) as b:
                    for n in range(N):
                        g, s = divmod(n, STEPS)
                        if s in Q_AT:
                            c = Q_AT.index(s)
                            i = place["q", g, c]
                            act.wait_ge(q_turned, b * (2 * KV_HEADS) + 2 * g + c + 3)
                            out = q_stack[(g + 1) % 2][:, :, 2 * c * P:2 * (c + 1) * P].rearrange(
                                "p h (j t) -> p j h t", t=P)
                            act.activation(out, slots[i % 3][:, :, :].rearrange("p j (h t) -> p j h t", t=P),
                                           ACT.Copy).then_inc(q_stacked, 1)
                        for half in range(2):
                            act.wait_ge(qk_done, b * (2 * N) + 2 * n + half + 1)
                            if half == 0:
                                m = n - RING
                                act.wait_ge(pv_done, b * N + m + 1 + PRIME)
                                for added in (dve_added, pool_added):
                                    act.wait_ge(added, adds(b, m) if m >= 0 else adds(b - 1, m + N))
                            i = place["exp", n, half]
                            wide = probs[:, n % RING, half * 2 * BLOCK:(half + 1) * 2 * BLOCK]
                            act.activation(wide, slots[i % 3][:, :, :].rearrange("p h t -> p (h t)"),
                                           ACT.Exp, scale=SCALE).then_inc(exp_done, 1)
                        if s == 0:
                            if g:
                                save_pv(b, g - 1)
                            else:
                                with act.If(b > 0):
                                    save_pv(b - 1, KV_HEADS - 1)
                        if s == 7:
                            if g:
                                enc_high(b, g - 1)
                            else:
                                with act.If(b > 0):
                                    enc_high(b - 1, KV_HEADS - 1)
                save_pv(BLOCKS - 1, KV_HEADS - 1)
                enc_high(BLOCKS - 1, KV_HEADS - 1)

            @block.vector
            def _(dve):
                for s in (dve_added, inverted, enc_made, enc_split, y_made):
                    dve.sem_inc(s, PRIME)
                dve.memset(ones[:, :], 1.0).then_inc(ones_made, 1)

                def rows_q(b, g, unit):
                    src = q_all[:, bass.ds(b * J, J), g * P:(g + 1) * P].rearrange("p j (h d) -> p j h d", d=HEAD)
                    if not isinstance(unit, int) or unit:
                        dve.wait_ge(q_turned, 2 * unit)
                    for r in (0, 1):
                        last = dve.tensor_copy(q_rows[:, :, :, r, :], src)
                    last.then_inc(qhi_made, 1)
                    dve.wait_ge(qhi_made, unit + 1)
                    for r in (2, 3):
                        last = dve.tensor_tensor(q_rows[:, :, :, r, :], src, q_rows[:, :, :, 0, :].bitcast(F32),
                                                 ALU.subtract)
                    last.then_inc(q_rows_made, 1)

                def invert(b, g):
                    dve.wait_ge(den_done, b * KV_HEADS + g + 1 + PRIME)
                    dve.reciprocal(inverse[:, :], den[:, :]).then_inc(inverted, 1)

                def encode(b, g):
                    dve.wait_ge(inverted, b * KV_HEADS + g + 1 + PRIME)
                    dve.wait_ge(pv_saved, b * KV_HEADS + g + 1 + PRIME)
                    dve.wait_ge(enc_split, b * KV_HEADS + g + PRIME)
                    dve.tensor_tensor(enc[:, :], pv_sb[:, :], inverse[:, :], ALU.mult).then_inc(enc_made, 1)

                def enc_low(b, g):
                    dve.wait_ge(enc_hi_made, b * KV_HEADS + g + 1 + PRIME)
                    dve.tensor_tensor(enc_lo[:, g, :], enc[:, :], enc_hi[:, g, :].bitcast(F32),
                                      ALU.subtract).then_inc(enc_split, 1)

                def add_out(b, k, slot):
                    dve.wait_ge(y_seeded, 16 * b + 16)
                    dve.wait_ge(out_done, 2 * b + k + 1 + PRIME)
                    for j in range(2):
                        dve.tensor_tensor(y[:, 2 * k + j, :], y[:, 2 * k + j, :], slots[slot][:, j, :],
                                          ALU.add).then_inc(y_made, 1)

                rows_q(0, 0, 0)
                with dve.Fori(0, BLOCKS) as b:
                    for n in range(N):
                        g, s = divmod(n, STEPS)
                        add_step(dve, b, n, slice(0, DVE_COLS), dve_added)
                        if s == 1:
                            if g + 1 < KV_HEADS:
                                rows_q(b, g + 1, b * KV_HEADS + g + 1)
                            else:
                                rows_q((b + 1) % BLOCKS, 0, b * KV_HEADS + g + 1)
                        for at, do in ((3, invert), (5, encode), (9, enc_low)):
                            if s == at:
                                if g:
                                    do(b, g - 1)
                                else:
                                    with dve.If(b > 0):
                                        do(b - 1, KV_HEADS - 1)
                        if n + 1 in OUT_AT:
                            k = OUT_AT.index(n + 1)
                            with dve.If(b > 0):
                                add_out(b - 1, k, place["out", 0, k] % 3)
                for do in (invert, encode, enc_low):
                    do(BLOCKS - 1, KV_HEADS - 1)
                for k in range(2):
                    add_out(BLOCKS - 1, k, k)

            @block.tensor
            def _(pe):
                for s in (pv_done, den_done, out_done):
                    pe.sem_inc(s, PRIME)

                def turn_q(slot, c):
                    for j in range(2):
                        for h in range(GROUP):
                            last = pe.transpose(slots[slot][:, j, h * P:(h + 1) * P],
                                                q_rows[:, 2 * c + j, h].rearrange("p r d -> p (r d)").bitcast(F32),
                                                ident[:, :])
                    last.then_inc(q_turned, 1)

                def logits(b, n, half):
                    g, s = divmod(n, STEPS)
                    i = place["exp", n, half]
                    released(pe, b, i - 3)
                    if s == 0 and half == 0:
                        pe.wait_ge(q_stacked, b * (2 * KV_HEADS) + 2 * g + 2)
                    for h in range(2):
                        last = pe.matmul(slots[i % 3][:, h, :], k_stack[:, g, s * P:(s + 1) * P],
                                         q_stack[g % 2][:, 2 * half + h, :], start=True, stop=True)
                    last.then_inc(qk_done, 1)

                def values(b, n):
                    g, s = divmod(n, STEPS)
                    pe.wait_ge(exp_done, exps(b, n, 1))
                    if s == 0:
                        pe.wait_ge(pv_saved, b * KV_HEADS + g + PRIME)
                    for h in range(GROUP):
                        last = pe.matmul(pv[h * HEAD:(h + 1) * HEAD, :], v_all[:, s, g * HEAD:(g + 1) * HEAD],
                                         probs[:, n % RING, h * BLOCK:(h + 1) * BLOCK],
                                         start=(s == 0), stop=(s == STEPS - 1), tile_position=(0, h * HEAD))
                    last.then_inc(pv_done, 1)

                def denominators(b, g):
                    for added in (dve_added, pool_added):
                        pe.wait_ge(added, adds(b, (g + 1) * STEPS - 1))
                    pe.wait_ge(inverted, b * KV_HEADS + g + PRIME)
                    for h in range(GROUP):
                        last = pe.matmul(den[h * HEAD:(h + 1) * HEAD, :], ones[:, :],
                                         sums[g % 2][:, h * BLOCK:(h + 1) * BLOCK], start=True, stop=True,
                                         tile_position=(0, h * HEAD))
                    last.then_inc(den_done, 1)

                def project(b, k, slot):
                    pe.wait_ge(enc_split, (b + 1) * KV_HEADS + PRIME)
                    for j in range(2):
                        cols = slice((2 * k + j) * P, (2 * k + j + 1) * P)
                        for g in range(KV_HEADS):
                            for m, (e, w) in enumerate(((enc_hi, wo_hi), (enc_hi, wo_lo), (enc_lo, wo_hi))):
                                last = pe.matmul(slots[slot][:, j, :], e[:, g, cols], w[:, g, :],
                                                 start=(g == 0 and m == 0), stop=(g == KV_HEADS - 1 and m == 2))
                    last.then_inc(out_done, 1)

                pe.wait_ge(q_rows_made, 1)
                for c in range(2):
                    turn_q(c, c)
                pe.wait_ge(ones_made, 1)
                pe.wait_ge(wo_split, 1)
                with pe.Fori(0, BLOCKS) as b:
                    for n in range(N):
                        g, s = divmod(n, STEPS)
                        if s in Q_AT:
                            c = Q_AT.index(s)
                            i = place["q", g, c]
                            pe.wait_ge(q_rows_made, b * KV_HEADS + g + 2)
                            released(pe, b, i - 3)
                            turn_q(i % 3, c)
                        if n in OUT_AT:
                            k = OUT_AT.index(n)
                            i = place["out", 0, k]
                            with pe.If(b > 0):
                                released(pe, b, i - 3)
                                project(b - 1, k, i % 3)
                        logits(b, n, 0)
                        if n >= 2:
                            values(b, n - 2)
                        else:
                            with pe.If(b > 0):
                                values(b - 1, N + n - 2)
                        logits(b, n, 1)
                        if s == 3:
                            if g:
                                denominators(b, g - 1)
                            else:
                                with pe.If(b > 0):
                                    denominators(b - 1, KV_HEADS - 1)
                last = BLOCKS - 1
                for n in (N - 2, N - 1):
                    values(last, n)
                denominators(last, KV_HEADS - 1)
                for k in range(2):
                    if k == 0:
                        pe.wait_ge(exp_done, exps(last, N - 1, 1))
                        pe.wait_ge(q_stacked, 2 * KV_HEADS * BLOCKS + 2)
                    project(last, k, k)


def build_ffn(nc, new_sem, name, x_in, x_out, w_ffn, scales, down_scale, ident, neg_half, low_any,
              low_known):
    T, C = x_in.shape
    I_TILES = w_ffn.shape[0]
    K_TILES = C // P
    J = 4
    BLOCK = J * P
    BLOCKS = T // BLOCK
    GU = K_TILES * 2 * P
    LAG = 2
    x_blk = x_in.rearrange("(b j p) c -> b p j c", p=P, j=J)
    y_blk = x_out.rearrange("(b j p) c -> b p j c", p=P, j=J)

    with ExitStack() as ctx:
        def sb(n, shape, dt=F32):
            return ctx.enter_context(nc.sbuf_tensor(f"{name}_{n}", shape, dt))

        def sem(n):
            return new_sem(f"{name}_{n}")

        stage = sb("stage", [P, 2, GU + C])
        gu_hi = sb("gu_hi", [P, I_TILES, K_TILES, 2 * P], F32R)
        gu_lo = sb("gu_lo", [P, I_TILES, K_TILES, 2 * P], F32R)
        dn_hi = sb("dn_hi", [P, I_TILES, C], F32R)
        dn_lo = sb("dn_lo", [P, I_TILES, C], F32R)
        scale = sb("scale", [P, 2, I_TILES])
        ds_row = sb("ds_row", [P, C])
        x = sb("x", [P, J, C])
        y = sb("y", [P, J, C])
        u = sb("u", [P, J, C])
        u_hi = sb("u_hi", [P, K_TILES, BLOCK], F32R)
        u_lo = sb("u_lo", [P, K_TILES, BLOCK], F32R)
        act_g = sb("act_g", [P, BLOCK])
        h = sb("h", [P, BLOCK])
        h_hi = sb("h_hi", [P, 2, BLOCK], F32R)
        h_lo = sb("h_lo", [P, 2, BLOCK], F32R)
        low_max = sb("low_max", [P, I_TILES, 2])
        low_col = sb("low_col", [P, 1])
        low_row = sb("low_row", [1, P])
        low_top = sb("low_top", [1, 1])
        stats = sb("stats", [P, J, 6])
        mv = sb("mv", [P, J, 2])
        veps = sb("veps", [P, J])
        rstd = sb("rstd", [P, J])
        gu_ps = ctx.enter_context(nc.psum_tensor(f"{name}_gu_ps", [P, 2, 2, BLOCK], F32))
        acc = ctx.enter_context(nc.psum_tensor(f"{name}_acc", [P, J, C], F32))

        consts_in = sem("consts_in")
        w_in = [sem(f"w_in{k}") for k in range(2)]
        w_hi_made = sem("w_hi_made")
        w_split = sem("w_split")
        low_seen = sem("low_seen")
        low_col_made = sem("low_col_made")
        low_row_in = sem("low_row_in")
        low_top_made = sem("low_top_made")
        low_any_made = sem("low_any_made")
        x_landed = sem("x_landed")
        y_seeded = sem("y_seeded")
        stats_made = sem("stats_made")
        stats_seen = sem("stats_seen")
        mean_made = sem("mean_made")
        veps_made = sem("veps_made")
        rstd_made = sem("rstd_made")
        u_made = sem("u_made")
        turned = sem("turned")
        uhi_made = sem("uhi_made")
        u_split = sem("u_split")
        gu_done = sem("gu_done")
        silu_done = sem("silu_done")
        h_made = sem("h_made")
        hhi_made = sem("hhi_made")
        h_split = sem("h_split")
        down_done = sem("down_done")
        acc_scaled = sem("acc_scaled")
        y_made = sem("y_made")
        y_stored = sem("y_stored")

        def slot(i):
            return (i + 1) % 2

        with nc.Block() as block:

            @block.sync
            def _(sp):
                sp.dma_start(x[:, :, :], x_blk[0]).then_inc(x_landed, 16)
                sp.dma_start(scale[:, :, :], scales).then_inc(consts_in, 16)
                sp.dma_start(ds_row[:, :], down_scale.partition_broadcast(P)).then_inc(consts_in, 16)
                for i in range(I_TILES):
                    if i >= 2:
                        sp.wait_ge(w_split, i - 1)
                    sp.dma_start(stage[:, i % 2, :], w_ffn[i]).then_inc(w_in[i % 2], 16)
                    if i == 2:
                        sp.dma_start(y[:, :, :], x_blk[0]).then_inc(y_seeded, 16)
                        sp.wait_ge(u_made, J)
                        sp.dma_start(x[:, :, :], x_blk[1]).then_inc(x_landed, 16)
                def swap_y(b):
                    sp.wait_ge(y_made, b * J)
                    sp.dma_start(y_blk[b - 1], y[:, :, :]).then_inc(y_stored, 16)
                    sp.wait_ge(y_stored, b * 16)
                    sp.dma_start(y[:, :, :], x_blk[b]).then_inc(y_seeded, 16)

                if not low_known:
                    sp.wait_ge(low_col_made, 1)
                    sp.dma_start(low_row[:, :], low_col[:, :]).then_inc(low_row_in, 16)
                with sp.Fori(1, BLOCKS - 1) as b:
                    swap_y(b)
                    sp.wait_ge(u_made, b * J + J)
                    sp.dma_start(x[:, :, :], x_blk[b + 1]).then_inc(x_landed, 16)
                swap_y(BLOCKS - 1)
                sp.wait_ge(y_made, BLOCKS * J)
                sp.dma_start(y_blk[BLOCKS - 1], y[:, :, :]).then_inc(y_stored, 16)
                sp.wait_ge(y_stored, 16 * BLOCKS)

            @block.gpsimd
            def _(pool):
                def rstd_block(b):
                    pool.wait_ge(veps_made, b + 1)
                    pool.tensor_tensor(rstd[:, :], veps[:, :], neg_half[:, 0:J], ALU.pow).then_inc(rstd_made, 1)

                def finish_y(b):
                    pool.wait_ge(y_seeded, b * 16 + 16)
                    for j in range(J):
                        pool.wait_ge(acc_scaled, b * J + j + 1)
                        pool.tensor_tensor(y[:, j, :], y[:, j, :], u[:, j, :], ALU.add).then_inc(y_made, 1)

                rstd_block(0)
                for i in range(I_TILES):
                    pool.wait_ge(w_hi_made, i + 1)
                    raw = stage[:, i % 2, :]
                    pool.tensor_tensor(gu_lo[:, i].rearrange("p k n -> p (k n)"), raw[:, 0:GU],
                                       gu_hi[:, i].rearrange("p k n -> p (k n)").bitcast(F32), ALU.subtract)
                    pool.tensor_tensor(dn_lo[:, i, :], raw[:, GU:GU + C], dn_hi[:, i, :].bitcast(F32),
                                       ALU.subtract).then_inc(w_split, 1)
                with pool.Fori(1, BLOCKS) as b:
                    rstd_block(b)
                    finish_y(b - 1)
                finish_y(BLOCKS - 1)

            @block.scalar
            def _(act):
                def u_high(b):
                    for k in range(K_TILES):
                        act.wait_ge(turned, b * K_TILES + k + 1)
                        act.activation(u_hi[:, k, :], gu_ps[:, k // 2, k % 2, :], ACT.Copy).then_inc(uhi_made, 1)

                def w_high(i):
                    act.wait_ge(w_in[i % 2], 16 * (i // 2 + 1))
                    act.activation(gu_hi[:, i].rearrange("p k n -> p (k n)"), stage[:, i % 2, 0:GU], ACT.Copy)
                    act.activation(dn_hi[:, i, :], stage[:, i % 2, GU:GU + C], ACT.Copy).then_inc(w_hi_made, 1)

                def body(b, first, last):
                    for i in range(I_TILES):
                        if first and i + 2 < I_TILES:
                            w_high(i + 2)
                        act.wait_ge(gu_done, b * I_TILES + i + 1)
                        act.activation(act_g[:, :], gu_ps[:, slot(i), 0, :], ACT.Silu,
                                       scale=scale[:, 0, i:i + 1]).then_inc(silu_done, 1)
                        act.wait_ge(h_made, b * I_TILES + i + 1)
                        if not first or i >= 2:
                            act.wait_ge(down_done, b * I_TILES + i - 1)
                        act.activation(h_hi[:, i % 2, :], h[:, :], ACT.Copy).then_inc(hhi_made, 1)
                    if not last:
                        u_high(b + 1)

                w_high(0)
                w_high(1)
                u_high(0)
                act.wait_ge(consts_in, 32)
                body(0, True, False)
                with act.Fori(1, BLOCKS - 1) as b:
                    body(b, False, False)
                body(BLOCKS - 1, False, True)

            @block.vector
            def _(dve):
                def layernorm(b, first=False):
                    dve.wait_ge(x_landed, b * 16 + 16)
                    for j in range(J):
                        dve.bn_stats(stats[:, j, :], x[:, j, :]).then_inc(stats_made, 1)
                    dve.wait_ge(stats_made, b * J + J)
                    dve.sem_inc(stats_seen, 1)
                    for j in range(J):
                        dve.bn_aggr(mv[:, j, :], stats[:, j, :]).then_inc(mean_made, 1)
                    dve.wait_ge(mean_made, b * J + J)
                    dve.tensor_scalar(veps[:, :], mv[:, :, 1], LN_EPS, None, ALU.add).then_inc(veps_made, 1)
                    dve.wait_ge(rstd_made, b + 1)
                    if not first:
                        dve.wait_ge(y_made, (b - 1) * J)
                    for j in range(J):
                        dve.tensor_scalar(u[:, j, :], x[:, j, :], mv[:, j, 0:1], rstd[:, j:j + 1],
                                          ALU.subtract, ALU.mult).then_inc(u_made, 1)

                def low_parts(i):
                    dve.wait_ge(w_split, i + 1)
                    for n, low in enumerate((gu_lo[:, i].rearrange("p k n -> p (k n)"), dn_lo[:, i, :])):
                        dve.tensor_reduce(low_max[:, i, n:n + 1], low.bitcast(F32), AX.X, ALU.max,
                                          apply_absolute_value=True).then_inc(low_seen, 1)

                def u_low(b):
                    for k in range(K_TILES):
                        dve.wait_ge(uhi_made, b * K_TILES + k + 1)
                        dve.tensor_tensor(u_lo[:, k, :], gu_ps[:, k // 2, k % 2, :],
                                          u_hi[:, k, :].bitcast(F32), ALU.subtract).then_inc(u_split, 1)

                def body(b, first, last):
                    for i in range(I_TILES):
                        dve.wait_ge(silu_done, b * I_TILES + i + 1)
                        if not first or i >= 1:
                            dve.wait_ge(h_split, b * I_TILES + i)
                        dve.scalar_tensor_tensor(out=h[:, :], in0=gu_ps[:, slot(i), 1, :],
                                                 scalar=scale[:, 1, i:i + 1], in1=act_g[:, :],
                                                 op0=ALU.mult, op1=ALU.mult).then_inc(h_made, 1)
                        dve.wait_ge(hhi_made, b * I_TILES + i + 1)
                        dve.tensor_tensor(h_lo[:, i % 2, :], h[:, :], h_hi[:, i % 2, :].bitcast(F32),
                                          ALU.subtract).then_inc(h_split, 1)
                        if first and not low_known:
                            low_parts(i)
                        if i == 8 and not last:
                            layernorm(b + 1, first)
                    if first and not low_known:
                        dve.wait_ge(low_seen, 2 * I_TILES)
                        dve.tensor_reduce(low_col[:, :], low_max[:, :, :].rearrange("p i n -> p (i n)"), AX.X,
                                          ALU.max).then_inc(low_col_made, 1)
                    if not last:
                        u_low(b + 1)
                    if first and not low_known:
                        dve.wait_ge(low_row_in, 16)
                        dve.tensor_reduce(low_top[:, :], low_row[:, :], AX.X, ALU.max).then_inc(low_top_made, 1)
                        dve.wait_ge(low_top_made, 1)
                        dve.tensor_scalar(low_any[:, :], low_top[:, :], 0.0, None, ALU.is_gt).then_inc(low_any_made, 1)
                    if last:
                        dve.wait_ge(y_made, b * J)
                    dve.wait_ge(down_done, b * I_TILES + I_TILES)
                    for j in range(J):
                        dve.tensor_tensor(u[:, j, :], acc[:, j, :], ds_row[:, :], ALU.mult).then_inc(acc_scaled, 1)

                layernorm(0, True)
                u_low(0)
                dve.wait_ge(consts_in, 32)
                body(0, True, False)
                with dve.Fori(1, BLOCKS - 1) as b:
                    body(b, False, False)
                body(BLOCKS - 1, False, True)

            @block.tensor
            def _(pe):
                def turn(b):
                    for k in range(K_TILES):
                        for j in range(J):
                            if k == 0:
                                pe.wait_ge(u_made, b * J + j + 1)
                            last = pe.transpose(gu_ps[:, k // 2, k % 2, j * P:(j + 1) * P],
                                                u[:, j, k * P:(k + 1) * P], ident[:, :])
                        last.then_inc(turned, 1)

                def gate_up(b, i, first, low):
                    if i == 0:
                        pe.wait_ge(u_split, b * K_TILES + K_TILES)
                    if not (first and i < 2):
                        pe.wait_ge(h_made, b * I_TILES + i - 1)
                    if first:
                        pe.wait_ge(w_split if low else w_hi_made, i + 1)
                    for half in range(2):
                        for k in range(K_TILES):
                            w_hi = gu_hi[:, i, k, half * P:(half + 1) * P]
                            w_lo = gu_lo[:, i, k, half * P:(half + 1) * P]
                            terms = [(w_hi, u_hi), (w_hi, u_lo)] + ([(w_lo, u_hi)] if low else [])
                            for n, (w, v) in enumerate(terms):
                                last = pe.matmul(gu_ps[:, slot(i), half, :], w, v[:, k, :],
                                                 start=(k == 0 and n == 0),
                                                 stop=(k == K_TILES - 1 and n == len(terms) - 1))
                    last.then_inc(gu_done, 1)

                def down(b, i, first, low):
                    pe.wait_ge(h_split, b * I_TILES + i + 1)
                    if i == 0 and not first:
                        pe.wait_ge(acc_scaled, b * J)
                    for j in range(J):
                        cols = slice(j * P, (j + 1) * P)
                        terms = [(h_hi, dn_hi)] + ([(h_hi, dn_lo)] if low else []) + [(h_lo, dn_hi)]
                        for n, (a, w) in enumerate(terms):
                            last = pe.matmul(acc[:, j, :], a[:, i % 2, cols], w[:, i, :],
                                             start=(i == 0 and n == 0),
                                             stop=(i == I_TILES - 1 and n == len(terms) - 1))
                    last.then_inc(down_done, 1)

                def body(b, first, last, low):
                    for i in range(I_TILES):
                        gate_up(b, i, first, low)
                        if i >= LAG:
                            down(b, i - LAG, first, low)
                    if not last:
                        pe.wait_ge(h_made, b * I_TILES + I_TILES)
                        turn(b + 1)
                    for i in range(I_TILES - LAG, I_TILES):
                        down(b, i, first, low)

                def rest(low):
                    with pe.Fori(1, BLOCKS - 1) as b:
                        body(b, False, False, low)
                    body(BLOCKS - 1, False, True, low)

                def either(path):
                    any_low = pe.value_load(low_any[0:1, 0:1], min_val=0, max_val=1)
                    with pe.If(any_low > 0):
                        path(True)
                    with pe.If(any_low < 1):
                        path(False)

                turn(0)
                if low_known:
                    def whole(low):
                        body(0, True, False, low)
                        rest(low)

                    either(whole)
                else:
                    body(0, True, False, True)
                    pe.wait_ge(low_any_made, 1)
                    either(rest)


def build_ssm(nc, new_sem, x_in, x_out, w_all, conv, per_head, norm_w, ident, neg_half):
    T, C = x_in.shape
    K_TILES = C // P
    J = 4
    BLOCK = J * P
    BLOCKS = T // BLOCK
    TILES = T // P
    INNER = SSM_HEADS * SSM_HEAD
    X_TILES = INNER // P
    CONV_TILES = X_TILES + 1
    PART = 4
    PARTS = SSM_HEADS // PART
    LOG_FLOOR = -110.0
    LOG_RATE_MAX = 80.0
    W_BC = 0
    W_X = W_BC + K_TILES * P
    W_GATE = W_X + X_TILES * K_TILES * P
    W_OUT = W_GATE + 2 * K_TILES * 512
    W_COLS = W_OUT + X_TILES * C
    x_tile = x_in.rearrange("(t p) c -> t p c", p=P)
    y_tile = x_out.rearrange("(t p) c -> t p c", p=P)
    x_blk = x_in.rearrange("(b j p) c -> b p j c", p=P, j=J)

    pieces = [(W_BC, K_TILES * P)] + [(a, 1024) for a in range(W_X, W_COLS, 1024)]
    first_gate_piece = 1 + (W_GATE - W_X) // 1024
    first_out_piece = 1 + (W_OUT - W_X) // 1024

    order = [("conv", 0), ("out", -1), ("conv", 1), ("conv", 2), ("conv", 3), ("conv", 4), ("cb", 0)]
    order += [("conv", n) for n in range(5, CONV_TILES)]
    order += [("gate", 0, 0), ("gate", 0, 1), ("decay", 0)]
    for q in range(1, J):
        order += [("gate", q, 0), ("gate", q, 1), ("out", q - 1)]
    order += [("turn", 0), ("turn", 1)]
    if len(order) % 2:
        order.insert(-2, None)
    at = {use: i for i, use in enumerate(order) if use}

    with ExitStack() as ctx:
        def sb(n, shape, dt=F32):
            return ctx.enter_context(nc.sbuf_tensor(f"ss_{n}", shape, dt))

        def sem(n):
            return new_sem(f"ss_{n}")

        w_hi = sb("w_hi", [P, W_COLS], F32R)
        w_lo = sb("w_lo", [P, W_COLS], F32R)
        conv_sb = sb("conv", [P, CONV_TILES, TAPS + 1])
        heads_sb = sb("heads", [P, 2, SSM_HEADS])
        rate = sb("rate", [P, SSM_HEADS])
        norm_sb = sb("norm", [P, X_TILES])
        upto = sb("upto", [P, P])
        beyond = sb("beyond", [P, P])
        beyond_r = sb("beyond_r", [P, P], F32R)
        ones = sb("ones", [P, P])
        u = sb("u", [P, J, C])
        u_hi = sb("u_hi", [P, J, C], F32R)
        u_lo = sb("u_lo", [P, J, C], F32R)
        res = sb("res", [P, 2, C])
        line = [sb(f"line{k}", [P, TAPS - 1 + BLOCK]) for k in range(2)]
        past = sb("past", [P, CONV_TILES, TAPS - 1])
        mixed = [sb(f"mixed{k}", [P, BLOCK]) for k in range(2)]
        bc = sb("bc", [P, BLOCK])
        c_rows = sb("c_rows", [STATE, BLOCK])
        x_tok = sb("x_tok", [P, J, INNER])
        bc_tok = sb("bc_tok", [P, J, P])
        small = [sb(f"dt_{n}", [P, J, SSM_HEADS]) for n in range(9)]
        dt_abs, dt_exp, dt_one, dt_log, dt_gap, dt_inv, dt_tail, dt, la = small
        decay = sb("decay", [P, 3, J * SSM_HEADS])
        spread = [sb(f"spread_{n}", [P, PART, P], F32R) for n in ("hi", "lo")]
        la_hi = sb("la_hi", [P, J, SSM_HEADS], F32R)
        la_lo = sb("la_lo", [P, J, SSM_HEADS], F32R)
        mix = sb("mix", [P, SSM_HEADS, P])
        cb = sb("cb", [P, J, P])
        dtx = sb("dtx", [P, INNER])
        tail_x = sb("tail_x", [P, INNER])
        gate = sb("gate", [P, INNER])
        y = sb("y", [P, INNER])
        y_hi = sb("y_hi", [P, INNER], F32R)
        y_lo = sb("y_lo", [P, INNER], F32R)
        state = sb("state", [STATE, INNER])
        stats = sb("stats", [P, J, 6])
        mv = sb("mv", [P, J, 2])
        veps = sb("veps", [P, J])
        rstd = sb("rstd", [P, J])
        ssq = sb("ssq", [P, J])
        geps = sb("geps", [P, J])
        gnorm = sb("gnorm", [P, J])
        stage = [mix[:, 8 * k:8 * k + 8, :].rearrange("p h t -> p (h t)") for k in range(2)] + [dtx, tail_x]
        STAGES = len(stage)

        proj = [ctx.enter_context(nc.psum_tensor(f"ss_proj{k}", [P, BLOCK], F32)) for k in range(2)]
        seg = [ctx.enter_context(nc.psum_tensor(f"ss_seg{k}", [P, PART * P], F32)) for k in range(2)]
        inside = ctx.enter_context(nc.psum_tensor("ss_inside", [P, INNER], F32))
        across = ctx.enter_context(nc.psum_tensor("ss_across", [P, INNER], F32))

        PRIME = 16
        primed = {}

        def primed_sem(n, engine):
            s = sem(n)
            primed.setdefault(engine, []).append(s)
            return s

        consts_in = sem("consts_in")
        norm_in = sem("norm_in")
        w_in = [sem(f"w_in{k}") for k in range(STAGES)]
        w_scaled = sem("w_scaled")
        w_hi_made = sem("w_hi_made")
        w_split = sem("w_split")
        ones_made = sem("ones_made")
        masks_made = sem("masks_made")
        rate_capped = sem("rate_capped")
        rate_made = sem("rate_made")
        state_zeroed = sem("state_zeroed")
        x_landed = sem("x_landed")
        res_landed = [sem(f"res_landed{k}") for k in range(2)]
        stats_made = sem("stats_made")
        stats_seen = sem("stats_seen")
        mean_made = sem("mean_made")
        veps_made = sem("veps_made")
        rstd_made = sem("rstd_made")
        u_made = sem("u_made")
        turned = primed_sem("turned", "pe")
        uhi_made = sem("uhi_made")
        u_split = primed_sem("u_split", "dve")
        proj_done = sem("proj_done")
        filled = primed_sem("filled", "act")
        past_in = sem("past_in")
        mixing = sem("mixing")
        mixed_made = primed_sem("mixed_made", "dve")
        silu_made = primed_sem("silu_made", "act")
        rows_turned = primed_sem("rows_turned", "pe")
        tok_stored = primed_sem("tok_stored", "act")
        abs_made = sem("abs_made")
        exp_made = sem("exp_made")
        one_made = sem("one_made")
        log_made = sem("log_made")
        dt_step = sem("dt_step")
        la_capped = sem("la_capped")
        la_hi_made = sem("la_hi_made")
        la_made = sem("la_made")
        beyond_made = sem("beyond_made")
        sums_done = sem("sums_done")
        decay_made = primed_sem("decay_made", "act")
        spread_made = sem("spread_made")
        high_spread = sem("high_spread")
        seg_done = primed_sem("seg_done", "pe")
        seg_exp = primed_sem("seg_exp", "act")
        cb_done = primed_sem("cb_done", "pe")
        cb_masked = primed_sem("cb_masked", "dve")
        mix_made = primed_sem("mix_made", "dve")
        dtx_made = primed_sem("dtx_made", "dve")
        tail_made = primed_sem("tail_made", "pool")
        skip_made = primed_sem("skip_made", "pool")
        gate_done = sem("gate_done")
        gate_made = primed_sem("gate_made", "act")
        across_done = primed_sem("across_done", "pe")
        across_read = primed_sem("across_read", "dve")
        inside_done = primed_sem("inside_done", "pe")
        inside_read = sem("inside_read")
        gated = primed_sem("gated", "dve")
        state_done = primed_sem("state_done", "pe")
        state_decayed = sem("state_decayed")
        state_made = primed_sem("state_made", "dve")
        squared = primed_sem("squared", "act")
        geps_made = sem("geps_made")
        gnorm_made = primed_sem("gnorm_made", "pool")
        y_turned = primed_sem("y_turned", "pe")
        yhi_made = primed_sem("yhi_made", "act")
        y_split = primed_sem("y_split", "dve")
        out_done = primed_sem("out_done", "pe")
        y_made = primed_sem("y_made", "dve")
        y_stored = [sem(f"y_stored{k}") for k in range(2)]

        def prime(engine, name):
            for s in primed[name]:
                engine.sem_inc(s, PRIME)

        def released(engine, b, i):
            if i < 0:
                b, i = b - 1, i + len(order)
            use = order[i]
            if use is None:
                return released(engine, b, i - 2)
            kind, n = use[:2]
            if kind == "turn":
                engine.wait_ge(u_split, J * (b + 1) + n + 1 + PRIME)
            elif kind == "conv":
                engine.wait_ge(filled, CONV_TILES * b + n + 1 + PRIME)
            elif kind == "decay":
                engine.wait_ge(decay_made, b + 1 + PRIME)
            elif kind == "gate":
                engine.wait_ge(gate_made, 2 * (J * b + n) + use[2] + 1 + PRIME)
            elif kind == "cb":
                engine.wait_ge(cb_masked, b + 1 + PRIME)
            else:
                engine.wait_ge(y_made, J * b + n + 1 + PRIME)

        def turn_bank(j):
            return proj[at["turn", j] % 2] if j < 2 else seg[j % 2]

        def by_head(ap, width=SSM_HEAD):
            return ap.rearrange("p (h d) -> p h d", d=width)

        def split3(a_hi, a_lo):
            return ((a_hi, w_hi), (a_hi, w_lo), (a_lo, w_hi))

        with nc.Block() as block:

            @block.sync
            def _(sp):
                sp.dma_start(u[:, :, :], x_blk[0]).then_inc(x_landed, 16)
                sp.dma_start(conv_sb[:, :, :], conv).then_inc(consts_in, 16)
                sp.dma_start(heads_sb[:, :, :], per_head.partition_broadcast(P)).then_inc(consts_in, 16)
                sp.dma_start(norm_sb[:, :], norm_w).then_inc(norm_in, 16)
                for n, (a, size) in enumerate(pieces):
                    if n >= STAGES:
                        sp.wait_ge(w_split, n - STAGES + 1)
                    sp.dma_start(stage[n % STAGES][:, 0:size], w_all[:, a:a + size]).then_inc(w_in[n % STAGES], 16)
                for k in range(2):
                    sp.dma_start(res[:, k, :], x_tile[k]).then_inc(res_landed[k], 16)
                with sp.Fori(0, BLOCKS) as b:
                    with sp.If(b < BLOCKS - 1):
                        sp.wait_ge(turned, J * b + J + PRIME)
                        sp.dma_start(u[:, :, :], x_blk[(b + 1) % BLOCKS]).then_inc(x_landed, 16)
                    for q in range(J):
                        k, c = q % 2, J * b + q

                        def refill():
                            sp.wait_ge(y_stored[k], 16 * (2 * b + q // 2 + 1))
                            sp.dma_start(res[:, k, :], x_tile[(c + 2) % TILES]).then_inc(res_landed[k], 16)

                        sp.wait_ge(y_made, c + 1 + PRIME)
                        sp.dma_start(y_tile[c], res[:, k, :]).then_inc(y_stored[k], 16)
                        if q < J - 2:
                            refill()
                        else:
                            with sp.If(b < BLOCKS - 1):
                                refill()
                for k in range(2):
                    sp.wait_ge(y_stored[k], 16 * BLOCKS * J // 2)

            @block.gpsimd
            def _(pool):
                prime(pool, "pool")
                for m in (upto, beyond, ones):
                    last = pool.memset(m[:, :], 1.0)
                last.then_inc(ones_made, 1)
                pool.wait_ge(ones_made, 1)
                pool.affine_select(out=upto[:, :], in_=upto[:, :], compare_op=ALU.is_ge, fill=0.0, base=0,
                                   pattern=[[1, P]], channel_multiplier=-1).then_inc(masks_made, 1)
                pool.affine_select(out=beyond[:, :], in_=beyond[:, :], compare_op=ALU.is_ge, fill=0.0, base=-1,
                                   pattern=[[-1, P]], channel_multiplier=1).then_inc(masks_made, 1)
                pool.wait_ge(veps_made, 1)
                pool.tensor_tensor(rstd[:, :], veps[:, :], neg_half[:, 0:J], ALU.pow).then_inc(rstd_made, 1)
                pool.wait_ge(masks_made, 2)
                pool.wait_ge(consts_in, 32)
                for n, (a, size) in enumerate(pieces):
                    pool.wait_ge(w_hi_made, n + 1)
                    pool.tensor_tensor(w_lo[:, a:a + size], stage[n % STAGES][:, 0:size],
                                       w_hi[:, a:a + size].bitcast(F32), ALU.subtract).then_inc(w_split, 1)

                def gate_rms(b, q):
                    pool.wait_ge(geps_made, J * b + q + 1)
                    pool.tensor_tensor(gnorm[:, q:q + 1], geps[:, q:q + 1], neg_half[:, 0:1],
                                       ALU.pow).then_inc(gnorm_made, 1)

                with pool.Fori(0, BLOCKS) as b:
                    with pool.If(b > 0):
                        gate_rms(b - 1, J - 1)
                    pool.wait_ge(la_made, b + 1)
                    for q in range(J):
                        c = J * b + q
                        for p in range(PARTS):
                            i = PARTS * q + p
                            pool.wait_ge(seg_done, J * PARTS * b + i + PRIME)
                            for dst, log in list(zip(spread, (la_hi, la_lo)))[q == 0:]:
                                last = pool.tensor_tensor(
                                    dst[:, :, :], upto[:, :].unsqueeze(1).to_broadcast([P, PART, P]),
                                    log[:, q, p * PART:(p + 1) * PART].bitcast(F32).unsqueeze(2).to_broadcast(
                                        [P, PART, P]), ALU.mult)
                            last.then_inc(spread_made, 1)
                        if q:
                            gate_rms(b, q - 1)
                        pool.wait_ge(gated, c + PRIME)
                        pool.wait_ge(y_turned, c + PRIME)
                        pool.wait_ge(squared, c + PRIME)
                        if q == 0:
                            pool.wait_ge(tok_stored, CONV_TILES * (b + 1) + PRIME)
                        pool.tensor_tensor(by_head(y[:, :]), by_head(x_tok[:, q, :]),
                                           heads_sb[:, 1, :].unsqueeze(2).to_broadcast([P, SSM_HEADS, SSM_HEAD]),
                                           ALU.mult).then_inc(skip_made, 1)
                        pool.wait_ge(w_split, len(pieces))
                        pool.wait_ge(dtx_made, c + 1 + PRIME)
                        pool.wait_ge(decay_made, b + 1 + PRIME)
                        pool.wait_ge(state_done, c + PRIME)
                        pool.tensor_tensor(
                            by_head(tail_x[:, :]), by_head(dtx[:, :]),
                            decay[:, 1, q * SSM_HEADS:(q + 1) * SSM_HEADS].unsqueeze(2).to_broadcast(
                                [P, SSM_HEADS, SSM_HEAD]), ALU.mult).then_inc(tail_made, 1)
                        if q == 2:
                            with pool.If(b < BLOCKS - 1):
                                pool.wait_ge(veps_made, b + 2)
                                pool.tensor_tensor(rstd[:, :], veps[:, :], neg_half[:, 0:J],
                                                   ALU.pow).then_inc(rstd_made, 1)
                gate_rms(BLOCKS - 1, J - 1)

            @block.scalar
            def _(act):
                prime(act, "act")

                def w_high(n):
                    a, size = pieces[n]
                    raw = stage[n % STAGES]
                    act.wait_ge(w_in[n % STAGES], 16 * (n // STAGES + 1))
                    if n >= first_out_piece:
                        act.wait_ge(norm_in, 16)
                        for k in range(2):
                            t = 2 * (n - first_out_piece) + k
                            act.activation(raw[:, k * C:(k + 1) * C], raw[:, k * C:(k + 1) * C], ACT.Copy,
                                           scale=norm_sb[:, t:t + 1]).then_inc(w_scaled, 1)
                        act.wait_ge(w_scaled, 2 * (n - first_out_piece) + 2)
                    act.activation(w_hi[:, a:a + size], raw[:, 0:size], ACT.Copy).then_inc(w_hi_made, 1)

                def turn_y(b, q):
                    c = J * b + q
                    act.wait_ge(y_turned, c + 1 + PRIME)
                    act.wait_ge(out_done, c + PRIME)
                    act.activation(y_hi[:, :], inside[:, :], ACT.Copy).then_inc(yhi_made, 1)

                def square_y(b, q):
                    c = J * b + q
                    act.wait_ge(gated, c + 1 + PRIME)
                    act.activation(gate[:, :], y[:, :], ACT.Square, accum_out=ssq[:, q:q + 1]).then_inc(squared, 1)

                def fill(b, n):
                    act.wait_ge(proj_done, CONV_TILES * b + n + 1)
                    act.wait_ge(mixed_made, CONV_TILES * b + n - 1 + PRIME)
                    act.activation(line[n % 2][:, TAPS - 1:], proj[at["conv", n] % 2][:, :],
                                   ACT.Copy).then_inc(filled, 1)

                def silu(b, n):
                    act.wait_ge(mixed_made, CONV_TILES * b + n + 1 + PRIME)
                    if n:
                        act.activation(mixed[n % 2][:, :], mixed[n % 2][:, :], ACT.Silu).then_inc(silu_made, 1)
                        return
                    act.wait_ge(cb_done, b + PRIME)
                    act.wait_ge(across_done, J * b + PRIME)
                    act.activation(bc[0:DT_ROW, :], mixed[0][0:DT_ROW, :], ACT.Silu)
                    act.activation(bc[DT_ROW:P, :], mixed[0][DT_ROW:P, :], ACT.Copy)
                    act.activation(c_rows[:, :], mixed[0][C_ROW:C_ROW + STATE, :], ACT.Silu).then_inc(silu_made, 1)

                def store_tok(b, n):
                    act.wait_ge(rows_turned, CONV_TILES * b + n + 1 + PRIME)
                    bank = seg[n % 2][:, :].rearrange("p (q c) -> p q c", c=P)
                    if n == 0:
                        act.wait_ge(state_done, J * b + PRIME)
                        act.activation(bc_tok[:, :, :], bank, ACT.Copy).then_inc(tok_stored, 1)
                        return
                    if n == 1:
                        act.wait_ge(dtx_made, J * b + PRIME)
                        act.wait_ge(skip_made, J * b + PRIME)
                    act.activation(x_tok[:, :, (n - 1) * P:n * P], bank, ACT.Copy).then_inc(tok_stored, 1)

                def step_logs(b, n):
                    act.wait_ge(tok_stored, CONV_TILES * b + 1 + PRIME)
                    act.activation(dt_abs[:, :, :], bc_tok[:, :, DT_ROW:DT_ROW + SSM_HEADS], ACT.Abs).then_inc(abs_made, 1)
                    act.wait_ge(abs_made, b + 1)
                    act.activation(dt_exp[:, :, :], dt_abs[:, :, :], ACT.Exp, scale=-1.0).then_inc(exp_made, 1)
                    act.wait_ge(one_made, b + 1)
                    act.activation(dt_log[:, :, :], dt_one[:, :, :], ACT.Ln).then_inc(log_made, 1)

                def high_u(b):
                    for j in range(J):
                        act.wait_ge(turned, J * b + j + 1 + PRIME)
                        act.activation(u_hi[:, j, :], turn_bank(j)[:, :], ACT.Copy).then_inc(uhi_made, 1)

                def open_gate(b, q):
                    for half in range(2):
                        act.wait_ge(gate_done, 2 * (J * b + q) + half + 1)
                        if half == 0:
                            act.wait_ge(squared, J * b + q + PRIME)
                        act.activation(gate[:, half * 512:(half + 1) * 512],
                                       proj[at["gate", q, half] % 2][:, :], ACT.Silu).then_inc(gate_made, 1)

                w_high(0)
                w_high(1)
                act.wait_ge(rate_capped, 1)
                act.activation(rate[:, :], rate[:, :], ACT.Exp).then_inc(rate_made, 1)
                pending = list(range(3, len(pieces)))
                high_u(0)
                w_high(2)
                with act.Fori(0, BLOCKS) as b:
                    with act.If(b > 0):
                        square_y(b - 1, J - 1)
                        turn_y(b - 1, J - 1)
                    steps = [(fill, 0), (silu, 0), (fill, 1), (store_tok, 0), (step_logs, 0), (silu, 1), (fill, 2)]
                    for n in range(3, CONV_TILES):
                        steps += [(fill, n), (silu, n - 1), (store_tok, n - 2)]
                    n = CONV_TILES
                    steps += [(silu, n - 1), (store_tok, n - 2), (store_tok, n - 1)]
                    for i, (step, n) in enumerate(steps):
                        if i >= 1 and pending and (pending[0] < first_out_piece or i % 4 == 1):
                            with act.If(b < 1):
                                w_high(pending.pop(0))
                        step(b, n)
                    open_gate(b, 0)
                    for q in range(J):
                        for p in range(PARTS):
                            i = PARTS * q + p
                            act.wait_ge(seg_done, J * PARTS * b + i + 1 + PRIME)
                            if p == 0:
                                act.wait_ge(w_split, len(pieces))
                                act.wait_ge(inside_done, J * b + q + PRIME)
                            act.activation(mix[:, p * PART:(p + 1) * PART, :].rearrange("p h t -> p (h t)"),
                                           seg[(i + 1) % 2][:, :], ACT.Exp).then_inc(seg_exp, 1)
                            if p == 1 and q == 0:
                                act.wait_ge(sums_done, b + 1)
                                act.wait_ge(state_made, J * b + PRIME)
                                act.wait_ge(across_read, J * b + PRIME)
                                act.wait_ge(tail_made, J * b + PRIME)
                                act.activation(decay[:, :, :].rearrange("p a n -> p (a n)"),
                                               proj[at["decay", 0] % 2][:, 0:3 * J * SSM_HEADS], ACT.Exp).then_inc(decay_made, 1)
                            elif p == 1:
                                square_y(b, q - 1)
                                open_gate(b, q)
                                turn_y(b, q - 1)
                    with act.If(b < BLOCKS - 1):
                        high_u(b + 1)
                square_y(BLOCKS - 1, J - 1)
                turn_y(BLOCKS - 1, J - 1)

            @block.vector
            def _(dve):
                prime(dve, "dve")

                def normalize(b):
                    dve.wait_ge(x_landed, b * 16 + 16)
                    for j in range(J):
                        dve.bn_stats(stats[:, j, :], u[:, j, :]).then_inc(stats_made, 1)
                    dve.wait_ge(stats_made, b * J + J)
                    dve.sem_inc(stats_seen, 1)
                    for j in range(J):
                        dve.bn_aggr(mv[:, j, :], stats[:, j, :]).then_inc(mean_made, 1)
                    dve.wait_ge(mean_made, b * J + J)
                    dve.tensor_scalar(veps[:, :], mv[:, :, 1], LN_EPS, None, ALU.add).then_inc(veps_made, 1)

                def apply_norm(b):
                    dve.wait_ge(rstd_made, b + 1)
                    for j in range(J):
                        dve.tensor_scalar(u[:, j, :], u[:, j, :], mv[:, j, 0:1], rstd[:, j:j + 1],
                                          ALU.subtract, ALU.mult).then_inc(u_made, 1)

                def y_low(b, q):
                    dve.wait_ge(yhi_made, J * b + q + 1 + PRIME)
                    dve.tensor_tensor(y_lo[:, :], inside[:, :], y_hi[:, :].bitcast(F32),
                                      ALU.subtract).then_inc(y_split, 1)

                def gate_eps(b, q):
                    dve.wait_ge(squared, J * b + q + 1 + PRIME)
                    dve.tensor_scalar(geps[:, q:q + 1], ssq[:, q:q + 1], 1.0 / INNER, GATE_EPS,
                                      ALU.mult, ALU.add).then_inc(geps_made, 1)

                def add_out(b, q):
                    c = J * b + q
                    dve.wait_ge(out_done, c + 1 + PRIME)
                    dve.wait_ge(gnorm_made, c + 1 + PRIME)
                    k = q % 2
                    dve.wait_ge(res_landed[k], 16 * (2 * b + q // 2 + 1))
                    dve.scalar_tensor_tensor(out=res[:, k, :], in0=proj[at["out", q if q < J - 1 else -1] % 2][:, :],
                                             scalar=gnorm[:, q:q + 1], in1=res[:, k, :], op0=ALU.mult,
                                             op1=ALU.add).then_inc(y_made, 1)

                def convolve(b, n):
                    i = CONV_TILES * b + n
                    src, dst = line[n % 2], mixed[n % 2]
                    dve.wait_ge(filled, i + 1 + PRIME)
                    dve.tensor_copy(src[:, 0:TAPS - 1], past[:, n, :]).then_inc(past_in, 1)
                    dve.wait_ge(past_in, i + 1)
                    dve.wait_ge(silu_made, i - 1 + PRIME)
                    dve.wait_ge(rows_turned, i - 1 + PRIME)
                    dve.tensor_scalar(dst[:, :], src[:, 0:BLOCK], conv_sb[:, n, 0:1], conv_sb[:, n, TAPS:TAPS + 1],
                                      ALU.mult, ALU.add).then_inc(mixing, 1)
                    dve.tensor_copy(past[:, n, :], src[:, BLOCK:BLOCK + TAPS - 1])
                    for k in range(1, TAPS):
                        dve.wait_ge(mixing, (TAPS - 1) * i + k)
                        ins = dve.scalar_tensor_tensor(out=dst[:, :], in0=src[:, k:k + BLOCK],
                                                       scalar=conv_sb[:, n, k:k + 1], in1=dst[:, :],
                                                       op0=ALU.mult, op1=ALU.add)
                        ins.then_inc(mixing if k < TAPS - 1 else mixed_made, 1)

                def low_u(b):
                    for j in range(J):
                        dve.wait_ge(uhi_made, J * b + j + 1)
                        dve.tensor_tensor(u_lo[:, j, :], turn_bank(j)[:, :], u_hi[:, j, :].bitcast(F32),
                                          ALU.subtract).then_inc(u_split, 1)

                def chain(b, made, ins):
                    ins.then_inc(dt_step, 1)
                    dve.wait_ge(dt_step, 9 * b + made)

                def log_terms(b):
                    dve.wait_ge(exp_made, b + 1)
                    dve.tensor_scalar(dt_one[:, :, :], dt_exp[:, :, :], 1.0, None, ALU.add).then_inc(one_made, 1)
                    dve.wait_ge(one_made, b + 1)
                    chain(b, 1, dve.tensor_scalar(dt_gap[:, :, :], dt_one[:, :, :], 1.0, None, ALU.subtract))
                    chain(b, 2, dve.tensor_scalar(dt_inv[:, :, :], dt_gap[:, :, :], 2.0 ** -24, None, ALU.max))
                    chain(b, 3, dve.reciprocal(dt_inv[:, :, :], dt_inv[:, :, :]))
                    chain(b, 4, dve.tensor_tensor(dt_inv[:, :, :], dt_inv[:, :, :], dt_exp[:, :, :], ALU.mult))
                    chain(b, 5, dve.scalar_tensor_tensor(out=dt_tail[:, :, :], in0=dt_gap[:, :, :], scalar=0.0,
                                                         in1=dt_exp[:, :, :], op0=ALU.is_equal, op1=ALU.mult))

                def time_steps(b):
                    raw = bc_tok[:, :, DT_ROW:DT_ROW + SSM_HEADS]
                    dve.wait_ge(log_made, b + 1)
                    chain(b, 6, dve.tensor_tensor(dt_gap[:, :, :], dt_log[:, :, :], dt_inv[:, :, :], ALU.mult))
                    chain(b, 7, dve.tensor_tensor(dt_gap[:, :, :], dt_gap[:, :, :], dt_tail[:, :, :], ALU.add))
                    dve.wait_ge(tok_stored, CONV_TILES * b + 1 + PRIME)
                    chain(b, 8, dve.scalar_tensor_tensor(out=dt[:, :, :], in0=raw, scalar=0.0, in1=dt_gap[:, :, :],
                                                         op0=ALU.max, op1=ALU.add))
                    dve.wait_ge(seg_done, J * PARTS * b + PRIME)
                    chain(b, 9, dve.tensor_tensor(la[:, :, :], dt[:, :, :],
                                                  rate[:, :].unsqueeze(1).to_broadcast([P, J, SSM_HEADS]), ALU.mult))
                    dve.tensor_scalar(la[:, :, :], la[:, :, :], -1.0, LOG_FLOOR, ALU.mult,
                                      ALU.max).then_inc(la_capped, 1)
                    dve.wait_ge(la_capped, b + 1)
                    dve.tensor_copy(la_hi[:, :, :], la[:, :, :]).then_inc(la_hi_made, 1)
                    dve.wait_ge(la_hi_made, b + 1)
                    dve.tensor_tensor(la_lo[:, :, :], la[:, :, :], la_hi[:, :, :].bitcast(F32),
                                      ALU.subtract).then_inc(la_made, 1)

                def spread_high(b, p):
                    if p:
                        dve.wait_ge(seg_done, J * PARTS * b + p + PRIME)
                    else:
                        dve.wait_ge(la_made, b + 1)
                    dve.tensor_tensor(
                        spread[0][:, :, :], upto[:, :].unsqueeze(1).to_broadcast([P, PART, P]),
                        la_hi[:, 0, p * PART:(p + 1) * PART].bitcast(F32).unsqueeze(2).to_broadcast([P, PART, P]),
                        ALU.mult).then_inc(high_spread, 1)

                def mask_cb(b):
                    dve.wait_ge(cb_done, b + 1 + PRIME)
                    dve.wait_ge(mix_made, PARTS * J * b + PRIME)
                    dve.tensor_tensor(cb[:, :, :], proj[at["cb", 0] % 2][:, :].rearrange("p (q t) -> p q t", t=P),
                                      upto[:, :].unsqueeze(1).to_broadcast([P, J, P]),
                                      ALU.mult).then_inc(cb_masked, 1)

                def chunk(b, q):
                    c = J * b + q
                    heads = slice(q * SSM_HEADS, (q + 1) * SSM_HEADS)
                    if q == 0:
                        spread_high(b, 1)
                        dve.wait_ge(tok_stored, CONV_TILES * (b + 1) + PRIME)
                    dve.wait_ge(inside_done, c + PRIME)
                    dve.wait_ge(tail_made, c + PRIME)
                    dve.wait_ge(w_split, len(pieces))
                    dve.tensor_tensor(by_head(dtx[:, :]), by_head(x_tok[:, q, :]),
                                      dt[:, q, :].unsqueeze(2).to_broadcast([P, SSM_HEADS, SSM_HEAD]),
                                      ALU.mult).then_inc(dtx_made, 1)
                    if q == 0:
                        spread_high(b, 2)
                        spread_high(b, 3)
                    if q:
                        gate_eps(b, q - 1)
                    dve.wait_ge(cb_masked, b + 1 + PRIME)
                    for p in range(PARTS):
                        dve.wait_ge(seg_exp, PARTS * c + p + 1 + PRIME)
                        part = mix[:, p * PART:(p + 1) * PART, :]
                        dve.tensor_tensor(part, part, cb[:, q, :].unsqueeze(1).to_broadcast([P, PART, P]),
                                          ALU.mult).then_inc(mix_made, 1)
                        if p == 1 and q:
                            y_low(b, q - 1)
                    dve.wait_ge(across_done, c + 1 + PRIME)
                    dve.wait_ge(skip_made, c + 1 + PRIME)
                    dve.wait_ge(decay_made, b + 1 + PRIME)
                    for h in range(SSM_HEADS):
                        cols = slice(h * SSM_HEAD, (h + 1) * SSM_HEAD)
                        i = q * SSM_HEADS + h
                        last = dve.scalar_tensor_tensor(out=y[:, cols], in0=across[:, cols],
                                                        scalar=decay[:, 0, i:i + 1], in1=y[:, cols],
                                                        op0=ALU.mult, op1=ALU.add)
                    last.then_inc(across_read, 1)
                    if q:
                        add_out(b, q - 1)
                    dve.wait_ge(state_made, c + PRIME)
                    dve.tensor_tensor(by_head(state[:, :]), by_head(state[:, :]),
                                      decay[0:STATE, 2, heads].unsqueeze(2).to_broadcast(
                                          [STATE, SSM_HEADS, SSM_HEAD]), ALU.mult).then_inc(state_decayed, 1)
                    dve.wait_ge(inside_done, c + 1 + PRIME)
                    dve.wait_ge(across_read, c + 1 + PRIME)
                    dve.tensor_tensor(y[:, :], y[:, :], inside[:, :], ALU.add).then_inc(inside_read, 1)
                    dve.wait_ge(inside_read, c + 1)
                    dve.wait_ge(gate_made, 2 * c + 2 + PRIME)
                    dve.tensor_tensor(y[:, :], y[:, :], gate[:, :], ALU.mult).then_inc(gated, 1)
                    if q == J - 1:
                        with dve.If(b < BLOCKS - 1):
                            low_u(b + 1)
                    dve.wait_ge(state_decayed, c + 1)
                    dve.wait_ge(state_done, c + 1 + PRIME)
                    dve.tensor_tensor(state[:, :], state[:, :], across[0:STATE, :], ALU.add).then_inc(state_made, 1)

                dve.memset(state[:, :], 0.0).then_inc(state_zeroed, 1)
                dve.memset(past[:, :, :], 0.0).then_inc(state_zeroed, 1)
                dve.wait_ge(consts_in, 32)
                dve.tensor_scalar(rate[:, :], heads_sb[:, 0, :], LOG_RATE_MAX, None, ALU.min).then_inc(rate_capped, 1)
                normalize(0)
                apply_norm(0)
                dve.wait_ge(state_zeroed, 2)
                dve.wait_ge(rate_made, 1)
                dve.wait_ge(masks_made, 2)
                dve.tensor_copy(beyond_r[:, :], beyond[:, :]).then_inc(beyond_made, 1)
                low_u(0)
                with dve.Fori(0, BLOCKS) as b:
                    with dve.If(b > 0):
                        gate_eps(b - 1, J - 1)
                        y_low(b - 1, J - 1)
                    convolve(b, 0)
                    with dve.If(b > 0):
                        add_out(b - 1, J - 1)
                    convolve(b, 1)
                    log_terms(b)
                    convolve(b, 2)
                    time_steps(b)
                    convolve(b, 3)
                    mask_cb(b)
                    for n in range(4, CONV_TILES):
                        if n == CONV_TILES - 1:
                            spread_high(b, 0)
                        convolve(b, n)
                    for q in range(J):
                        chunk(b, q)
                        if q == 1:
                            with dve.If(b < BLOCKS - 1):
                                normalize(b + 1)
                        if q == 2:
                            with dve.If(b < BLOCKS - 1):
                                apply_norm(b + 1)
                gate_eps(BLOCKS - 1, J - 1)
                y_low(BLOCKS - 1, J - 1)
                add_out(BLOCKS - 1, J - 1)

            @block.tensor
            def _(pe):
                prime(pe, "pe")

                def bank(b, use):
                    i = at[use]
                    released(pe, b, i - 2)
                    return proj[i % 2]

                def turn_u(b):
                    for j in range(J):
                        pe.wait_ge(u_made, J * b + j + 1)
                        if not isinstance(b, int):
                            if j < 2:
                                bank(b - 1, ("turn", j))
                            else:
                                pe.wait_ge(seg_exp, J * PARTS * b + PRIME)
                        for k in range(K_TILES):
                            last = pe.transpose(turn_bank(j)[:, k * P:(k + 1) * P], u[:, j, k * P:(k + 1) * P],
                                                ident[:, :])
                        last.then_inc(turned, 1)

                def convolved(b, n):
                    dst = bank(b, ("conv", n))
                    pe.wait_ge(w_split, 1 if n == 0 else 2 + (n - 1) // 2)
                    for k in range(K_TILES):
                        a = W_BC + k * P if n == 0 else W_X + ((n - 1) * K_TILES + k) * P
                        cols = slice(k * P, (k + 1) * P)
                        for m, (w, v) in enumerate(((w_hi, u_hi), (w_hi, u_lo), (w_lo, u_hi))):
                            last = pe.matmul(dst[:, :], w[:, a:a + P], v[:, :, cols],
                                             start=(k == 0 and m == 0), stop=(k == K_TILES - 1 and m == 2))
                    last.then_inc(proj_done, 1)

                def rows(b, n):
                    if n < 2:
                        pe.wait_ge(u_split, J * (b + 1) + PRIME)
                    else:
                        pe.wait_ge(tok_stored, CONV_TILES * b + n - 1 + PRIME)
                    dst = seg[n % 2]
                    pe.wait_ge(silu_made, CONV_TILES * b + n + 1 + PRIME)
                    src = mixed[n % 2] if n else bc
                    for q in range(J):
                        last = pe.transpose(dst[:, q * P:(q + 1) * P], src[:, q * P:(q + 1) * P], ident[:, :])
                    last.then_inc(rows_turned, 1)

                def gate_half(b, q, half):
                    dst = bank(b, ("gate", q, half))
                    pe.wait_ge(w_split, first_gate_piece + 2 * half + 2)
                    for k in range(K_TILES):
                        cols = slice(k * P, (k + 1) * P)
                        a = W_GATE + (half * K_TILES + k) * 512
                        for m, (v, w) in enumerate(split3(u_hi, u_lo)):
                            last = pe.matmul(dst[:, :], v[:, q, cols], w[:, a:a + 512],
                                             start=(k == 0 and m == 0), stop=(k == K_TILES - 1 and m == 2))
                    last.then_inc(gate_done, 1)

                def turn_y(b, q):
                    pe.wait_ge(gated, J * b + q + 1 + PRIME)
                    for t in range(X_TILES):
                        last = pe.transpose(inside[:, t * P:(t + 1) * P], y[:, t * P:(t + 1) * P], ident[:, :])
                    last.then_inc(y_turned, 1)

                def project(b, q, use, half):
                    src_block = b if use[1] >= 0 else b - 1
                    if half:
                        dst = proj[at[use] % 2]
                    elif isinstance(b, int):
                        i = at[use]
                        released(pe, b - 1, max(n for n, o in enumerate(order)
                                                if o and o[0] != "turn" and n % 2 == i % 2))
                        dst = proj[i % 2]
                    else:
                        dst = bank(b, use)
                    pe.wait_ge(w_split, len(pieces))
                    pe.wait_ge(y_split, J * src_block + q + 1 + PRIME)
                    for t in range(half * X_TILES // 2, (half + 1) * X_TILES // 2):
                        cols = slice(t * P, (t + 1) * P)
                        a = W_OUT + t * C
                        for m, (v, w) in enumerate(split3(y_hi, y_lo)):
                            last = pe.matmul(dst[:, :], v[:, cols], w[:, a:a + C],
                                             start=(t == 0 and m == 0), stop=(t == X_TILES - 1 and m == 2))
                    if half:
                        last.then_inc(out_done, 1)

                def decays(b):
                    dst = bank(b, ("decay", 0))
                    pe.wait_ge(la_made, b + 1)
                    for m, mask in enumerate((upto, beyond, ones)):
                        last = pe.matmul(dst[:, m * J * SSM_HEADS:(m + 1) * J * SSM_HEADS], mask[:, :],
                                         la[:, :, :], start=True, stop=True)
                    last.then_inc(sums_done, 1)

                def segment(b, q, p):
                    i = PARTS * q + p
                    pe.wait_ge(spread_made, J * PARTS * b + i + 1)
                    if q == 0:
                        pe.wait_ge(high_spread, PARTS * b + p + 1)
                    if i < 2:
                        pe.wait_ge(tok_stored, CONV_TILES * (b + 1) - 1 + i + PRIME)
                    else:
                        pe.wait_ge(seg_exp, J * PARTS * b + i - 1 + PRIME)
                    pe.wait_ge(beyond_made, 1)
                    for dst, start in zip(spread, (True, False)):
                        last = pe.matmul(seg[(i + 1) % 2][:, :], beyond_r[:, :],
                                         dst[:, :, :].rearrange("p h t -> p (h t)"), start=start, stop=not start)
                    last.then_inc(seg_done, 1)

                def products(b):
                    dst = bank(b, ("cb", 0))
                    pe.wait_ge(silu_made, CONV_TILES * b + 1 + PRIME)
                    for q in range(J):
                        cols = slice(q * P, (q + 1) * P)
                        last = pe.matmul(dst[:, cols], bc[B_ROW:B_ROW + STATE, cols], c_rows[:, cols],
                                         start=True, stop=True)
                    last.then_inc(cb_done, 1)

                def from_state(b, q):
                    c = J * b + q
                    pe.wait_ge(state_made, c + PRIME)
                    for half in range(2):
                        cols = slice(half * 512, (half + 1) * 512)
                        last = pe.matmul(across[:, cols], c_rows[:, q * P:(q + 1) * P], state[:, cols],
                                         start=True, stop=True)
                    last.then_inc(across_done, 1)

                def from_chunk(b, q):
                    c = J * b + q
                    pe.wait_ge(y_split, c + PRIME)
                    pe.wait_ge(dtx_made, c + 1 + PRIME)
                    for h in range(SSM_HEADS):
                        if h % PART == 0:
                            pe.wait_ge(mix_made, PARTS * c + h // PART + 1 + PRIME)
                        cols = slice(h * SSM_HEAD, (h + 1) * SSM_HEAD)
                        last = pe.matmul(inside[:, cols], mix[:, h, :], dtx[:, cols], start=True, stop=True)
                    last.then_inc(inside_done, 1)

                def to_state(b, q):
                    c = J * b + q
                    pe.wait_ge(across_read, c + 1 + PRIME)
                    pe.wait_ge(tail_made, c + 1 + PRIME)
                    for half in range(2):
                        cols = slice(half * 512, (half + 1) * 512)
                        last = pe.matmul(across[0:STATE, cols], bc_tok[:, q, B_ROW:B_ROW + STATE],
                                         tail_x[:, cols], start=True, stop=True)
                    last.then_inc(state_done, 1)

                pe.wait_ge(masks_made, 2)
                turn_u(0)
                with pe.Fori(0, BLOCKS) as b:
                    with pe.If(b > 0):
                        turn_y(b - 1, J - 1)
                    pe.wait_ge(u_split, J * (b + 1) + PRIME)
                    convolved(b, 0)
                    with pe.If(b > 0):
                        for half in range(2):
                            project(b, J - 1, ("out", -1), half)
                    convolved(b, 1)
                    rows(b, 0)
                    convolved(b, 2)
                    for n in range(3, CONV_TILES):
                        convolved(b, n)
                        if n == 4:
                            products(b)
                        rows(b, n - 2)
                    gate_half(b, 0, 0)
                    rows(b, CONV_TILES - 2)
                    gate_half(b, 0, 1)
                    segment(b, 0, 0)
                    rows(b, CONV_TILES - 1)
                    for q in range(J):
                        if q == 0:
                            segment(b, q, 1)
                            from_state(b, q)
                            decays(b)
                            segment(b, q, 2)
                            gate_half(b, 1, 0)
                            segment(b, q, 3)
                        else:
                            if q > 1:
                                gate_half(b, q, 0)
                            segment(b, q, 1)
                            gate_half(b, q, 1)
                            segment(b, q, 2)
                            turn_y(b, q - 1)
                            from_state(b, q)
                            segment(b, q, 3)
                            project(b, q - 1, ("out", q - 1), 0)
                            project(b, q - 1, ("out", q - 1), 1)
                        from_chunk(b, q)
                        if q == J - 1:
                            with pe.If(b < BLOCKS - 1):
                                turn_u(b + 1)
                        else:
                            segment(b, q + 1, 0)
                        to_state(b, q)
                turn_y(BLOCKS - 1, J - 1)
                for half in range(2):
                    project(BLOCKS, J - 1, ("out", -1), half)


def build_program(nc, x, w_qkv, w_out, rope, w_ssm, conv, per_head, norm_w, w_ffn, ffn_scales,
                  down_scale, eye, out):
    T, C = x.shape
    K_TILES = C // P
    after = [nc.dram_tensor(f"x_after_{n}", [T, C], F32, kind="Internal").ap()
             for n in ("attention", "ffn", "ssm")]
    with ExitStack() as ctx:
        ident = ctx.enter_context(nc.sbuf_tensor("ident", [P, P], F32))
        neg_half = ctx.enter_context(nc.sbuf_tensor("neg_half", [P, 4], F32))
        low_any = ctx.enter_context(nc.sbuf_tensor("low_any", [1, 1], mybir.dt.int32))

        def new_sem(name):
            return ctx.enter_context(nc.semaphore(name))

        ident_in = new_sem("ident_in")
        with nc.Block() as block:
            @block.sync
            def _(sp):
                sp.dma_start(ident[:, :], eye).then_inc(ident_in, 16)
                sp.wait_ge(ident_in, 16)

            @block.vector
            def _(dve):
                dve.memset(neg_half[:, :], -0.5)

        with ExitStack() as passing:
            own = []

            def own_sem(name):
                own.append(passing.enter_context(nc.semaphore(name)))
                return own[-1]

            with ExitStack() as attention:
                q_all = attention.enter_context(nc.sbuf_tensor("q_all", [P, T // P, HEADS * HEAD], F32))
                k_stack = attention.enter_context(nc.sbuf_tensor("k_stack", [P, KV_HEADS, T], F32R))
                v_all = attention.enter_context(nc.sbuf_tensor("v_all", [P, T // P, KV_HEADS * HEAD], F32))
                build_qkv(nc, own_sem, x, w_qkv, rope, ident, neg_half, q_all, k_stack, v_all)
                build_attention(nc, new_sem, x, after[0], w_out, ident, q_all, k_stack, v_all)
            build_ffn(nc, own_sem, "f1", after[0], after[1], w_ffn, ffn_scales, down_scale, ident, neg_half,
                      low_any, low_known=False)
            with nc.Block() as block:
                @block.sync
                def _(sp):
                    for s in own:
                        sp.sem_clear(s)
        build_ssm(nc, new_sem, after[1], after[2], w_ssm, conv, per_head, norm_w, ident, neg_half)
        build_ffn(nc, new_sem, "f2", after[2], out, w_ffn, ffn_scales, down_scale, ident, neg_half,
                  low_any, low_known=True)




def kernel(**inputs):
    import numpy as np
    import concourse.bacc as _bacc
    from concourse import mybir as _mybir
    from concourse.bass_utils import run_bass_kernel_spmd as _run

    f32 = np.float32
    a = {name.removeprefix("L0_"): np.asarray(value) for name, value in inputs.items()}
    _, T, C = a["attn_a_x"].shape
    K = C // P

    def rows_in_tiles(w):
        return w.reshape(-1, P, w.shape[1]).transpose(1, 0, 2)

    fraction = np.arange(0, HEAD, 2, dtype=f32) / f32(HEAD)
    inv_freq = (f32(1.0) / f32(10000.0) ** fraction).astype(f32)
    angle = np.arange(T, dtype=f32)[:, None] * inv_freq[None, :]
    cos, sin = np.cos(angle), np.sin(angle)
    rope = np.stack([np.concatenate([cos, cos], -1), np.concatenate([-sin, sin], -1)], 1)
    rope = rope.reshape(T // P, P, 2, HEAD).transpose(1, 0, 2, 3)

    w_qkv = np.concatenate([a["attn_a_q_kernel"], a["attn_a_k_kernel"], a["attn_a_v_kernel"]], 1)

    inner = SSM_HEADS * SSM_HEAD
    w_in = a["attn_b_W_in"]
    w_gate, w_x = w_in[:, 0:inner], w_in[:, inner:2 * inner]
    rest = w_in[:, 2 * inner:]
    w_bc = np.zeros((C, P), f32)
    w_bc[:, B_ROW:B_ROW + STATE] = rest[:, 0:STATE]
    w_bc[:, C_ROW:C_ROW + STATE] = rest[:, STATE:2 * STATE]
    w_bc[:, DT_ROW:DT_ROW + SSM_HEADS] = rest[:, 2 * STATE:]
    w_ssm = np.concatenate([
        rows_in_tiles(w_bc).reshape(P, -1),
        w_x.reshape(K, P, inner // P, P).transpose(1, 2, 0, 3).reshape(P, -1),
        w_gate.reshape(K, P, 2, inner // 2).transpose(1, 2, 0, 3).reshape(P, -1),
        rows_in_tiles(a["attn_b_W_out"]).reshape(P, -1)], 1)
    taps, bias = a["attn_b_conv_w"], a["attn_b_conv_b"]
    conv = np.zeros((P, 1 + inner // P, TAPS + 1), f32)
    conv[:, 1:, 0:TAPS] = taps[0:inner].reshape(-1, P, TAPS).transpose(1, 0, 2)
    conv[:, 1:, TAPS] = bias[0:inner].reshape(-1, P).T
    for row, start in ((B_ROW, inner), (C_ROW, inner + STATE)):
        conv[row:row + STATE, 0, 0:TAPS] = taps[start:start + STATE]
        conv[row:row + STATE, 0, TAPS] = bias[start:start + STATE]
    conv[DT_ROW:DT_ROW + SSM_HEADS, 0, TAPS - 1] = 1.0
    conv[DT_ROW:DT_ROW + SSM_HEADS, 0, TAPS] = a["attn_b_dt_bias"]
    per_head = np.stack([a["attn_b_A_log"], a["attn_b_D_skip"]])

    gate_w, up_w, down_w = a["ffn_gate_w"], a["ffn_up_w"], a["ffn_down_w"]
    I = gate_w.shape[0] // P
    gate_up = np.stack([gate_w.T.reshape(K, P, I, P), up_w.T.reshape(K, P, I, P)], 3)
    gate_up = gate_up.transpose(2, 1, 0, 3, 4).reshape(I, P, -1)
    w_ffn = np.concatenate([gate_up, down_w.T.reshape(I, P, C)], 2)
    ffn_scales = np.stack([a["ffn_gate_s"].reshape(I, P).T, a["ffn_up_s"].reshape(I, P).T], 1)

    arrays = {
        "x": a["attn_a_x"][0], "w_qkv": rows_in_tiles(w_qkv), "w_out": rows_in_tiles(a["attn_a_out_kernel"]),
        "rope": rope, "w_ssm": w_ssm, "conv": conv, "per_head": per_head,
        "norm_w": a["attn_b_norm_w"].reshape(-1, P).T, "w_ffn": w_ffn, "ffn_scales": ffn_scales,
        "down_scale": a["ffn_down_s"], "eye": np.eye(P, dtype=f32)}
    arrays = {n: np.ascontiguousarray(v) for n, v in arrays.items()}

    nc = _bacc.Bacc("TRN2", target_bir_lowering=False, num_devices=1)
    args = [nc.dram_tensor(n, v.shape, _mybir.dt.from_np(v.dtype), kind="ExternalInput").ap()
            for n, v in arrays.items()]
    args.append(nc.dram_tensor("out", [T, C], _mybir.dt.from_np(np.dtype(f32)), kind="ExternalOutput").ap())
    build_program(nc, *args)
    r = _run(nc, [arrays], core_ids=[0])
    return r.results[0]["out"].reshape(1, T, C)
```
